# Optimizing a Trainium2 kernel written in Bass

```python
import numpy as np
import jax
import jax.numpy as jnp

def _softmax(x, axis=-1):
    return jax.nn.softmax(x, axis=axis)

def _gelu(x):
    return jax.nn.gelu(x, approximate=True)

def _silu(x):
    return jax.nn.silu(x)

def _sigmoid(x):
    return jax.nn.sigmoid(x)

def _layernorm(x, axis=-1, eps=1e-05):
    m = jnp.mean(x, axis=axis, keepdims=True)
    v = jnp.var(x, axis=axis, keepdims=True)
    return (x - m) / jnp.sqrt(v + eps)

def _scatter_add(tgt, idx, src, axis=0):
    return tgt.at[idx].add(src)

def _segment_sum(src, seg, n):
    return jax.ops.segment_sum(src, seg, n)
kernel_name = 'mk_decoder_postln_d1_seqx_r4_ff8827'

def setup_inputs(seed: int=0):
    np.random.seed(seed)
    _w = jnp.asarray

    def _rec_inputs():
        import jax
        import jax.numpy as jnp
        _rk = jax.random.key(seed)
        x = -0.0002928 + 1 * jax.random.normal(jax.random.fold_in(_rk, 1), (8, 256, 256), jnp.float32)
        _lenS = 256 - jax.random.randint(jax.random.fold_in(_rk, 7), (8,), 0, max(1, 256 // 4) + 1, jnp.int32)
        _lenS2 = 256 - jax.random.randint(jax.random.fold_in(_rk, 8), (8,), 0, max(1, 256 // 4) + 1, jnp.int32)
        _ctx_1024P = jax.random.normal(jax.random.fold_in(_rk, 11), (8, 16, 256), jnp.float32)
        _ctx_1024c = jax.random.dirichlet(jax.random.fold_in(_rk, 511), 0.3 * jnp.ones((16,), jnp.float32), (8, 256))
        _ctx_1024t = jnp.einsum('bsk,bkd->bsd', _ctx_1024c, _ctx_1024P)
        _ctx_1024t = _ctx_1024t * jax.lax.rsqrt(jnp.mean(jnp.square(_ctx_1024t)) + 1e-12) * 0.953939
        ctx_1024 = -1.39393e-06 + 0.999914 * (_ctx_1024t + 0.3 * jax.random.normal(jax.random.fold_in(_rk, 611), (8, 256, 256), jnp.float32))
        return (x, ctx_1024)
    x, ctx_1024 = _rec_inputs()

    def _L0_attn_setup():
        import jax, jax.numpy as jnp
        import numpy as np
        D_MODEL, N_HEADS, N_LAYERS, D_FF = (256, 16, 6, 1024)
        B, L = (4, 512)
        CHUNK = 128
        EPS = 1e-06
        LN_EPS = 1e-05

        def layer_norm(x, g, b):
            mu = x.mean(-1, keepdims=True)
            var = ((x - mu) ** 2).mean(-1, keepdims=True)
            return (x - mu) * jax.lax.rsqrt(var + LN_EPS) * g + b

        def feature_map(x):
            return jax.nn.elu(x) + 1.0

        def causal_linear_attn(q, k, v):
            Bq, Lq, H, D = q.shape
            M = v.shape[-1]
            NC = Lq // CHUNK
            qc = q.reshape(Bq, NC, CHUNK, H, D)
            kc = k.reshape(Bq, NC, CHUNK, H, D)
            vc = v.reshape(Bq, NC, CHUNK, H, M)
            A = jnp.einsum('bnihd,bnjhd->bnhij', qc, kc)
            A = A * jnp.tril(jnp.ones((CHUNK, CHUNK), dtype=q.dtype))
            intra = jnp.einsum('bnhij,bnjhm->bnihm', A, vc)
            KV = jnp.einsum('bnjhd,bnjhm->bnhdm', kc, vc)
            KV = jnp.cumsum(KV, axis=1)
            KV = jnp.concatenate([jnp.zeros_like(KV[:, :1]), KV[:, :-1]], axis=1)
            inter = jnp.einsum('bnihd,bnhdm->bnihm', qc, KV)
            num = intra + inter
            k_cum = jnp.cumsum(kc, axis=2)
            z = jnp.cumsum(kc.sum(axis=2), axis=1)
            z = jnp.concatenate([jnp.zeros_like(z[:, :1]), z[:, :-1]], axis=1)
            den = jnp.einsum('bnihd,bnihd->bnih', qc, k_cum) + jnp.einsum('bnihd,bnhd->bnih', qc, z) + EPS
            out = num / den[..., None]
            return out.reshape(Bq, Lq, H, M)

        def forward(x, Wq, bq, Wk, bk, Wv, bv, Wo, bo, g1, be1, W1, b1, W2, b2, g2, be2, gf, bf):
            Bx, Lx, dm = x.shape
            dh = dm // N_HEADS
            x = jnp.flip(x, axis=1)
            for l in range(N_LAYERS):
                q = (x @ Wq[l] + bq[l]).reshape(Bx, Lx, N_HEADS, dh)
                k = (x @ Wk[l] + bk[l]).reshape(Bx, Lx, N_HEADS, dh)
                v = (x @ Wv[l] + bv[l]).reshape(Bx, Lx, N_HEADS, dh)
                a = causal_linear_attn(feature_map(q), feature_map(k), v)
                a = a.reshape(Bx, Lx, dm) @ Wo[l] + bo[l]
                x = x + a
                y = x = layer_norm(x, g1[l], be1[l])
                y = jax.nn.gelu(y @ W1[l] + b1[l], approximate=False) @ W2[l] + b2[l]
                x = layer_norm(x + y, g2[l], be2[l])
            x = layer_norm(x, gf, bf)
            return jnp.flip(x, axis=1)
        key = jax.random.key(seed)
        ks = jax.random.split(key, 8)
        dm, NL, dff = (D_MODEL, N_LAYERS, D_FF)
        w = lambda k, shape: jax.random.normal(k, shape, jnp.float32) * 0.02
        return {'x': jax.random.normal(ks[0], (B, L, dm), jnp.float32), 'Wq': w(ks[1], (NL, dm, dm)), 'bq': jnp.zeros((NL, dm), jnp.float32), 'Wk': w(ks[2], (NL, dm, dm)), 'bk': jnp.zeros((NL, dm), jnp.float32), 'Wv': w(ks[3], (NL, dm, dm)), 'bv': jnp.zeros((NL, dm), jnp.float32), 'Wo': w(ks[4], (NL, dm, dm)), 'bo': jnp.zeros((NL, dm), jnp.float32), 'g1': jnp.ones((NL, dm), jnp.float32), 'be1': jnp.zeros((NL, dm), jnp.float32), 'W1': w(ks[5], (NL, dm, dff)), 'b1': jnp.zeros((NL, dff), jnp.float32), 'W2': w(ks[6], (NL, dff, dm)), 'b2': jnp.zeros((NL, dm), jnp.float32), 'g2': jnp.ones((NL, dm), jnp.float32), 'be2': jnp.zeros((NL, dm), jnp.float32), 'gf': jnp.ones((dm,), jnp.float32), 'bf': jnp.zeros((dm,), jnp.float32)}
    _L0_attn_all = _L0_attn_setup()
    _L0_attn_in = {k: v for k, v in _L0_attn_all.items() if k in ('Wq', 'bq', 'Wk', 'bk', 'Wv', 'bv', 'Wo', 'bo', 'g1', 'be1', 'W1', 'b1', 'W2', 'b2', 'g2', 'be2', 'gf', 'bf')}
    del _L0_attn_all

    def _L0_xattn_setup():
        import jax, jax.numpy as jnp
        import numpy as np
        DIM = 256
        H = 16
        HD = DIM // H
        EPS = 1e-05
        key = jax.random.key(seed)
        ks = jax.random.split(key, 10)
        B, S = (2, 512)
        lim_h = 1.0 / np.sqrt(HD)
        lim_d = 1.0 / np.sqrt(DIM)
        u = lambda k, shape, lim: jax.random.uniform(k, shape, jnp.float32, -lim, lim)
        return {'q': jax.random.normal(ks[0], (B, S, DIM), jnp.float32), 'k': jax.random.normal(ks[1], (B, S, DIM), jnp.float32), 'v': jax.random.normal(ks[2], (B, S, DIM), jnp.float32), 'wq1': u(ks[3], (H, HD, HD), lim_h), 'wk1': u(ks[4], (H, HD, HD), lim_h), 'wq2': u(ks[5], (H, HD, HD), lim_h), 'wk2': u(ks[6], (H, HD, HD), lim_h), 'wv': u(ks[7], (H, HD, HD), lim_h), 'wo': u(ks[8], (DIM, DIM), lim_d), 'gain': jnp.float32(0.3)}
    _L0_xattn_all = _L0_xattn_setup()
    _L0_xattn_in = {k: v for k, v in _L0_xattn_all.items() if k in ('wq1', 'wk1', 'wq2', 'wk2', 'wv', 'wo', 'gain')}
    del _L0_xattn_all

    def _L0_ffn_setup():
        import jax, jax.numpy as jnp
        import numpy as np
        B, S, DIM = (4, 1024, 256)
        BASE_COUPLING = 0.1
        NUM_CYCLES = 3

        def _gelu(x):
            return jax.nn.gelu(x, approximate=False)

        def _coupling_net(h, w1, b1, w2, b2, w3, b3, w4, b4):
            h = _gelu(h @ w1 + b1)
            h = _gelu(h @ w2 + b2)
            h = _gelu(h @ w3 + b3)
            return jax.nn.sigmoid(h @ w4 + b4)

        def _global_net(h, w1, b1, w2, b2, w3, b3):
            h = _gelu(h @ w1 + b1)
            h = _gelu(h @ w2 + b2)
            return jax.nn.sigmoid(h @ w3 + b3)

        def _twist(x):
            o_r, o_i, p_r, p_i = jnp.split(x, 4, axis=-1)
            return jnp.concatenate([p_r, -p_i, -o_r, o_i], axis=-1)
        key = jax.random.key(seed)
        ks = jax.random.split(key, 9)
        d = DIM

        def w(k, fan_in, fan_out):
            return jax.random.normal(k, (fan_in, fan_out), dtype=jnp.float32) / np.sqrt(fan_in).astype(np.float32)
        inp = {'x': jax.random.normal(ks[0], (B, S, d), dtype=jnp.float32)}
        cn_dims = [(d, d), (d, d // 2), (d // 2, d // 4), (d // 4, 1)]
        for i, (a, b) in enumerate(cn_dims):
            inp[f'cn_w{i + 1}'] = w(ks[1 + i], a, b)
            inp[f'cn_b{i + 1}'] = jnp.zeros((b,), dtype=jnp.float32)
        gc_dims = [(d, d // 2), (d // 2, d // 4), (d // 4, 1)]
        for i, (a, b) in enumerate(gc_dims):
            inp[f'gc_w{i + 1}'] = w(ks[5 + i], a, b)
            inp[f'gc_b{i + 1}'] = jnp.zeros((b,), dtype=jnp.float32)
        inp['adaptive_range'] = jnp.full((1,), 0.2, dtype=jnp.float32)
        return inp
    _L0_ffn_all = _L0_ffn_setup()
    _L0_ffn_in = {k: v for k, v in _L0_ffn_all.items() if k in ('cn_w1', 'cn_b1', 'cn_w2', 'cn_b2', 'cn_w3', 'cn_b3', 'cn_w4', 'cn_b4', 'gc_w1', 'gc_b1', 'gc_w2', 'gc_b2', 'gc_w3', 'gc_b3', 'adaptive_range')}
    del _L0_ffn_all
    return {'x': x, 'ctx_1024': ctx_1024, 'L0_attn_Wq': _L0_attn_in['Wq'], 'L0_attn_bq': _L0_attn_in['bq'], 'L0_attn_Wk': _L0_attn_in['Wk'], 'L0_attn_bk': _L0_attn_in['bk'], 'L0_attn_Wv': _L0_attn_in['Wv'], 'L0_attn_bv': _L0_attn_in['bv'], 'L0_attn_Wo': _L0_attn_in['Wo'], 'L0_attn_bo': _L0_attn_in['bo'], 'L0_attn_g1': _L0_attn_in['g1'], 'L0_attn_be1': _L0_attn_in['be1'], 'L0_attn_W1': _L0_attn_in['W1'], 'L0_attn_b1': _L0_attn_in['b1'], 'L0_attn_W2': _L0_attn_in['W2'], 'L0_attn_b2': _L0_attn_in['b2'], 'L0_attn_g2': _L0_attn_in['g2'], 'L0_attn_be2': _L0_attn_in['be2'], 'L0_attn_gf': _L0_attn_in['gf'], 'L0_attn_bf': _L0_attn_in['bf'], 'L0_xattn_wq1': _L0_xattn_in['wq1'], 'L0_xattn_wk1': _L0_xattn_in['wk1'], 'L0_xattn_wq2': _L0_xattn_in['wq2'], 'L0_xattn_wk2': _L0_xattn_in['wk2'], 'L0_xattn_wv': _L0_xattn_in['wv'], 'L0_xattn_wo': _L0_xattn_in['wo'], 'L0_xattn_gain': _L0_xattn_in['gain'], 'L0_ffn_cn_w1': _L0_ffn_in['cn_w1'], 'L0_ffn_cn_b1': _L0_ffn_in['cn_b1'], 'L0_ffn_cn_w2': _L0_ffn_in['cn_w2'], 'L0_ffn_cn_b2': _L0_ffn_in['cn_b2'], 'L0_ffn_cn_w3': _L0_ffn_in['cn_w3'], 'L0_ffn_cn_b3': _L0_ffn_in['cn_b3'], 'L0_ffn_cn_w4': _L0_ffn_in['cn_w4'], 'L0_ffn_cn_b4': _L0_ffn_in['cn_b4'], 'L0_ffn_gc_w1': _L0_ffn_in['gc_w1'], 'L0_ffn_gc_b1': _L0_ffn_in['gc_b1'], 'L0_ffn_gc_w2': _L0_ffn_in['gc_w2'], 'L0_ffn_gc_b2': _L0_ffn_in['gc_b2'], 'L0_ffn_gc_w3': _L0_ffn_in['gc_w3'], 'L0_ffn_gc_b3': _L0_ffn_in['gc_b3'], 'L0_ffn_adaptive_range': _L0_ffn_in['adaptive_range']}

def reference(x, ctx_1024, L0_attn_Wq, L0_attn_bq, L0_attn_Wk, L0_attn_bk, L0_attn_Wv, L0_attn_bv, L0_attn_Wo, L0_attn_bo, L0_attn_g1, L0_attn_be1, L0_attn_W1, L0_attn_b1, L0_attn_W2, L0_attn_b2, L0_attn_g2, L0_attn_be2, L0_attn_gf, L0_attn_bf, L0_xattn_wq1, L0_xattn_wk1, L0_xattn_wq2, L0_xattn_wk2, L0_xattn_wv, L0_xattn_wo, L0_xattn_gain, L0_ffn_cn_w1, L0_ffn_cn_b1, L0_ffn_cn_w2, L0_ffn_cn_b2, L0_ffn_cn_w3, L0_ffn_cn_b3, L0_ffn_cn_w4, L0_ffn_cn_b4, L0_ffn_gc_w1, L0_ffn_gc_b1, L0_ffn_gc_w2, L0_ffn_gc_b2, L0_ffn_gc_w3, L0_ffn_gc_b3, L0_ffn_adaptive_range):
    import jax
    import jax.numpy as jnp

    def _L0_attn_ref(x, Wq, bq, Wk, bk, Wv, bv, Wo, bo, g1, be1, W1, b1, W2, b2, g2, be2, gf, bf):
        import jax, jax.numpy as jnp
        import numpy as np
        D_MODEL, N_HEADS, N_LAYERS, D_FF = (256, 16, 6, 1024)
        B, L = (4, 512)
        CHUNK = 128
        EPS = 1e-06
        LN_EPS = 1e-05

        def layer_norm(x, g, b):
            mu = x.mean(-1, keepdims=True)
            var = ((x - mu) ** 2).mean(-1, keepdims=True)
            return (x - mu) * jax.lax.rsqrt(var + LN_EPS) * g + b

        def feature_map(x):
            return jax.nn.elu(x) + 1.0

        def causal_linear_attn(q, k, v):
            Bq, Lq, H, D = q.shape
            M = v.shape[-1]
            NC = Lq // CHUNK
            qc = q.reshape(Bq, NC, CHUNK, H, D)
            kc = k.reshape(Bq, NC, CHUNK, H, D)
            vc = v.reshape(Bq, NC, CHUNK, H, M)
            A = jnp.einsum('bnihd,bnjhd->bnhij', qc, kc)
            A = A * jnp.tril(jnp.ones((CHUNK, CHUNK), dtype=q.dtype))
            intra = jnp.einsum('bnhij,bnjhm->bnihm', A, vc)
            KV = jnp.einsum('bnjhd,bnjhm->bnhdm', kc, vc)
            KV = jnp.cumsum(KV, axis=1)
            KV = jnp.concatenate([jnp.zeros_like(KV[:, :1]), KV[:, :-1]], axis=1)
            inter = jnp.einsum('bnihd,bnhdm->bnihm', qc, KV)
            num = intra + inter
            k_cum = jnp.cumsum(kc, axis=2)
            z = jnp.cumsum(kc.sum(axis=2), axis=1)
            z = jnp.concatenate([jnp.zeros_like(z[:, :1]), z[:, :-1]], axis=1)
            den = jnp.einsum('bnihd,bnihd->bnih', qc, k_cum) + jnp.einsum('bnihd,bnhd->bnih', qc, z) + EPS
            out = num / den[..., None]
            return out.reshape(Bq, Lq, H, M)

        def forward(x, Wq, bq, Wk, bk, Wv, bv, Wo, bo, g1, be1, W1, b1, W2, b2, g2, be2, gf, bf):
            Bx, Lx, dm = x.shape
            dh = dm // N_HEADS
            x = jnp.flip(x, axis=1)
            for l in range(N_LAYERS):
                q = (x @ Wq[l] + bq[l]).reshape(Bx, Lx, N_HEADS, dh)
                k = (x @ Wk[l] + bk[l]).reshape(Bx, Lx, N_HEADS, dh)
                v = (x @ Wv[l] + bv[l]).reshape(Bx, Lx, N_HEADS, dh)
                a = causal_linear_attn(feature_map(q), feature_map(k), v)
                a = a.reshape(Bx, Lx, dm) @ Wo[l] + bo[l]
                x = x + a
                y = x = layer_norm(x, g1[l], be1[l])
                y = jax.nn.gelu(y @ W1[l] + b1[l], approximate=False) @ W2[l] + b2[l]
                x = layer_norm(x + y, g2[l], be2[l])
            x = layer_norm(x, gf, bf)
            return jnp.flip(x, axis=1)
        return forward(x, Wq, bq, Wk, bk, Wv, bv, Wo, bo, g1, be1, W1, b1, W2, b2, g2, be2, gf, bf)

    def _L0_xattn_ref(q, k, v, wq1, wk1, wq2, wk2, wv, wo, gain):
        import jax, jax.numpy as jnp
        import numpy as np
        DIM = 256
        H = 16
        HD = DIM // H
        EPS = 1e-05
        B, S, D = q.shape
        h, hd = (wq1.shape[0], wq1.shape[1])
        scale = jnp.sqrt(jnp.asarray(hd, jnp.float32))
        qh = q.reshape(B, S, h, hd)
        kh = k.reshape(B, S, h, hd)
        vh = v.reshape(B, S, h, hd)
        q1 = jnp.einsum('bshd,hed->bshe', qh, wq1)
        k1 = jnp.einsum('bshd,hed->bshe', kh, wk1)
        q2 = jnp.einsum('bshd,hed->bshe', qh, wq2)
        k2 = jnp.einsum('bshd,hed->bshe', kh, wk2)
        vp = jnp.einsum('bshd,hed->bshe', vh, wv)
        s1 = jnp.einsum('bshe,bthe->bhst', q1, k1) / scale
        s2 = jnp.einsum('bshe,bthe->bhst', q2, k2) / scale
        attn = jax.nn.softmax(s1, axis=-1) - gain * jax.nn.softmax(s2, axis=-1)
        o = jnp.einsum('bhst,bthe->bshe', attn, vp)
        mean = jnp.mean(o, axis=-1, keepdims=True)
        var = jnp.mean(jnp.square(o - mean), axis=-1, keepdims=True)
        o = (o - mean) / jnp.sqrt(var + EPS)
        out = o.reshape(B, S, D) @ wo.T
        return out

    def _L0_ffn_ref(x, cn_w1, cn_b1, cn_w2, cn_b2, cn_w3, cn_b3, cn_w4, cn_b4, gc_w1, gc_b1, gc_w2, gc_b2, gc_w3, gc_b3, adaptive_range):
        import jax, jax.numpy as jnp
        import numpy as np
        B, S, DIM = (4, 1024, 256)
        BASE_COUPLING = 0.1
        NUM_CYCLES = 3

        def _gelu(x):
            return jax.nn.gelu(x, approximate=False)

        def _coupling_net(h, w1, b1, w2, b2, w3, b3, w4, b4):
            h = _gelu(h @ w1 + b1)
            h = _gelu(h @ w2 + b2)
            h = _gelu(h @ w3 + b3)
            return jax.nn.sigmoid(h @ w4 + b4)

        def _global_net(h, w1, b1, w2, b2, w3, b3):
            h = _gelu(h @ w1 + b1)
            h = _gelu(h @ w2 + b2)
            return jax.nn.sigmoid(h @ w3 + b3)

        def _twist(x):
            o_r, o_i, p_r, p_i = jnp.split(x, 4, axis=-1)
            return jnp.concatenate([p_r, -p_i, -o_r, o_i], axis=-1)
        global_context = x.mean(axis=1, keepdims=True)
        gf = _global_net(global_context, gc_w1, gc_b1, gc_w2, gc_b2, gc_w3, gc_b3)
        out = x
        for _ in range(NUM_CYCLES):
            tf = _coupling_net(out, cn_w1, cn_b1, cn_w2, cn_b2, cn_w3, cn_b3, cn_w4, cn_b4)
            combined = 0.7 * gf + 0.3 * tf
            coupling = BASE_COUPLING + adaptive_range * (combined - 0.5) * 2.0
            out = out + coupling * _twist(out)
        return out
    x = _layernorm(x + _L0_attn_ref(x, L0_attn_Wq, L0_attn_bq, L0_attn_Wk, L0_attn_bk, L0_attn_Wv, L0_attn_bv, L0_attn_Wo, L0_attn_bo, L0_attn_g1, L0_attn_be1, L0_attn_W1, L0_attn_b1, L0_attn_W2, L0_attn_b2, L0_attn_g2, L0_attn_be2, L0_attn_gf, L0_attn_bf), axis=-1)
    x = _layernorm(x + _L0_xattn_ref(x, ctx_1024, ctx_1024, L0_xattn_wq1, L0_xattn_wk1, L0_xattn_wq2, L0_xattn_wk2, L0_xattn_wv, L0_xattn_wo, L0_xattn_gain), axis=-1)
    x = _layernorm(x + _L0_ffn_ref(x, L0_ffn_cn_w1, L0_ffn_cn_b1, L0_ffn_cn_w2, L0_ffn_cn_b2, L0_ffn_cn_w3, L0_ffn_cn_b3, L0_ffn_cn_w4, L0_ffn_cn_b4, L0_ffn_gc_w1, L0_ffn_gc_b1, L0_ffn_gc_w2, L0_ffn_gc_b2, L0_ffn_gc_w3, L0_ffn_gc_b3, L0_ffn_adaptive_range), axis=-1)
    return x

_drawn_inputs = setup_inputs


def setup_inputs(seed=0):
    import zlib

    import numpy as np

    out = dict(_drawn_inputs(seed))
    spreads = {'L0_attn_bq': (0.0, 2.0),
     'L0_attn_bk': (0.0, 2.0),
     'L0_attn_bv': (0.0, 0.1),
     'L0_attn_bo': (0.0, 0.1),
     'L0_attn_g1': (1.0, 0.2),
     'L0_attn_be1': (0.0, 0.1),
     'L0_attn_b1': (0.0, 0.1),
     'L0_attn_b2': (0.0, 0.1),
     'L0_attn_g2': (1.0, 0.2),
     'L0_attn_be2': (0.0, 0.1),
     'L0_attn_gf': (1.0, 0.2),
     'L0_attn_bf': (0.0, 0.1),
     'L0_ffn_cn_b1': (0.0, 2.0),
     'L0_ffn_cn_b2': (0.0, 2.0),
     'L0_ffn_cn_b3': (0.0, 2.0),
     'L0_ffn_gc_b1': (0.0, 0.8),
     'L0_ffn_gc_b2': (0.0, 0.8)}
    factors = {'L0_attn_Wq': 64.0,
     'L0_attn_Wk': 47.799,
     'L0_ffn_cn_w1': 6.92,
     'L0_ffn_cn_w2': 7.67,
     'L0_ffn_cn_w3': 6.385,
     'L0_ffn_cn_w4': 7.075,
     'L0_ffn_gc_w1': 2.895,
     'L0_ffn_gc_w2': 6.431,
     'L0_ffn_gc_w3': 3.532}
    for name, (base, spread) in spreads.items():
        noise = np.random.default_rng([zlib.crc32(name.encode()), seed]).standard_normal(out[name].shape)
        drawn = base * np.exp(spread * noise) if base else spread * noise
        out[name] = jnp.asarray(drawn.astype(out[name].dtype))
    for name, factor in factors.items():
        out[name] = (out[name] * factor).astype(out[name].dtype)
    return out
```

```python
from contextlib import ExitStack

import concourse.bass as bass
from concourse import mybir

F32 = mybir.dt.float32
F32R = mybir.dt.float32r
ALU = mybir.AluOpType
ACT = mybir.ActivationFunctionType
AX = mybir.AxisListType

P = 128
D = 256
KC = D // P
B, S = 8, 256
T = B * S
TT = 512
NT = T // TT
SB = TT // P
NB = T // P
H, DH = 16, 16
HC = P // DH
HX = DH + 1
L = 6
DFF = 1024
FC = DFF // P
LN_EPS = 1e-5
DEN_EPS = 1e-6


def blk(s):
    return slice(s * P, (s + 1) * P)


def wait(eng, sem, value):
    if isinstance(value, int) and value <= 0:
        return
    eng.wait_ge(sem, value)


def encoder(nc, ctx, consts, X, dram):
    own = ExitStack()

    def sb(name, shape, dt=F32):
        return own.enter_context(nc.sbuf_tensor("e_" + name, [P] + shape, dt))

    def sem(name):
        return ctx.enter_context(nc.semaphore("e_" + name))

    ident, amask, headmask, blockmask = consts["ident"], consts["amask"], consts["headmask"], consts["blockmask"]

    HR = 4

    names_a = ["Wq", "Wk", "Wv", "Wo"]
    raw_a = sb("raw_a", [4, KC, D])
    raw_m = sb("raw_m", [KC * DFF])
    hi = {w: sb(w + "_hi", [KC, D], F32R) for w in names_a}
    lo = {w: sb(w + "_lo", [KC, D], F32R) for w in names_a}
    hi["W1"], lo["W1"] = sb("W1_hi", [KC, DFF], F32R), sb("W1_lo", [KC, DFF], F32R)
    hi["W2"], lo["W2"] = sb("W2_hi", [FC, D], F32R), sb("W2_lo", [FC, D], F32R)
    rows_a = {n: sb(n, [D]) for n in ("bv", "bo", "g1", "be1")}
    rows_m = {n: sb(n, [D]) for n in ("b2", "g2", "be2")}
    qk_bias_all, qk_bias, qk_bias1 = sb("qk_bias_all", [L * 2 * KC]), sb("qk_bias", [2 * KC]), sb("qk_bias1", [2 * KC])
    h_bias_all, h_bias = sb("h_bias_all", [L * FC]), sb("h_bias", [FC])

    xT_hi, xT_lo = sb("xT_hi", [KC, TT], F32R), sb("xT_lo", [KC, TT], F32R)
    qkT = sb("qkT", [2 * KC, TT])
    qx = sb("qx", [KC, HC, TT])
    ktok = sb("ktok", [2, KC, P])
    vx = sb("vx", [SB, H, HX])
    kv = sb("kv", [2, KC, HC * HX])
    am = sb("am", [2, 4, 4, P])
    den, rden = sb("den", [SB, H]), sb("rden", [SB, H])
    a_tok = sb("a_tok", [SB, D])
    yT_hi, yT_lo = sb("yT_hi", [KC, TT], F32R), sb("yT_lo", [KC, TT], F32R)
    h_f = sb("h_f", [HR, TT])
    h_hi, h_lo = sb("h_hi", [FC, TT], F32R), sb("h_lo", [FC, TT], F32R)
    st = {i: sb(f"st{i}", [SB, 6]) for i in (1, 2)}
    mv = {i: sb(f"mv{i}", [SB, 2]) for i in (1, 2)}
    ve = {i: sb(f"ve{i}", [SB]) for i in (1, 2)}
    rs = {i: sb(f"rs{i}", [SB]) for i in (1, 2)}
    table = sb("table", [1])
    half = sb("half", [SB])

    ps_tr = [own.enter_context(nc.psum_tensor(f"e_tr{i}", [P, TT], F32)) for i in range(2)]
    ps_pr = [own.enter_context(nc.psum_tensor(f"e_pr{i}", [P, TT], F32)) for i in range(2)]
    ps_sc = [own.enter_context(nc.psum_tensor(f"e_sc{i}", [P, TT], F32)) for i in range(2)]
    ps_tk = [own.enter_context(nc.psum_tensor(f"e_tk{i}", [P, TT], F32)) for i in range(2)]

    x0_loaded, x_loaded, biases_loaded = sem("x0_loaded"), sem("x_loaded"), sem("biases_loaded")
    raw_qkv_loaded, raw_o_loaded, raw_1_loaded, raw_2_loaded = (
        sem("raw_qkv_loaded"), sem("raw_o_loaded"), sem("raw_1_loaded"), sem("raw_2_loaded"))
    bv_loaded, bo_loaded, ln1_rows_loaded = sem("bv_loaded"), sem("bo_loaded"), sem("ln1_rows_loaded")
    b2_loaded, ln2_rows_loaded = sem("b2_loaded"), sem("ln2_rows_loaded")
    xT_tr, qk_full, v_full, ktr_full = sem("xT_tr"), sem("qk_full"), sem("v_full"), sem("ktr_full")
    kv_full, sc_full, out_full = sem("kv_full"), sem("sc_full"), sem("out_full")
    aT_tr, wo_full = sem("aT_tr"), sem("wo_full")
    yT_tr, h_full, m_full = sem("yT_tr"), sem("h_full"), sem("m_full")
    xT_hi_done, qk_exp, ktok_done, aT_hi_done = sem("xT_hi_done"), sem("qk_exp"), sem("ktok_done"), sem("aT_hi_done")
    yT_hi_done, gelu_done, qx_act_done = sem("yT_hi_done"), sem("gelu_done"), sem("qx_act_done")
    qkv_hi, o_hi, w1_hi, w2_hi = sem("qkv_hi"), sem("o_hi"), sem("w1_hi"), sem("w2_hi")
    xT_lo_done, qk_min, phi_done, qx_done, vx_done = sem("xT_lo_done"), sem("qk_min"), sem("phi_done"), sem("qx_done"), sem("vx_done")
    kv_done, am_done, a_done, aT_lo_done = sem("kv_done"), sem("am_done"), sem("a_done"), sem("aT_lo_done")
    den_done, rden_done = sem("den_done"), sem("rden_done")
    yT_lo_done, h_hi_done = sem("yT_lo_done"), sem("h_hi_done")
    z_done = {i: sem(f"z{i}_done") for i in (1, 2)}
    st_done = {i: sem(f"st{i}_done") for i in (1, 2)}
    mv_done = {i: sem(f"mv{i}_done") for i in (1, 2)}
    ve_done = {i: sem(f"ve{i}_done") for i in (1, 2)}
    xc_done = {i: sem(f"xc{i}_done") for i in (1, 2)}
    ln_done = {i: sem(f"ln{i}_done") for i in (1, 2)}
    qk_bias_set, h_bias_set, ones_set = sem("qk_bias_set"), sem("h_bias_set"), sem("ones_set")
    rs_done = {i: sem(f"rs{i}_done") for i in (1, 2)}
    qx_pool_done, xbo_done, xb2_done, h_lo_done, half_set = sem("qx_pool_done"), sem("xbo_done"), sem("xb2_done"), sem("h_lo_done"), sem("half_set")
    qkv_lo, o_lo, w1_lo, w2_lo = sem("qkv_lo"), sem("o_lo"), sem("w1_lo"), sem("w2_lo")

    def steps(eng, step):
        step(0, -1, -1, True, False, True)
        step(0, 0, 0, True, True, True)
        with eng.Fori(0, L - 1) as l:
            for q in range(1, NT):
                step(l, q, l * NT + q, True, True, True)
            step(l + 1, 0, l * NT + NT, True, True, True)
        for q in range(1, NT):
            step(L - 1, q, (L - 1) * NT + q, q < NT - 1, True, q < NT - 2)

    UP_AT = {(0, 1): 4, (1, 1): 5, (2, 0): 6, (3, 0): 7}

    def lagging(u):
        return not (isinstance(u, int) and u <= 0)

    def split3(pe, out, stat, mov, first, last):
        pe.matmul(out, stat[0], mov[0], start=first, stop=False)
        pe.matmul(out, stat[0], mov[1], start=False, stop=False)
        return pe.matmul(out, stat[1], mov[0], start=False, stop=last)

    def blk(s):
        return slice(s * P, (s + 1) * P)

    with nc.Block() as block:

        @block.sync
        def _(sp):
            def load_attn_weights(l, which, done):
                for w in which:
                    sp.dma_start(raw_a[:, names_a.index(w)], dram[w][l, :, :].rearrange("(c p) n -> p c n", p=P)).then_inc(done, 16)

            def load_rows(l, which, rows, done):
                for n in which:
                    sp.dma_start(rows[n][:, :], dram[n][l, :].partition_broadcast(P)).then_inc(done, 16)

            def load_w1(l):
                sp.dma_start(raw_m[:, :].rearrange("p (c n) -> p c n", c=KC),
                             dram["W1"][l, :, :].rearrange("(c p) n -> p c n", p=P)).then_inc(raw_1_loaded, 16)

            def load_w2(l):
                sp.dma_start(raw_m[:, :].rearrange("p (c n) -> p c n", c=FC),
                             dram["W2"][l, :, :].rearrange("(c p) n -> p c n", p=P)).then_inc(raw_2_loaded, 16)

            xv = dram["x"].rearrange("b (h p) d -> p (b h) d", p=P)
            sp.dma_start(X[:, 0:SB], xv[:, 0:SB]).then_inc(x0_loaded, 16)
            load_attn_weights(0, ["Wq", "Wk", "Wv"], raw_qkv_loaded)
            with nc.allow_non_contiguous_dma(reason="biases by partition, once"):
                for j, (n, c) in enumerate((n, c) for n in ("bq", "bk") for c in range(KC)):
                    sp.dma_start(qk_bias_all[:, j::2 * KC], dram[n][:, blk(c)].rearrange("l p -> p l")).then_inc(biases_loaded, 16)
                for c in range(FC):
                    sp.dma_start(h_bias_all[:, c::FC], dram["b1"][:, blk(c)].rearrange("l p -> p l")).then_inc(biases_loaded, 16)
            load_rows(0, ["bv"], rows_a, bv_loaded)
            sp.dma_start(X[:, SB:NB], xv[:, SB:NB]).then_inc(x_loaded, 16)
            load_rows(0, ["bo"], rows_a, bo_loaded)
            load_attn_weights(0, ["Wo"], raw_o_loaded)
            load_w1(0)
            load_rows(0, ["g1", "be1"], rows_a, ln1_rows_loaded)
            load_rows(0, ["b2"], rows_m, b2_loaded)
            load_rows(0, ["g2", "be2"], rows_m, ln2_rows_loaded)

            sp.wait_ge(w1_lo, 1)
            load_w2(0)
            with sp.Fori(0, L - 1) as l:
                sp.wait_ge(qkv_lo, l + 1)
                load_attn_weights(l + 1, ["Wq", "Wk", "Wv"], raw_qkv_loaded)
                sp.wait_ge(o_lo, l + 1)
                load_attn_weights(l + 1, ["Wo"], raw_o_loaded)
                sp.wait_ge(vx_done, 2 * (NT * l + NT))
                load_rows(l + 1, ["bv"], rows_a, bv_loaded)
                sp.wait_ge(xbo_done, NT * l + NT)
                load_rows(l + 1, ["bo"], rows_a, bo_loaded)
                sp.wait_ge(w2_lo, l + 1)
                load_w1(l + 1)
                sp.wait_ge(ln_done[1], SB * (NT * l + NT))
                load_rows(l + 1, ["g1", "be1"], rows_a, ln1_rows_loaded)
                sp.wait_ge(xb2_done, NT * l + NT)
                load_rows(l + 1, ["b2"], rows_m, b2_loaded)
                sp.wait_ge(w1_lo, l + 2)
                load_w2(l + 1)
                sp.wait_ge(ln_done[2], SB * (NT * l + NT))
                load_rows(l + 1, ["g2", "be2"], rows_m, ln2_rows_loaded)

        @block.tensor
        def _(pe):
            def step(l, q, u, attn, mlp, following):
                t = u + 1
                ta = (q + 1) % NT
                la = l + 1 if q == NT - 1 else l

                def x_transpose(t, tile):
                    for c in range(KC):
                        wait(pe, aT_lo_done, 2 * (t - 1) + c + 1)
                        for s in range(SB):
                            mm = pe.transpose(ps_tr[c][:, blk(s)], X[:, tile * SB + s, blk(c)], ident[:, :])
                        mm.then_inc(xT_tr, 1)

                if q < 0:
                    pe.wait_ge(consts["ready"], consts["count"])
                    pe.wait_ge(x0_loaded, 16)
                    x_transpose(0, 0)

                def qk(j):
                    w = names_a[j // KC]
                    for c in range(KC):
                        cols = blk(j % KC)
                        mm = split3(pe, ps_pr[j % 2][:, :], (hi[w][:, c, cols], lo[w][:, c, cols]),
                                    (xT_hi[:, c, :], xT_lo[:, c, :]), c == 0, c == KC - 1)
                    mm.then_inc(qk_full, 1)

                if attn:
                    pe.wait_ge(qkv_lo, la + 1)
                    pe.wait_ge(xT_lo_done, 2 * t + 2)
                    for j in range(KC):
                        if mlp and lagging(u):
                            pe.wait_ge(gelu_done, FC * u - 1 + j)
                        elif mlp:
                            pe.wait_ge(kv_done, 2 * (t - 1) + j + 1)
                        qk(j)
                    for j in range(2):
                        if mlp and lagging(u):
                            pe.wait_ge(z_done[2], SB * u - 1 + j)
                        for s in (2 * j, 2 * j + 1):
                            for c in range(KC):
                                mm = split3(pe, ps_tk[j][:, (s % 2) * D:(s % 2 + 1) * D],
                                            (xT_hi[:, c, blk(s)], xT_lo[:, c, blk(s)]),
                                            (hi["Wv"][:, c, :], lo["Wv"][:, c, :]), c == 0, c == KC - 1)
                        mm.then_inc(v_full, 1)
                if mlp:
                    pe.wait_ge(ln_done[1], SB * u + SB)
                    for c in range(KC):
                        wait(pe, xT_lo_done if attn else aT_lo_done, 2 * t + c + 1 if attn else 2 * u + c + 1)
                        for s in range(SB):
                            mm = pe.transpose(ps_tr[c][:, blk(s)], X[:, q * SB + s, blk(c)], ident[:, :])
                        mm.then_inc(yT_tr, 1)

                if attn:
                    for j in range(KC, 2 * KC):
                        pe.wait_ge(phi_done, 4 * t + j - 1)
                        qk(j)

                def mlp_up(m):
                    if m < 2:
                        if attn:
                            pe.wait_ge(phi_done, 4 * t + 3 + m)
                        else:
                            pe.wait_ge(gelu_done, FC * u - 1 + m)
                    elif m in (4, 5) and attn:
                        pe.wait_ge(kv_done, 2 * t + m - 3)
                    else:
                        pe.wait_ge(gelu_done, FC * u + m - 1)
                    if m == 0:
                        pe.wait_ge(w1_lo, l + 1)
                        pe.wait_ge(yT_lo_done, 2 * u + 2)
                    for c in range(KC):
                        mm = split3(pe, ps_pr[m % 2][:, :], (hi["W1"][:, c, blk(m)], lo["W1"][:, c, blk(m)]),
                                    (yT_hi[:, c, :], yT_lo[:, c, :]), c == 0, c == KC - 1)
                    mm.then_inc(h_full, 1)

                def mlp_down(s, chunks=range(FC)):
                    if 0 in chunks:
                        if s < 2 and attn:
                            pe.wait_ge(a_done, SB * t + s + 3)
                        elif attn:
                            pe.wait_ge(z_done[1], SB * t + s + 1)
                        else:
                            pe.wait_ge(z_done[2], SB * u + s - 1)
                        if s == 0:
                            pe.wait_ge(w2_lo, l + 1)
                    for c in chunks:
                        if s == 0:
                            pe.wait_ge(h_lo_done, FC * u + c + 1)
                        mm = split3(pe, ps_tk[s % 2][:, 0:D], (h_hi[:, c, blk(s)], h_lo[:, c, blk(s)]),
                                    (hi["W2"][:, c, :], lo["W2"][:, c, :]), c == 0, c == FC - 1)
                    if FC - 1 in chunks:
                        mm.then_inc(m_full, 1)

                def scores(s, banks=range(4)):
                    for k in banks:
                        n = 4 * s + k
                        c, g = k // 2, k % 2
                        if n < 2:
                            wait(pe, am_done, 16 * (t - 1) + 15 + n) if q >= 0 else None
                        else:
                            pe.wait_ge(am_done, 16 * t + n - 1)
                        if s == 0 and k == 0:
                            pe.wait_ge(qx_done, t + 1)
                            pe.wait_ge(qx_act_done, t + 1)
                            pe.wait_ge(qx_pool_done, t + 1)
                        pe.matmul(ps_sc[n % 2][:, :], qkT[:, KC + c, blk(s)], qx[:, c, 4 * g:4 * g + 4, blk(s)],
                                  start=True, stop=True).then_inc(sc_full, 1)

                def attend(s, groups=range(4)):
                    out = ps_tk[s % 2]
                    if 0 in groups:
                        if s >= 2:
                            pe.wait_ge(a_done, SB * t + s - 1)
                        else:
                            pe.wait_ge(vx_done, 2 * t + s + 1)
                    if 0 in groups and s % 2 == 0:
                        pe.wait_ge(kv_done, 2 * t + s // 2 + 1)
                        for c in range(KC):
                            pe.matmul(out[:, c * HC * HX:(c + 1) * HC * HX], qkT[:, c, blk(s)], kv[:, s // 2, c, :],
                                      start=(c == 0), stop=False, skip_group_check=True)
                    for g in groups:
                        pe.wait_ge(am_done, 16 * t + 4 * s + g + 1)
                        for h in range(4 * g, 4 * g + 4):
                            mm = pe.matmul(out[:, h * HX:(h + 1) * HX], am[:, s % 2, g, h % 4, :], vx[:, s, h, :],
                                           start=(s % 2 == 1 and h == 0), stop=(h == H - 1), skip_group_check=True)
                    if 3 in groups:
                        mm.then_inc(out_full, 1)

                if mlp:
                    mlp_up(0)
                if attn:
                    pe.wait_ge(phi_done, 4 * t + 4)
                    pe.wait_ge(yT_lo_done if mlp else xT_lo_done, 2 * u + 2 if mlp else 2 * t + 2)
                    for b in range(2):
                        for c in range(KC):
                            mm = pe.transpose(ps_tr[0][:, blk(b * KC + c)], qkT[:, KC + c, blk(2 * b + 1)], ident[:, :])
                    mm.then_inc(ktr_full, 1)
                if mlp:
                    for m in range(1, 4):
                        mlp_up(m)
                if attn:
                    pe.wait_ge(ktok_done, t + 1)
                    pe.wait_ge(vx_done, 2 * t + 2)
                    for b in range(2):
                        if mlp:
                            pe.wait_ge(gelu_done, FC * u + 3 + b)
                        for c in range(KC):
                            mm = pe.matmul(ps_pr[b][:, c * HC * HX:(c + 1) * HC * HX], ktok[:, b, c, :],
                                           vx[:, 2 * b + 1, c * HC:(c + 1) * HC, :], start=True, stop=True,
                                           skip_group_check=True)
                        mm.then_inc(kv_full, 1)
                    scores(0)
                for s in range(SB):
                    for k in range(4):
                        if attn and s + 1 < SB:
                            scores(s + 1, [k])
                        if mlp and (s, k) in UP_AT:
                            mlp_up(UP_AT[s, k])
                        if attn:
                            attend(s, [k])
                        if mlp and s == SB - 1:
                            mlp_down(0, [2 * k, 2 * k + 1])
                if attn:
                    pe.wait_ge(a_done, SB * t + SB)
                    pe.wait_ge(ktok_done, t + 1)
                    for c in range(KC):
                        for s in range(SB):
                            mm = pe.transpose(ps_tr[c][:, blk(s)], a_tok[:, s, blk(c)], ident[:, :])
                        mm.then_inc(aT_tr, 1)
                if mlp:
                    mlp_down(1)
                if attn:
                    pe.wait_ge(o_lo, la + 1)
                    pe.wait_ge(aT_lo_done, 2 * t + 2)
                    for s in range(SB):
                        if s >= 2:
                            pe.wait_ge(z_done[1], SB * t + s - 1)
                        elif mlp:
                            pe.wait_ge(z_done[2], SB * u + s + 1)
                        for c in range(KC):
                            mm = split3(pe, ps_tk[s % 2][:, 0:D], (xT_hi[:, c, blk(s)], xT_lo[:, c, blk(s)]),
                                        (hi["Wo"][:, c, :], lo["Wo"][:, c, :]), c == 0, c == KC - 1)
                        mm.then_inc(wo_full, 1)
                if mlp:
                    mlp_down(2)
                if following:
                    if q < 0:
                        pe.wait_ge(x_loaded, 16)
                    x_transpose(t + 1, (q + 2) % NT)
                if mlp:
                    mlp_down(3)

            steps(pe, step)

        @block.scalar
        def _(act):
            def split_hi(raw, out, n, ready, value, done):
                act.wait_ge(ready, value)
                for j in range(n):
                    a = act.activation(out[j], raw[j], ACT.Copy)
                a.then_inc(done, 1)

            def split_qkv():
                pass

            def w_qkv(l):
                for j, w in enumerate(names_a[:3]):
                    a = act.activation(hi[w][:, :, :], raw_a[:, j], ACT.Copy)
                a.then_inc(qkv_hi, 1)

            def w_o(l):
                act.activation(hi["Wo"][:, :, :], raw_a[:, 3], ACT.Copy).then_inc(o_hi, 1)

            def w_m(w, done):
                flat = hi[w][:, :, :].rearrange("p c n -> p (c n)")
                for j in range(4):
                    a = act.activation(flat[:, j * TT:(j + 1) * TT], raw_m[:, j * TT:(j + 1) * TT], ACT.Copy)
                a.then_inc(done, 1)

            act.wait_ge(raw_qkv_loaded, 48)
            w_qkv(0)
            act.wait_ge(raw_o_loaded, 16)
            w_o(0)
            act.wait_ge(raw_1_loaded, 16)
            w_m("W1", w1_hi)

            def step(l, q, u, attn, mlp, following):
                t = u + 1
                more = not (isinstance(l, int) and l == L - 1)

                def x_hi(t):
                    for c in range(KC):
                        act.wait_ge(xT_tr, 2 * t + c + 1)
                        if c == 0:
                            wait(act, wo_full, SB * t)
                        act.activation(xT_hi[:, c, :], ps_tr[c][:, :], ACT.Copy).then_inc(xT_hi_done, 1)

                if q < 0:
                    x_hi(0)
                def exp(j):
                    act.wait_ge(qk_min, 4 * t + j + 1)
                    act.activation(qkT[:, j, :], qkT[:, j, :], ACT.Exp).then_inc(qk_exp, 1)

                if attn:
                    act.activation(table[:, :], consts["ident"][:, 0:1], ACT.Exp)
                    for j in range(KC):
                        exp(j)
                if mlp:
                    for c in range(KC):
                        act.wait_ge(yT_tr, 2 * u + c + 1)
                        act.activation(yT_hi[:, c, :], ps_tr[c][:, :], ACT.Copy).then_inc(yT_hi_done, 1)
                if attn:
                    for j in range(KC, 2 * KC):
                        exp(j)
                if mlp:
                    act.activation(table[:, :], consts["ident"][:, 0:1], ACT.Gelu)
                    if q == 0:
                        act.wait_ge(h_bias_set, l + 1)

                def gelu(m):
                    act.wait_ge(h_full, FC * u + m + 1)
                    if m >= HR:
                        act.wait_ge(h_lo_done, FC * u + m - HR + 1)
                    act.activation(h_f[:, m % HR, :], ps_pr[m % 2][:, :], ACT.Gelu,
                                   bias=h_bias[:, m:m + 1]).then_inc(gelu_done, 1)

                for m in range(4):
                    if mlp:
                        gelu(m)
                    if attn and m == 0:
                        act.wait_ge(ktr_full, t + 1)
                        act.activation(ktok[:, :, :, :], ps_tr[0][:, :].rearrange("p (b c n) -> p b c n", b=2, c=KC),
                                       ACT.Copy).then_inc(ktok_done, 1)
                    if attn:
                        if m == 0:
                            act.wait_ge(phi_done, 4 * t + 2)
                        c, h = m // 2, 2 * (m % 2)
                        a = act.activation(qx[:, c, h, :], qkT[:, c, :], ACT.Copy, scale=headmask[:, h:h + 1])
                        if m == 3:
                            a.then_inc(qx_act_done, 1)
                if q == 0:
                    act.wait_ge(raw_2_loaded, 16 * (l + 1))
                    if not isinstance(l, int) or l > 0:
                        wait(act, m_full, SB * NT * l)
                    w_m("W2", w2_hi)
                if more and q == NT - 2:
                    act.wait_ge(raw_qkv_loaded, 48 * (l + 2))
                    act.wait_ge(v_full, 2 * t + 2)
                    w_qkv(l + 1)
                if q == NT - 1 and attn:
                    act.wait_ge(raw_o_loaded, 16 * (l + 2))
                    act.wait_ge(wo_full, SB * t)
                    w_o(l + 1)
                if mlp:
                    for m in range(4, FC):
                        gelu(m)
                if attn:
                    for c in range(KC):
                        act.wait_ge(aT_tr, 2 * t + c + 1)
                        act.activation(xT_hi[:, c, :], ps_tr[c][:, :], ACT.Copy).then_inc(aT_hi_done, 1)
                if following:
                    x_hi(t + 1)
                if more and q == NT - 1:
                    act.wait_ge(raw_1_loaded, 16 * (l + 2))
                    act.wait_ge(h_full, FC * u + FC)
                    w_m("W1", w1_hi)

            steps(act, step)

        @block.gpsimd
        def _(pool):
            def lo_part(w, raw, n, done):
                flat_hi = hi[w][:, :, :].rearrange("p c n -> p (c n)").bitcast(F32)
                flat_lo = lo[w][:, :, :].rearrange("p c n -> p (c n)")
                for j in range(n):
                    cols = slice(j * TT, (j + 1) * TT)
                    a = pool.tensor_tensor(flat_lo[:, cols], raw[:, cols], flat_hi[:, cols], ALU.subtract)
                if done is not None:
                    a.then_inc(done, 1)

            def w_qkv(value):
                pool.wait_ge(qkv_hi, value)
                for j, w in enumerate(names_a[:3]):
                    lo_part(w, raw_a[:, j].rearrange("p c n -> p (c n)"), 1, qkv_lo if j == 2 else None)

            def w_o(value):
                pool.wait_ge(o_hi, value)
                lo_part("Wo", raw_a[:, 3].rearrange("p c n -> p (c n)"), 1, o_lo)

            def w_m(w, ready, value, done):
                pool.wait_ge(ready, value)
                lo_part(w, raw_m, 4, done)

            pool.memset(half[:, :], -0.5).then_inc(half_set, 1)
            w_qkv(1)
            w_o(1)
            w_m("W1", w1_hi, 1, w1_lo)

            def step(l, q, u, attn, mlp, following):
                t = u + 1
                ta = (q + 1) % NT
                la = l + 1 if q == NT - 1 else l
                more = not (isinstance(l, int) and l == L - 1)

                def add_row(tile, row, ready, value, loaded, want, done):
                    pool.wait_ge(loaded, want)
                    pool.wait_ge(ready, value)
                    v = X[:, tile * SB:(tile + 1) * SB, :]
                    pool.tensor_tensor(v, v, row[:, :].unsqueeze(1).broadcast_to([P, SB, D]), ALU.add).then_inc(done, 1)

                def rsqrt(i, ready, value):
                    if q <= 0:
                        pool.wait_ge(half_set, 1)
                    pool.wait_ge(ready, value)
                    pool.tensor_tensor(rs[i][:, :], ve[i][:, :], half[:, :], ALU.pow).then_inc(rs_done[i], 1)

                if q < 0:
                    add_row(0, rows_a["bo"], xT_tr, 2, bo_loaded, 16, xbo_done)
                if attn:
                    pool.wait_ge(phi_done, 4 * t + 2)
                    for c in range(KC):
                        for h in (4, 6):
                            a = pool.tensor_tensor(qx[:, c, h, :], qkT[:, c, :], headmask[:, h:h + 1].broadcast_to([P, TT]), ALU.mult)
                    a.then_inc(qx_pool_done, 1)
                if mlp:
                    add_row(q, rows_m["b2"], yT_tr, 2 * u + 2, b2_loaded, 16 * (l + 1), xb2_done)
                    for m in range(FC):
                        if m == 5 and lagging(u):
                            rsqrt(2, ve_done[2], u)
                        if m == 4 and q == 0:
                            w_m("W2", w2_hi, l + 1, w2_lo)
                        if m == 4 and more and q == NT - 2:
                            w_qkv(l + 2)
                        if m == 4 and attn and q == NT - 1:
                            w_o(l + 2)
                        pool.wait_ge(h_hi_done, FC * u + m + 1)
                        pool.tensor_tensor(h_lo[:, m, :], h_f[:, m % HR, :], h_hi[:, m, :].bitcast(F32),
                                           ALU.subtract).then_inc(h_lo_done, 1)
                if attn:
                    rsqrt(1, ve_done[1], t + 1)
                if following:
                    ln = l + 1 if q >= NT - 2 else l
                    add_row((q + 2) % NT, rows_a["bo"], xT_tr, 2 * t + 4, bo_loaded, 16 * (ln + 1), xbo_done)
                if not attn:
                    rsqrt(2, ve_done[2], u + 1)
                if more and q == NT - 1:
                    w_m("W1", w1_hi, l + 2, w1_lo)

            steps(pool, step)

        @block.vector
        def _(dve):
            def set_bias(out, every, n, l, done):
                dve.tensor_copy(out[:, :], every[:, bass.ds(l * n, n)]).then_inc(done, 1)

            dve.memset(vx[:, :, :, DH:HX], 1.0).then_inc(ones_set, 1)
            dve.wait_ge(biases_loaded, 16 * (2 * KC + FC))
            dve.tensor_copy(qk_bias[:, :], qk_bias_all[:, 0:2 * KC]).then_inc(qk_bias_set, 1)
            dve.tensor_scalar(qk_bias1[:, :], qk_bias_all[:, 0:2 * KC], 1.0, None, ALU.add).then_inc(qk_bias_set, 1)
            dve.tensor_copy(h_bias[:, :], h_bias_all[:, 0:FC]).then_inc(h_bias_set, 1)

            def step(l, q, u, attn, mlp, following):
                t = u + 1
                ta = (q + 1) % NT
                la = l + 1 if q == NT - 1 else l
                more = not (isinstance(l, int) and l == L - 1)

                def low(out, bank, part):
                    return dve.tensor_tensor(out, bank, part.bitcast(F32), ALU.subtract)

                def hidden_hi(m):
                    dve.wait_ge(gelu_done, FC * u + m + 1)
                    dve.tensor_copy(h_hi[:, m, :], h_f[:, m % HR, :]).then_inc(h_hi_done, 1)

                def mask(s):
                    for k in range(4):
                        n = 4 * s + k
                        dve.wait_ge(sc_full, 16 * t + n + 1)
                        if s >= 2 and k == 0:
                            dve.wait_ge(out_full, SB * t + s - 1)
                        dve.tensor_tensor(am[:, s % 2, k, :, :],
                                          ps_sc[n % 2][:, :].rearrange("p (h n) -> p h n", n=P),
                                          amask[:, :].unsqueeze(1).broadcast_to([P, 4, P]), ALU.mult).then_inc(am_done, 1)

                def divide(s):
                    dve.wait_ge(out_full, SB * t + s + 1)
                    o = ps_tk[s % 2][:, 0:H * HX].rearrange("p (h d) -> p h d", d=HX)
                    dve.tensor_scalar(den[:, s, :].unsqueeze(2), o[:, :, DH:HX], DEN_EPS, None, ALU.add).then_inc(den_done, 1)
                    dve.wait_ge(den_done, SB * t + s + 1)
                    dve.reciprocal(rden[:, s, :], den[:, s, :]).then_inc(rden_done, 1)
                    dve.wait_ge(rden_done, SB * t + s + 1)
                    dve.tensor_tensor(a_tok[:, s, :].rearrange("p (h d) -> p h d", d=DH), o[:, :, 0:DH],
                                      rden[:, s, :].unsqueeze(2).broadcast_to([P, H, DH]), ALU.mult).then_inc(a_done, 1)

                def residual(i, s, n, tile, ready, added):
                    dve.wait_ge(ready, SB * n + s + 1)
                    if s == 0:
                        dve.wait_ge(added, n + 1)
                    x = X[:, tile * SB + s, :]
                    dve.tensor_tensor(x, ps_tk[s % 2][:, 0:D], x, ALU.add).then_inc(z_done[i], 1)

                def statistics(i, n, tile):
                    for s in range(SB):
                        dve.wait_ge(z_done[i], SB * n + s + 1)
                        dve.bn_stats(st[i][:, s, :], X[:, tile * SB + s, :]).then_inc(st_done[i], 1)
                    dve.wait_ge(st_done[i], SB * n + SB)
                    dve.memset(ve[i][:, :], LN_EPS)
                    for s in range(SB):
                        dve.bn_aggr(mv[i][:, s, :], st[i][:, s, :]).then_inc(mv_done[i], 1)
                    dve.wait_ge(mv_done[i], SB * n + SB)
                    dve.tensor_tensor(ve[i][:, :].unsqueeze(2), ve[i][:, :].unsqueeze(2), mv[i][:, :, 1:2], ALU.add).then_inc(ve_done[i], 1)

                def centre(i, n, tile, gain, loaded, want):
                    dve.wait_ge(loaded, want)
                    dve.wait_ge(mv_done[i], SB * n + SB)
                    for s in range(SB):
                        x = X[:, tile * SB + s, :]
                        dve.scalar_tensor_tensor(x, x, mv[i][:, s, 0:1], gain[:, :], ALU.subtract, ALU.mult).then_inc(xc_done[i], 1)

                def scale(i, n, tile, bias):
                    dve.wait_ge(rs_done[i], n + 1)
                    for s in range(SB):
                        x = X[:, tile * SB + s, :]
                        dve.wait_ge(xc_done[i], SB * n + s + 1)
                        dve.scalar_tensor_tensor(x, x, rs[i][:, s:s + 1], bias[:, :], ALU.mult, ALU.add).then_inc(ln_done[i], 1)

                def negative(j):
                    dve.wait_ge(qk_full, 4 * t + j + 1)
                    if j == 0 and (q < 0 or q == NT - 1):
                        dve.wait_ge(qk_bias_set, 2 * (la + 1))
                    dve.tensor_scalar(qkT[:, j, :], ps_pr[j % 2][:, :], qk_bias[:, j:j + 1], 0.0,
                                      ALU.add, ALU.min).then_inc(qk_min, 1)

                def phi(j):
                    dve.wait_ge(qk_exp, 4 * t + j + 1)
                    dve.scalar_tensor_tensor(qkT[:, j, :], ps_pr[j % 2][:, :], qk_bias1[:, j:j + 1], qkT[:, j, :],
                                             ALU.add, ALU.max).then_inc(phi_done, 1)

                def x_lo(t):
                    for c in range(KC):
                        dve.wait_ge(xT_hi_done, 2 * t + c + 1)
                        low(xT_lo[:, c, :], ps_tr[c][:, :], xT_hi[:, c, :]).then_inc(xT_lo_done, 1)

                if q < 0:
                    x_lo(0)
                if attn:
                    negative(0)
                    negative(1)
                if mlp:
                    scale(1, u, q, rows_a["be1"])
                if attn:
                    phi(0)
                    phi(1)
                if mlp:
                    for c in range(KC):
                        dve.wait_ge(yT_hi_done, 2 * u + c + 1)
                        low(yT_lo[:, c, :], ps_tr[c][:, :], yT_hi[:, c, :]).then_inc(yT_lo_done, 1)
                if attn:
                    if q < 0 or q == NT - 1:
                        dve.wait_ge(bv_loaded, 16 * (la + 1))
                    for j in range(2):
                        negative(KC + j)
                        dve.wait_ge(v_full, 2 * t + j + 1)
                        dve.tensor_tensor(
                            vx[:, 2 * j:2 * j + 2, :, 0:DH], ps_tk[j][:, :].rearrange("p (s h d) -> p s h d", s=2, d=DH),
                            rows_a["bv"][:, :].rearrange("p (h d) -> p h d", d=DH).unsqueeze(1).broadcast_to([P, 2, H, DH]),
                            ALU.add).then_inc(vx_done, 1)
                        phi(KC + j)
                last = (q - 1) % NT
                rows = 32 * (l if q == 0 else l + 1)
                for c in range(KC):
                    if attn:
                        if c == 0:
                            dve.wait_ge(phi_done, 4 * t + 2)
                        for h in range(1, HC, 2):
                            a = dve.tensor_scalar(qx[:, c, h, :], qkT[:, c, :], headmask[:, h:h + 1], None, ALU.mult)
                        if c == KC - 1:
                            a.then_inc(qx_done, 1)
                    if mlp:
                        hidden_hi(2 * c)
                        hidden_hi(2 * c + 1)
                if more and q == NT - 2:
                    set_bias(qk_bias, qk_bias_all, 2 * KC, l + 1, qk_bias_set)
                    dve.tensor_scalar(qk_bias1[:, :], qk_bias_all[:, bass.ds((l + 1) * 2 * KC, 2 * KC)], 1.0, None,
                                      ALU.add).then_inc(qk_bias_set, 1)
                if attn:
                    for b in range(2):
                        dve.wait_ge(kv_full, 2 * t + b + 1)
                        dve.tensor_tensor(kv[:, b, :, :], ps_pr[b][:, 0:KC * HC * HX].rearrange("p (c n) -> p c n", c=KC),
                                          blockmask[:, :].unsqueeze(1).broadcast_to([P, KC, HC * HX]), ALU.mult).then_inc(kv_done, 1)
                    mask(0)
                for s in range(SB):
                    if attn and s + 1 < SB:
                        mask(s + 1)
                    for k in range(4):
                        if mlp and (s, k) in UP_AT:
                            hidden_hi(UP_AT[s, k])
                    if attn:
                        divide(s)
                    if mlp and lagging(u):
                        if s == 0:
                            statistics(2, u - 1, last)
                        elif s == 1:
                            centre(2, u - 1, last, rows_m["g2"], ln2_rows_loaded, rows)
                        elif s == 2:
                            scale(2, u - 1, last, rows_m["be2"])
                if more and q == NT - 1:
                    set_bias(h_bias, h_bias_all, FC, l + 1, h_bias_set)
                if mlp:
                    residual(2, 0, u, q, m_full, xb2_done)
                if attn:
                    for c in range(KC):
                        dve.wait_ge(aT_hi_done, 2 * t + c + 1)
                        low(xT_lo[:, c, :], ps_tr[c][:, :], xT_hi[:, c, :]).then_inc(aT_lo_done, 1)
                if mlp:
                    residual(2, 1, u, q, m_full, xb2_done)
                if attn:
                    for s in range(SB):
                        residual(1, s, t, ta, wo_full, xbo_done)
                    statistics(1, t, ta)
                if mlp:
                    residual(2, 2, u, q, m_full, xb2_done)
                if attn:
                    centre(1, t, ta, rows_a["g1"], ln1_rows_loaded, 32 * (la + 1))
                if following:
                    x_lo(t + 1)
                if mlp:
                    residual(2, 3, u, q, m_full, xb2_done)
                if not attn:
                    statistics(2, u, q)
                    centre(2, u, q, rows_m["g2"], ln2_rows_loaded, 32 * (l + 1))
                    scale(2, u, q, rows_m["be2"])

            steps(dve, step)

    own.close()


def cross(nc, ctx, consts, X, dram):
    own = ExitStack()

    def sb(name, shape, dt=F32):
        return own.enter_context(nc.sbuf_tensor("x_" + name, [P] + shape, dt))

    def sem(name):
        return ctx.enter_context(nc.semaphore("x_" + name))

    NP = H // 2
    QB = S // P
    NU = QB * NP
    NJ = 2 * NP
    REP = 4
    XS = 3 * QB + 1
    LS = 2 * QB + 1
    AS = 6
    ident, headmask = consts["ident"], consts["headmask"]
    names_w = ["wq1", "wq2", "wk1", "wk2", "wv"]

    raw_w, raw_wo = sb("raw_w", [5, KC, DH]), sb("raw_wo", [KC, D])
    bd = sb("bd", [5 * KC, HC, DH])
    w4 = sb("w4", [4, KC, HC, REP, DH])
    wv = sb("wv", [KC, P])
    woT = sb("woT", [KC, D])
    gain, gf, bf = sb("gain", [1]), sb("gf", [D]), sb("bf", [D])
    neg_gain = sb("neg_gain", [1])
    qlow, klow = sb("qlow", [1]), sb("klow", [1])
    half, halfh = sb("half", [QB]), sb("halfh", [H])

    xo, ctok = sb("xo", [QB, D]), sb("ctok", [QB, D])
    xw = sb("xw", [QB, D])
    x1 = sb("x1", [2, QB, D])
    x1T, cT = sb("x1T", [KC, S]), sb("cT", [KC, S])
    part = sb("part", [2, 2, S], F32R)
    qs, ks = sb("qs", [2, NP, 2, S], F32R), sb("ks", [2, NP, 2, S], F32R)
    vp = sb("vp", [2, QB, D])
    mx = sb("mx", [2, 2, 2])
    ex = sb("ex", [2, 4, S])
    sums = sb("sums", [2, QB, 2, H])
    rec2, ratio = sb("rec2", [2, 2]), sb("ratio", [2, 2])
    pr = sb("pr", [2, 2, S])
    pT = sb("pT", [2, 2 * QB, P])
    r1, o = sb("r1", [QB, H]), sb("o", [QB, D])
    om, sq, ov, ors = sb("om", [QB, H]), sb("sq", [QB, D]), sb("ov", [QB, H]), sb("ors", [QB, H])
    on, oT = sb("on", [QB, D]), sb("oT", [KC, S])
    z = sb("z", [QB, D])
    st = [sb(f"st{k}", [QB, 6]) for k in range(3)]
    mv = [sb(f"mv{k}", [QB, 2]) for k in range(3)]
    ve = [sb(f"ve{k}", [QB]) for k in range(3)]
    rs = [sb(f"rs{k}", [QB]) for k in range(3)]

    ps_sc = [own.enter_context(nc.psum_tensor(f"x_sc{i}", [P, 2, TT], F32)) for i in range(2)]
    ps_pj = [own.enter_context(nc.psum_tensor(f"x_pj{i}", [P, TT], F32)) for i in range(2)]
    ps_tr = own.enter_context(nc.psum_tensor("x_tr", [P, TT], F32))
    ps_ov = own.enter_context(nc.psum_tensor("x_att", [P, TT], F32))

    w_loaded, wo_loaded, gain_loaded, rows_loaded = sem("w_loaded"), sem("wo_loaded"), sem("gain_loaded"), sem("rows_loaded")
    xo_loaded, c_loaded = sem("xo_loaded"), sem("c_loaded")
    half_set, scalars_set = sem("half_set"), sem("scalars_set")
    bd_done, prep_tr, prep_copied = sem("bd_done"), sem("prep_tr"), sem("prep_copied")
    ln_step = [sem(f"ln{k}_step") for k in range(3)]
    rs_done = [sem(f"rs{k}_done") for k in range(3)]
    x1_step, z_done = sem("x1_step"), sem("z_done")
    c_tr, cT_done, x1_tr, x1T_done = sem("c_tr"), sem("cT_done"), sem("x1_tr"), sem("x1T_done")
    pj_full, part_done, pj_done = sem("pj_full"), sem("part_done"), sem("pj_done")
    v_full, v_done = sem("v_full"), sem("v_done")
    sc_full, mx_done, ex_done = sem("sc_full"), sem("mx_done"), sem("ex_done")
    ratio_step, pr_done = sem("ratio_step"), sem("pr_done")
    p_tr, pT_done, ov_full = sem("p_tr"), sem("pT_done"), sem("ov_full")
    o_read, norm_step, ors_done, on_done = sem("o_read"), sem("norm_step"), sem("ors_done"), sem("on_done")
    o_tr, oT_done, wo_full = sem("o_tr"), sem("oT_done"), sem("wo_full")

    CTX, X1T, V, OT, WO = 0, 8, 9, 5, 6
    K_AT = [1, 2, 3, 4, 5, 6, 7, 8]
    Q_AT = [9, 10, 11, 12, 13, 14, 15, 15]
    PJ_AT = K_AT + Q_AT

    def steps(eng, prepare, seq, tail):
        prepare()
        seq(0, 0, False, True)
        with eng.Fori(0, B // 2 - 1) as g:
            seq(2 * g + 1, 1, True, True)
            seq(2 * g + 2, 0, True, True)
        seq(B - 1, 1, True, False)
        tail()

    def unit(b, j, n):
        if n >= NU:
            return b + 1, 1 - j, n - NU, NU * b + n
        if n < 0:
            return b - 1, 1 - j, n + NU, NU * b + n
        return b, j, n, NU * b + n

    def prep_items():
        return [("w", i, c) for i in range(5) for c in range(KC)] + [("wo", n, m) for n in range(KC) for m in range(KC)]

    def prep_bank(n):
        return ps_pj[n % 2][:, 0:P]

    with nc.Block() as block:

        @block.sync
        def _(sp):
            xv = dram["x"].rearrange("b (h p) d -> p (b h) d", p=P)
            cv = dram["ctx"].rearrange("b (h p) d -> p (b h) d", p=P)
            for i, w in enumerate(names_w):
                sp.dma_start(raw_w[:, i], dram[w].rearrange("(c h) e d -> (h e) c d", c=KC)).then_inc(w_loaded, 16)
            sp.dma_start(gf[:, :], dram["gf"].partition_broadcast(P)).then_inc(rows_loaded, 16)
            sp.dma_start(bf[:, :], dram["bf"].partition_broadcast(P)).then_inc(rows_loaded, 16)
            sp.dma_start(gain[:, :], dram["gain"].partition_broadcast(P)).then_inc(gain_loaded, 16)
            sp.dma_start(ctok[:, :, :], cv[:, 0:QB]).then_inc(c_loaded, 16)
            sp.dma_start(xo[:, :, :], xv[:, 0:QB]).then_inc(xo_loaded, 16)
            sp.dma_start(raw_wo[:, :, :], dram["wo"].rearrange("(c p) m -> p c m", p=P)).then_inc(wo_loaded, 16)
            with sp.Fori(1, B) as e:
                sp.wait_ge(c_tr, e)
                sp.dma_start(ctok[:, :, :], cv[:, bass.ds(e * QB, QB)]).then_inc(c_loaded, 16)
                sp.wait_ge(x1_step, XS * e - QB)
                sp.dma_start(xo[:, :, :], xv[:, bass.ds(e * QB, QB)]).then_inc(xo_loaded, 16)

        @block.tensor
        def _(pe):
            for n, (kind, i, c) in enumerate(prep_items()):
                if kind == "w":
                    pe.wait_ge(bd_done, i * KC + c + 1)
                    src = bd[:, i * KC + c, :, :].rearrange("p h d -> p (h d)")
                else:
                    if i == 0 and c == 0:
                        pe.wait_ge(wo_loaded, 16)
                    src = raw_wo[:, i, blk(c)]
                if n >= 2:
                    pe.wait_ge(prep_copied, n - 1)
                pe.transpose(prep_bank(n), src, ident[:, :]).then_inc(prep_tr, 1)
            pe.wait_ge(prep_copied, len(prep_items()))

            def transpose_to(bank, src):
                for c in range(KC):
                    for s in range(QB):
                        mm = pe.transpose(bank[:, (c * QB + s) * P:(c * QB + s + 1) * P], src[:, s, blk(c)], ident[:, :])
                return mm

            def context(e):
                pe.wait_ge(c_loaded, 16 * e + 16)
                transpose_to(ps_tr, ctok).then_inc(c_tr, 1)

            def project(e, p):
                bank = ps_pj[p % 2]
                wait(pe, pj_done, NJ * e + p - 1)
                if p == 0:
                    pe.wait_ge(cT_done, e + 1)
                elif p == NP:
                    pe.wait_ge(x1T_done, e + 1)
                r, c = p % NP, (p % NP) // (HC // 2)
                src = cT if p < NP else x1T
                for k in range(2):
                    w = (2 if p < NP else 0) + k
                    h = 2 * r % HC
                    mm = pe.matmul(bank[:, k * S:(k + 1) * S], w4[:, w, c, h:h + 2, :, :].rearrange("p h r e -> p (h r e)"),
                                   src[:, c, :], start=True, stop=True, skip_group_check=True)
                mm.then_inc(pj_full, 1)

            def values(e):
                for s in range(QB):
                    for c in range(KC):
                        mm = pe.matmul(ps_tr[:, s * D + c * P:s * D + (c + 1) * P], cT[:, c, blk(s)], wv[:, c, :],
                                       start=True, stop=True, skip_group_check=True)
                mm.then_inc(v_full, 1)

            def x1_transpose(e, j):
                pe.wait_ge(x1_step, XS * e + XS)
                transpose_to(ps_tr, x1[:, j]).then_inc(x1_tr, 1)

            def scores(b, j, n):
                b, j, n, N = unit(b, j, n)
                i, r = n // NP, n % NP
                pe.wait_ge(pj_done, NJ * b + NP + r + 1)
                if not isinstance(N, int) or N >= 2:
                    pe.wait_ge(ex_done, N - 1)
                for k in range(2):
                    for a in range(2):
                        rows = slice(64 * a, 64 * a + 64)
                        mm = pe.matmul(ps_sc[n % 2][:, a, k * S:(k + 1) * S], qs[rows, j, r, k, blk(i)], ks[rows, j, r, k, :],
                                       start=True, stop=True, skip_group_check=True)
                mm.then_inc(sc_full, 1)

            def transposes(b, j, n):
                b, j, n, N = unit(b, j, n)
                pe.wait_ge(pr_done, N + 1)
                wait(pe, pT_done, N)
                for a in range(2):
                    for c in range(QB):
                        mm = pe.transpose(ps_tr[:, blk(a * QB + c)], pr[:, n % 2, a, blk(c)], ident[:, :])
                mm.then_inc(p_tr, 1)

            def attend(b, j, n):
                b, j, n, N = unit(b, j, n)
                i, r = n // NP, n % NP
                pe.wait_ge(pT_done, N + 1)
                if r == 0:
                    if i == 0:
                        pe.wait_ge(v_done, b + 1)
                    wait(pe, o_read, QB * b + i)
                for a in range(2):
                    h = 2 * r + a
                    for c in range(QB):
                        mm = pe.matmul(ps_ov[:, h * DH:(h + 1) * DH], pT[:, n % 2, a * QB + c, :], vp[:, j, c, h * DH:(h + 1) * DH],
                                       start=(h == 0 and c == 0), stop=(c == QB - 1), skip_group_check=True)
                if r == NP - 1:
                    mm.then_inc(ov_full, 1)

            def out_transpose(d):
                pe.wait_ge(on_done, QB * d + QB)
                transpose_to(ps_tr, on).then_inc(o_tr, 1)

            def out_project(d):
                pe.wait_ge(oT_done, d + 1)
                for s in range(QB):
                    for c in range(KC):
                        mm = pe.matmul(ps_tr[:, s * D:(s + 1) * D], oT[:, c, blk(s)], woT[:, c, :], start=(c == 0),
                                       stop=(c == KC - 1), skip_group_check=True)
                mm.then_inc(wo_full, 1)

            def projections(n, e):
                for p in range(NJ):
                    if PJ_AT[p] == n:
                        project(e, p)

            def beside(n, b, j, before, after):
                e, d = b + 1, b - 1
                if (after and n in (CTX, X1T, V)) or (before and n in (OT, WO)):
                    wait(pe, pT_done, NU * b + n)
                if after and n == CTX:
                    context(e)
                    pe.wait_ge(cT_done, e + 1)
                if before and n == OT:
                    out_transpose(d)
                    pe.wait_ge(oT_done, d + 1)
                if before and n == WO:
                    out_project(d)
                    pe.wait_ge(z_done, d + 1)
                if after and n == X1T:
                    x1_transpose(e, 1 - j)
                    pe.wait_ge(x1T_done, e + 1)
                if after and n == V:
                    values(e)
                    pe.wait_ge(v_done, e + 1)

            def prepare():
                for n in range(NU):
                    beside(n, -1, 1, False, True)
                    projections(n, 0)
                scores(0, 0, 0)
                scores(0, 0, 1)

            def seq(b, j, before, after):
                for n in range(NU):
                    if after or n + 2 < NU:
                        scores(b, j, n + 2)
                    if after:
                        projections(n, b + 1)
                    if before or n >= 2:
                        attend(b, j, n - 2)
                    beside(n, b, j, before, after)
                    transposes(b, j, n)

            def tail():
                attend(B - 1, 1, NU - 2)
                attend(B - 1, 1, NU - 1)
                out_transpose(B - 1)
                out_project(B - 1)

            steps(pe, prepare, seq, tail)

        @block.scalar
        def _(act):
            for n, (kind, i, c) in enumerate(prep_items()):
                act.wait_ge(prep_tr, n + 1)
                src = prep_bank(n)
                if kind == "w" and i < 4:
                    out = w4[:, i, c, :, :, :]
                    src = src.rearrange("p (h e) -> p h e", e=DH).unsqueeze(2).broadcast_to([P, HC, REP, DH])
                    a = act.activation(out, src, ACT.Copy, scale=DH ** -0.5 if i < 2 else 1.0)
                elif kind == "w":
                    a = act.activation(wv[:, c, :], src, ACT.Copy)
                else:
                    a = act.activation(woT[:, c, blk(i)], src, ACT.Copy)
                a.then_inc(prep_copied, 1)

            def copy(out, bank, ready, value, done):
                act.wait_ge(ready, value)
                act.activation(out.rearrange("p c n -> p (c n)"), bank[:, :], ACT.Copy).then_inc(done, 1)

            def rounded(e, p):
                act.wait_ge(pj_full, NJ * e + p + 1)
                if p >= 2:
                    act.wait_ge(pj_done, NJ * e + p - 1)
                act.activation(part[:, p % 2, :, :].rearrange("p k n -> p (k n)"), ps_pj[p % 2][:, :], ACT.Copy).then_inc(part_done, 1)

            def exps(b, j, n):
                b, j, n, N = unit(b, j, n)
                i, r = n // NP, n % NP
                act.wait_ge(mx_done, N + 1)
                if not isinstance(N, int) or N >= 2:
                    act.wait_ge(pr_done, N - 1)
                for a in range(2):
                    for k in range(2):
                        x = act.activation(ex[:, n % 2, 2 * a + k, :], ps_sc[n % 2][:, a, k * S:(k + 1) * S], ACT.Exp,
                                           bias=mx[:, n % 2, a, k:k + 1],
                                           accum_out=sums[:, j, i, k, 2 * r + a:2 * r + a + 1])
                x.then_inc(ex_done, 1)

            def probs(b, j, n):
                b, j, n, N = unit(b, j, n)
                copy(pT[:, n % 2, :, :], ps_tr, p_tr, N + 1, pT_done)

            def beside(n, b, j, before, after):
                e = b + 1
                if after and n == CTX:
                    copy(cT[:, :, :], ps_tr, c_tr, e + 1, cT_done)
                if before and n == OT:
                    copy(oT[:, :, :], ps_tr, o_tr, b, oT_done)
                if after and n == X1T:
                    copy(x1T[:, :, :], ps_tr, x1_tr, e + 1, x1T_done)
                if after and n == V:
                    copy(vp[:, 1 - j], ps_tr, v_full, e + 1, v_done)

            def projections(n, e):
                for p in range(NJ):
                    if PJ_AT[p] == n:
                        rounded(e, p)

            def prepare():
                for n in range(NU):
                    beside(n, -1, 1, False, True)
                    projections(n, 0)
                exps(0, 0, 0)

            def seq(b, j, before, after):
                for n in range(NU):
                    if after or n + 1 < NU:
                        exps(b, j, n + 1)
                    if before or n >= 1:
                        probs(b, j, n - 1)
                    beside(n, b, j, before, after)
                    if after:
                        projections(n, b + 1)

            def tail():
                probs(B - 1, 1, NU - 1)
                copy(oT[:, :, :], ps_tr, o_tr, B, oT_done)

            steps(act, prepare, seq, tail)

        @block.gpsimd
        def _(pool):
            pool.memset(half[:, :], -0.5).then_inc(half_set, 1)
            pool.memset(halfh[:, :], -0.5).then_inc(half_set, 1)
            pool.wait_ge(half_set, 2)

            def rsqrt(k, i):
                pool.wait_ge(ln_step[k], LS * i + LS)
                pool.tensor_tensor(rs[k][:, :], ve[k][:, :], half[:, :], ALU.pow).then_inc(rs_done[k], 1)

            def heads_rsqrt(b, i):
                pool.wait_ge(norm_step, AS * (QB * b + i) + AS)
                pool.tensor_tensor(ors[:, i, :], ov[:, i, :], halfh[:, :], ALU.pow).then_inc(ors_done, 1)

            def prepare():
                rsqrt(0, 0)
                rsqrt(1, 0)

            def seq(b, j, before, after):
                if after:
                    rsqrt(0, b + 1)
                if before:
                    heads_rsqrt(b - 1, 1)
                if after:
                    rsqrt(1, b + 1)
                if before:
                    rsqrt(2, b - 1)
                heads_rsqrt(b, 0)

            def tail():
                heads_rsqrt(B - 1, 1)
                rsqrt(2, B - 1)

            steps(pool, prepare, seq, tail)

        @block.vector
        def _(dve):
            dve.tensor_reduce(qlow[:, :], headmask[:, 1::2], AX.X, ALU.add, negate=True).then_inc(scalars_set, 1)
            dve.tensor_reduce(klow[:, :], headmask[:, :].rearrange("p (a b c) -> p a b c", b=2, c=2)[:, :, 1, :],
                              AX.XY, ALU.add, negate=True).then_inc(scalars_set, 1)
            dve.wait_ge(w_loaded, 16 * 5)
            for i in range(5):
                for c in range(KC):
                    dve.tensor_tensor(bd[:, i * KC + c, :, :], raw_w[:, i, c, :].unsqueeze(1).broadcast_to([P, HC, DH]),
                                      headmask[:, :].unsqueeze(2).broadcast_to([P, HC, DH]), ALU.mult).then_inc(bd_done, 1)
            dve.wait_ge(gain_loaded, 16)
            dve.tensor_scalar(neg_gain[:, :], gain[:, :], -1.0, None, ALU.mult).then_inc(scalars_set, 1)
            dve.wait_ge(rows_loaded, 32)
            dve.wait_ge(scalars_set, 3)

            def xt(b, s):
                return X[:, bass.ds(b * QB + s, 1), :].rearrange("p o d -> p (o d)")

            def statistics(k, i, src):
                for s in range(QB):
                    dve.bn_stats(st[k][:, s, :], src(s)).then_inc(ln_step[k], 1)
                dve.wait_ge(ln_step[k], LS * i + QB)
                dve.memset(ve[k][:, :], LN_EPS)
                for s in range(QB):
                    dve.bn_aggr(mv[k][:, s, :], st[k][:, s, :]).then_inc(ln_step[k], 1)
                dve.wait_ge(ln_step[k], LS * i + 2 * QB)
                dve.tensor_tensor(ve[k][:, :].unsqueeze(2), ve[k][:, :].unsqueeze(2), mv[k][:, :, 1:2], ALU.add).then_inc(ln_step[k], 1)

            def encoder_norm_a(e):
                statistics(0, e, lambda s: xt(e, s))

            def encoder_norm_b(e):
                for s in range(QB):
                    dve.scalar_tensor_tensor(xw[:, s, :], xt(e, s), mv[0][:, s, 0:1], gf[:, :], ALU.subtract, ALU.mult).then_inc(x1_step, 1)

            def encoder_norm_c(e):
                dve.wait_ge(rs_done[0], e + 1)
                for s in range(QB):
                    dve.wait_ge(x1_step, XS * e + s + 1)
                    dve.scalar_tensor_tensor(xw[:, s, :], xw[:, s, :], rs[0][:, s:s + 1], bf[:, :], ALU.mult, ALU.add).then_inc(x1_step, 1)

            def add_x(e):
                dve.wait_ge(x1_step, XS * e + 2 * QB)
                dve.wait_ge(xo_loaded, 16 * e + 16)
                dve.tensor_tensor(xw[:, :, :], xw[:, :, :], xo[:, :, :], ALU.add).then_inc(x1_step, 1)

            def x1_norm_a(e):
                dve.wait_ge(x1_step, XS * e + 2 * QB + 1)
                statistics(1, e, lambda s: xw[:, s, :])

            def x1_norm_b(e, j):
                dve.wait_ge(rs_done[1], e + 1)
                for s in range(QB):
                    dve.tensor_scalar(x1[:, j, s, :], xw[:, s, :], mv[1][:, s, 0:1], rs[1][:, s:s + 1],
                                      ALU.subtract, ALU.mult).then_inc(x1_step, 1)

            def stacked(e, j, p):
                out, low = (ks, klow) if p < NP else (qs, qlow)
                dve.wait_ge(part_done, NJ * e + p + 1)
                dve.scalar_tensor_tensor(out[:, j, p % NP, :, :].rearrange("p k n -> p (k n)"),
                                         part[:, p % 2, :, :].rearrange("p k n -> p (k n)").bitcast(F32), low[:, :],
                                         ps_pj[p % 2][:, :], ALU.mult, ALU.add).then_inc(pj_done, 1)

            def maxima(b, j, n):
                b, j, n, N = unit(b, j, n)
                dve.wait_ge(sc_full, N + 1)
                if not isinstance(N, int) or N >= 2:
                    dve.wait_ge(ex_done, N - 1)
                dve.tensor_reduce(mx[:, n % 2, :, :], ps_sc[n % 2][:, :, :].rearrange("p a (k j) -> p a k j", j=S),
                                  AX.X, ALU.max, negate=True).then_inc(mx_done, 1)

            def combine(b, j, n):
                b, j, n, N = unit(b, j, n)
                i, r = n // NP, n % NP
                dve.wait_ge(ex_done, N + 1)
                dve.reciprocal(rec2[:, n % 2, :], sums[:, j, i, 1, 2 * r:2 * r + 2]).then_inc(ratio_step, 1)
                dve.wait_ge(ratio_step, 2 * N + 1)
                dve.scalar_tensor_tensor(ratio[:, n % 2, :], sums[:, j, i, 0, 2 * r:2 * r + 2], neg_gain[:, :],
                                         rec2[:, n % 2, :], ALU.mult, ALU.mult).then_inc(ratio_step, 1)
                dve.wait_ge(ratio_step, 2 * N + 2)
                if not isinstance(N, int) or N >= 2:
                    dve.wait_ge(p_tr, N - 1)
                for a in range(2):
                    d = dve.scalar_tensor_tensor(pr[:, n % 2, a, :], ex[:, n % 2, 2 * a + 1, :], ratio[:, n % 2, a:a + 1],
                                                 ex[:, n % 2, 2 * a, :], ALU.mult, ALU.add)
                d.then_inc(pr_done, 1)

            def heads(ap):
                return ap.rearrange("p (h d) -> p h d", d=DH)

            def spread(ap):
                return ap.unsqueeze(2).broadcast_to([P, H, DH])

            def norm_a(b, j, i):
                at = AS * (QB * b + i)
                dve.reciprocal(r1[:, i, :], sums[:, j, i, 0, :]).then_inc(norm_step, 1)
                dve.wait_ge(ov_full, QB * b + i + 1)
                dve.wait_ge(norm_step, at + 1)
                dve.tensor_tensor(heads(o[:, i, :]), heads(ps_ov[:, 0:D]), spread(r1[:, i, :]), ALU.mult).then_inc(o_read, 1)

            def norm_b(b, j, i):
                at = AS * (QB * b + i)
                dve.wait_ge(o_read, QB * b + i + 1)
                dve.tensor_reduce(om[:, i, :], heads(o[:, i, :]), AX.X, ALU.add).then_inc(norm_step, 1)
                dve.wait_ge(norm_step, at + 2)
                dve.scalar_tensor_tensor(heads(o[:, i, :]), spread(om[:, i, :]), -1.0 / DH, heads(o[:, i, :]),
                                         ALU.mult, ALU.add).then_inc(norm_step, 1)
                dve.wait_ge(norm_step, at + 3)
                dve.tensor_tensor(sq[:, i, :], o[:, i, :], o[:, i, :], ALU.mult).then_inc(norm_step, 1)
                dve.wait_ge(norm_step, at + 4)
                dve.tensor_reduce(om[:, i, :], heads(sq[:, i, :]), AX.X, ALU.add).then_inc(norm_step, 1)
                dve.wait_ge(norm_step, at + 5)
                dve.tensor_scalar(ov[:, i, :], om[:, i, :], 1.0 / DH, LN_EPS, ALU.mult, ALU.add).then_inc(norm_step, 1)

            def norm_c(b, i):
                dve.wait_ge(ors_done, QB * b + i + 1)
                dve.tensor_tensor(heads(on[:, i, :]), heads(o[:, i, :]), spread(ors[:, i, :]), ALU.mult).then_inc(on_done, 1)

            def residual(d, j):
                dve.wait_ge(wo_full, d + 1)
                dve.tensor_tensor(z[:, :, :].rearrange("p s d -> p (s d)"), ps_tr[:, :],
                                  x1[:, j, :, :].rearrange("p s d -> p (s d)"), ALU.add).then_inc(z_done, 1)

            def x2_norm_a(d):
                dve.wait_ge(z_done, d + 1)
                statistics(2, d, lambda s: z[:, s, :])

            def x2_norm_b(d):
                dve.wait_ge(rs_done[2], d + 1)
                for s in range(QB):
                    dve.tensor_scalar(xt(d, s), z[:, s, :], mv[2][:, s, 0:1], rs[2][:, s:s + 1], ALU.subtract, ALU.mult)

            def projections(n, e, j):
                for p in range(NJ):
                    if PJ_AT[p] == n:
                        stacked(e, j, p)

            def early(n, b, j, before, after):
                if after and n > 0:
                    projections(n - 1, b + 1, 1 - j)
                if before and n == 0:
                    projections(NU - 1, b, j)
                if before and n == WO:
                    residual(b - 1, 1 - j)
                if before and n == 2:
                    norm_a(b - 1, 1 - j, 1)
                if n == NP + 2:
                    norm_a(b, j, 0)

            def beside(n, b, j, before, after):
                e, d = b + 1, b - 1
                alone = isinstance(b, int) and b < 0
                if after and n == 0:
                    encoder_norm_a(e)
                if after and n == 1:
                    encoder_norm_b(e)
                if before and n == 2:
                    norm_b(d, 1 - j, 1)
                if after and n == 3:
                    encoder_norm_c(e)
                if before and n == 4:
                    norm_c(d, 1)
                if after and n == 4:
                    add_x(e)
                if after and n == 5:
                    x1_norm_a(e)
                if after and n == 7:
                    x1_norm_b(e, 1 - j)
                if before and n == 8:
                    x2_norm_a(d)
                if before and n == 9:
                    x2_norm_b(d)
                if not alone and n == NP + 2:
                    norm_b(b, j, 0)
                if not alone and n == NP + 4:
                    norm_c(b, 0)

            def prepare():
                for n in range(NU):
                    beside(n, -1, 1, False, True)
                    projections(n, 0, 0)
                maxima(0, 0, 0)

            def seq(b, j, before, after):
                for n in range(NU):
                    if after or n + 1 < NU:
                        maxima(b, j, n + 1)
                    early(n, b, j, before, after)
                    combine(b, j, n)
                    beside(n, b, j, before, after)

            def tail():
                norm_a(B - 1, 1, 1)
                norm_b(B - 1, 1, 1)
                norm_c(B - 1, 1)
                residual(B - 1, 1)
                x2_norm_a(B - 1)
                x2_norm_b(B - 1)

            steps(dve, prepare, seq, tail)

    own.close()


def feed_forward(nc, ctx, consts, X, dram, out):
    own = ExitStack()

    def sb(name, shape, dt=F32):
        return own.enter_context(nc.sbuf_tensor("f_" + name, [P] + shape, dt))

    def sem(name):
        return ctx.enter_context(nc.semaphore("f_" + name))

    CYCLES = 3
    HALF = P // 2
    D2, D3 = D // 2, D // 4
    ident = consts["ident"]

    w1, w2, w3 = sb("w1", [KC, D]), sb("w2", [KC, D2]), sb("w3", [D3])
    w4, w4r = sb("w4", [1]), sb("w4r", [P])
    g1, g2, g3, g3r = sb("g1", [KC, D2]), sb("g2", [D3]), sb("g3", [1]), sb("g3r", [P])
    b1, b2, b3, b4 = sb("b1", [KC]), sb("b2", [1]), sb("b3", [1]), sb("b4", [1])
    gb1, gb2, gb3 = sb("gb1", [1]), sb("gb2", [1]), sb("gb3", [1])
    b4h, gb3h = sb("b4h", [1]), sb("gb3h", [1])
    ar, sgn, slope, tanh_g = sb("ar", [1]), sb("sgn", [1]), sb("slope", [1]), sb("tanh_g", [B])
    ar7, base, offset = sb("ar7", [1]), sb("base", [B]), sb("offset", [B])
    R = sb("R", [KC, T])
    gsum, gm = sb("gsum", [KC, B]), sb("gm", [KC, B])
    gh1, gh2 = sb("gh1", [B]), sb("gh2", [B])
    h1, h2, h3 = sb("h1", [NT, KC, TT]), sb("h2", [NT, TT]), sb("h3", [NT, TT])
    th, cp = sb("th", [NT, TT]), sb("cp", [NT, TT])
    m0, m1 = sb("m0", [2, TT]), sb("m1", [2, TT])
    st, mv = sb("st", [SB, 6]), sb("mv", [SB, 2])
    ve, rs, half = sb("ve", [SB]), sb("rs", [SB]), sb("half", [SB])

    banks = [own.enter_context(nc.psum_tensor(f"f_bank{i}", [P, TT], F32)) for i in range(8)]

    loaded = sem("loaded")
    half_set, set1, set2 = sem("half_set"), sem("set1"), sem("set2")
    x_tr, x_copied, mean_step = sem("x_tr"), sem("x_copied"), sem("mean_step")
    g_full, g_act, offset_step = sem("g_full"), sem("g_act"), sem("offset_step")
    f1, f2, f3, f4 = sem("f1"), sem("f2"), sem("f3"), sem("f4")
    a1, a2, a3, a4 = sem("a1"), sem("a2"), sem("a3"), sem("a4")
    cp_done, m0_done, m1_done, r0_done = sem("cp_done"), sem("m0_done"), sem("m1_done"), sem("r0_done")
    r_done = [sem(f"r_done{k}") for k in range(NT)]
    o_tr, z_done, st_done, mv_done, ve_done, rs_done, y_done, stored = (
        sem("o_tr"), sem("z_done"), sem("st_done"), sem("mv_done"), sem("ve_done"), sem("rs_done"), sem("y_done"), sem("stored"))
    LOADS = 16

    with nc.Block() as block:

        @block.sync
        def _(sp):
            def load(dst, src):
                sp.dma_start(dst, src).then_inc(loaded, 16)

            with nc.allow_non_contiguous_dma(reason="weights and biases by partition, once"):
                load(g1[:, :, :], dram["gc_w1"].rearrange("(c p) n -> p c n", p=P))
                load(g2[:, :], dram["gc_w2"])
                load(g3[0:D3, :], dram["gc_w3"])
                load(gb1[:, :], dram["gc_b1"].rearrange("(p o) -> p o", o=1))
                load(gb2[0:D3, :], dram["gc_b2"].rearrange("(p o) -> p o", o=1))
                load(gb3[:, :], dram["gc_b3"].partition_broadcast(P))
                load(w1[:, :, :], dram["cn_w1"].rearrange("(c p) n -> p c n", p=P))
                load(w2[:, :, :], dram["cn_w2"].rearrange("(c p) n -> p c n", p=P))
                load(w3[:, 0:D3], dram["cn_w3"])
                load(w4[0:D3, :], dram["cn_w4"])
                for c in range(KC):
                    load(b1[:, c:c + 1], dram["cn_b1"][blk(c)].rearrange("(p o) -> p o", o=1))
                load(b2[:, :], dram["cn_b2"].rearrange("(p o) -> p o", o=1))
                load(b3[0:D3, :], dram["cn_b3"].rearrange("(p o) -> p o", o=1))
                load(b4[:, :], dram["cn_b4"].partition_broadcast(P))
                load(ar[:, :], dram["ar"].partition_broadcast(P))
            ov = out.rearrange("b (h p) d -> p (b h) d", p=P)
            for k in range(NT):
                sp.wait_ge(y_done, SB * k + SB)
                sp.dma_start(ov[:, k * SB:(k + 1) * SB], X[:, k * SB:(k + 1) * SB]).then_inc(stored, 16)
            sp.wait_ge(stored, 16 * NT)

        @block.tensor
        def _(pe):
            for k in range(NT):
                for c in range(KC):
                    for s in range(SB):
                        mm = pe.transpose(banks[2 * k + c][:, blk(s)], X[:, k * SB + s, blk(c)], ident[:, :])
                    mm.then_inc(x_tr, 1)
            pe.wait_ge(mean_step, 2)
            pe.wait_ge(set1, 2)
            for c in range(KC):
                mm = pe.matmul(banks[0][:, 0:B], g1[:, c, :], gm[:, c, :], start=(c == 0), stop=(c == KC - 1))
            mm.then_inc(g_full, 1)
            pe.wait_ge(g_act, 1)
            pe.matmul(banks[1][0:D3, 0:B], g2[:, :], gh1[:, :], start=True, stop=True).then_inc(g_full, 1)
            pe.wait_ge(g_act, 2)
            pe.matmul(banks[2][:, 0:B], g3r[0:D3, :], gh2[0:D3, :], start=True, stop=True).then_inc(g_full, 1)
            pe.wait_ge(g_act, 3)
            with pe.Fori(0, CYCLES) as y:
                for k in range(NT):
                    pe.wait_ge(r_done[k], y)
                    for m in range(KC):
                        if k < 2:
                            pe.wait_ge(a4, NT * y)
                        for c in range(KC):
                            mm = pe.matmul(banks[2 * k + m][:, :], w1[:, c, blk(m)], R[:, c, k * TT:(k + 1) * TT],
                                           start=(c == 0), stop=(c == KC - 1))
                        mm.then_inc(f1, 1)
                for k in range(NT):
                    pe.wait_ge(a1, 2 * NT * y + 2 * k + 2)
                    for c in range(KC):
                        mm = pe.matmul(banks[k][:, :], w2[:, c, :], h1[:, k, c, :], start=(c == 0), stop=(c == KC - 1))
                    mm.then_inc(f2, 1)
                for k in range(NT):
                    pe.wait_ge(a2, NT * y + k + 1)
                    pe.matmul(banks[4 + k][0:D3, :], w3[:, 0:D3], h2[:, k, :], start=True, stop=True).then_inc(f3, 1)
                for k in range(NT):
                    pe.wait_ge(a3, NT * y + k + 1)
                    pe.matmul(banks[k][:, :], w4r[0:D3, :], h3[0:D3, k, :], start=True, stop=True).then_inc(f4, 1)
            for k in range(NT):
                pe.wait_ge(r_done[k], CYCLES)
                pe.wait_ge(a4, NT * CYCLES)
                for s in range(SB):
                    bank = banks[2 * k + s // 2]
                    for c in range(KC):
                        mm = pe.transpose(bank[:, (s % 2) * D + c * P:(s % 2) * D + (c + 1) * P],
                                          R[:, c, k * TT + s * P:k * TT + (s + 1) * P], ident[:, :])
                    if s % 2:
                        mm.then_inc(o_tr, 1)

        @block.scalar
        def _(act):
            for n in range(2 * NT):
                act.wait_ge(x_tr, n + 1)
                act.activation(R[:, n % 2, (n // 2) * TT:(n // 2 + 1) * TT], banks[n][:, :], ACT.Copy).then_inc(x_copied, 1)
            act.wait_ge(set1, 4)
            act.wait_ge(g_full, 1)
            act.activation(gh1[:, :], banks[0][:, 0:B], ACT.Gelu, bias=gb1[:, :]).then_inc(g_act, 1)
            act.wait_ge(g_full, 2)
            act.activation(gh2[0:D3, :], banks[1][0:D3, 0:B], ACT.Gelu, bias=gb2[0:D3, :]).then_inc(g_act, 1)
            act.wait_ge(g_full, 3)
            act.activation(tanh_g[:, :], banks[2][:, 0:B], ACT.Tanh, bias=gb3h[:, :], scale=0.5).then_inc(g_act, 1)
            with act.Fori(0, CYCLES) as y:
                for k in range(NT):
                    for m in range(KC):
                        act.wait_ge(f1, 2 * NT * y + 2 * k + m + 1)
                        act.activation(h1[:, k, m, :], banks[2 * k + m][:, :], ACT.Gelu, bias=b1[:, m:m + 1]).then_inc(a1, 1)
                for k in range(NT):
                    act.wait_ge(f2, NT * y + k + 1)
                    act.activation(h2[:, k, :], banks[k][:, :], ACT.Gelu, bias=b2[:, :]).then_inc(a2, 1)
                for k in range(NT):
                    act.wait_ge(f3, NT * y + k + 1)
                    act.activation(h3[0:D3, k, :], banks[4 + k][0:D3, :], ACT.Gelu, bias=b3[0:D3, :]).then_inc(a3, 1)
                for k in range(NT):
                    act.wait_ge(f4, NT * y + k + 1)
                    act.wait_ge(cp_done, 2 * NT * y)
                    act.activation(th[:, k, :], banks[k][:, :], ACT.Tanh, bias=b4h[:, :], scale=0.5).then_inc(a4, 1)

        @block.gpsimd
        def _(pool):
            pool.memset(half[:, :], -0.5).then_inc(half_set, 1)
            pool.wait_ge(half_set, 1)
            with pool.Fori(0, CYCLES) as y:
                for k in range(NT):
                    tok = slice(k * TT, (k + 1) * TT)
                    pool.wait_ge(cp_done, 2 * NT * y + 2 * k + 2)
                    pool.wait_ge(r_done[(k + 2) % NT], y + k // 2)
                    pool.tensor_tensor(m1[:, k % 2, :], cp[:, k, :], R[:, 0, tok], ALU.mult).then_inc(m1_done, 1)
            for k in range(NT):
                pool.wait_ge(ve_done, k + 1)
                pool.tensor_tensor(rs[:, :], ve[:, :], half[:, :], ALU.pow).then_inc(rs_done, 1)

        @block.vector
        def _(dve):
            dve.memset(sgn[:, :], -1.0).then_inc(set2, 1)
            dve.wait_ge(set2, 1)
            dve.memset(sgn[0:HALF, :], 1.0).then_inc(set2, 1)
            dve.wait_ge(loaded, 16 * LOADS)
            dve.tensor_copy(w4r[0:D3, :], w4[0:D3, :].broadcast_to([D3, P])).then_inc(set1, 1)
            dve.tensor_copy(g3r[0:D3, :], g3[0:D3, :].broadcast_to([D3, P])).then_inc(set1, 1)
            dve.tensor_scalar(b4h[:, :], b4[:, :], 0.5, None, ALU.mult).then_inc(set1, 1)
            dve.tensor_scalar(gb3h[:, :], gb3[:, :], 0.5, None, ALU.mult).then_inc(set1, 1)
            dve.tensor_scalar(ar7[:, :], ar[:, :], 0.7, None, ALU.mult).then_inc(set2, 1)
            dve.tensor_scalar(slope[:, :], ar[:, :], 0.3, None, ALU.mult).then_inc(set2, 1)
            dve.wait_ge(set2, 4)
            dve.tensor_tensor(slope[:, :], slope[:, :], sgn[:, :], ALU.mult).then_inc(set2, 1)
            dve.wait_ge(x_copied, 2 * NT)
            dve.tensor_reduce(gsum[:, :, :], R[:, :, :].rearrange("p c (b s) -> p c b s", s=S), AX.X, ALU.add).then_inc(mean_step, 1)
            dve.wait_ge(mean_step, 1)
            dve.tensor_scalar(gm[:, :, :], gsum[:, :, :], 1.0 / S, None, ALU.mult).then_inc(mean_step, 1)
            dve.wait_ge(g_act, 3)
            dve.tensor_scalar(base[:, :], tanh_g[:, :], ar7[:, :], 0.1, ALU.mult, ALU.add).then_inc(offset_step, 1)
            dve.wait_ge(offset_step, 1)
            dve.wait_ge(set2, 5)
            dve.tensor_scalar(offset[:, :], base[:, :], sgn[:, :], None, ALU.mult).then_inc(offset_step, 1)
            dve.wait_ge(offset_step, 2)

            with dve.Fori(0, CYCLES) as y:
                for k in range(NT):
                    tok = slice(k * TT, (k + 1) * TT)
                    dve.wait_ge(a4, NT * y + k + 1)
                    dve.wait_ge(m1_done, NT * y)
                    for b in range(2):
                        cols = slice(b * S, (b + 1) * S)
                        dve.tensor_scalar(cp[:, k, cols], th[:, k, cols], slope[:, :], offset[:, 2 * k + b:2 * k + b + 1],
                                          ALU.mult, ALU.add).then_inc(cp_done, 1)
                    dve.wait_ge(cp_done, 2 * NT * y + 2 * k + 2)
                    dve.wait_ge(r0_done, NT * y + k)
                    dve.tensor_tensor(m0[:, k % 2, :], cp[:, k, :], R[:, 1, tok], ALU.mult).then_inc(m0_done, 1)
                    dve.wait_ge(m0_done, NT * y + k + 1)
                    dve.wait_ge(m1_done, NT * y + k + 1)
                    dve.tensor_tensor(R[:, 0, tok], R[:, 0, tok], m0[:, k % 2, :], ALU.add).then_inc(r0_done, 1)
                    dve.tensor_tensor(R[:, 1, tok], R[:, 1, tok], m1[:, k % 2, :], ALU.subtract).then_inc(r_done[k], 1)
            for k in range(NT):
                for s in range(SB):
                    if s % 2 == 0:
                        dve.wait_ge(o_tr, 2 * k + s // 2 + 1)
                    x = X[:, k * SB + s, :]
                    dve.tensor_tensor(x, x, banks[2 * k + s // 2][:, (s % 2) * D:(s % 2 + 1) * D], ALU.add).then_inc(z_done, 1)
                for s in range(SB):
                    dve.wait_ge(z_done, SB * k + s + 1)
                    dve.bn_stats(st[:, s, :], X[:, k * SB + s, :]).then_inc(st_done, 1)
                for s in range(SB):
                    dve.wait_ge(st_done, SB * k + s + 1)
                    dve.bn_aggr(mv[:, s, :], st[:, s, :]).then_inc(mv_done, 1)
                dve.wait_ge(mv_done, SB * k + SB)
                dve.tensor_scalar(ve[:, :].unsqueeze(2), mv[:, :, 1:2], LN_EPS, None, ALU.add).then_inc(ve_done, 1)
                dve.wait_ge(rs_done, k + 1)
                for s in range(SB):
                    x = X[:, k * SB + s, :]
                    dve.tensor_scalar(x, x, mv[:, s, 0:1], rs[:, s:s + 1], ALU.subtract, ALU.mult).then_inc(y_done, 1)

    own.close()


def constants(nc, ctx):
    consts = {name: ctx.enter_context(nc.sbuf_tensor("c_" + name, shape, F32))
              for name, shape in (("ident", [P, P]), ("amask", [P, P]), ("headmask", [P, HC]), ("blockmask", [P, HC * HX]))}
    ready = ctx.enter_context(nc.semaphore("c_ready"))
    filled = ctx.enter_context(nc.semaphore("c_filled"))
    lower = ctx.enter_context(nc.semaphore("c_lower"))
    ident, amask, headmask = consts["ident"][:, :], consts["amask"][:, :], consts["headmask"][:, :]
    blockmask = consts["blockmask"][:, :].rearrange("p (h d) -> p h d", d=HX)

    with nc.Block() as block:

        @block.gpsimd
        def _(pool):
            pool.memset(ident, 0.0).then_inc(filled, 1)
            for table in (amask, headmask, consts["blockmask"][:, :]):
                pool.memset(table, 1.0).then_inc(filled, 1)
            pool.wait_ge(filled, 4)
            pool.affine_select(ident, ident, [[-1, P]], ALU.not_equal, 1.0, base=0, channel_multiplier=1).then_inc(ready, 1)
            pool.affine_select(amask, amask, [[-1, P]], ALU.is_ge, 0.0, base=0, channel_multiplier=1).then_inc(ready, 1)
            pool.affine_select(headmask, headmask, [[-DH, HC]], ALU.is_ge, 0.0, base=0, channel_multiplier=1).then_inc(lower, 1)
            pool.affine_select(blockmask, blockmask, [[-DH, HC], [0, HX]], ALU.is_ge, 0.0, base=0, channel_multiplier=1).then_inc(lower, 1)
            pool.wait_ge(lower, 2)
            pool.affine_select(headmask, headmask, [[DH, HC]], ALU.is_ge, 0.0, base=DH - 1, channel_multiplier=-1).then_inc(ready, 1)
            pool.affine_select(blockmask, blockmask, [[DH, HC], [0, HX]], ALU.is_ge, 0.0, base=DH - 1, channel_multiplier=-1).then_inc(ready, 1)

    consts["ready"], consts["count"] = ready, 4
    return consts


def build(nc, dram, out):
    with ExitStack() as ctx:
        X = ctx.enter_context(nc.sbuf_tensor("X", [P, NB, D], F32))
        consts = constants(nc, ctx)
        encoder(nc, ctx, consts, X, dram)
        cross(nc, ctx, consts, X, dram)
        feed_forward(nc, ctx, consts, X, dram, out)


_NAMES = {"x": "x", "ctx": "ctx_1024", "ar": "L0_ffn_adaptive_range", "gain": "L0_xattn_gain"}
_NAMES.update({n: "L0_attn_" + n for n in ("Wq", "bq", "Wk", "bk", "Wv", "bv", "Wo", "bo", "g1", "be1", "W1", "b1",
                                           "W2", "b2", "g2", "be2", "gf", "bf")})
_NAMES.update({n: "L0_xattn_" + n for n in ("wq1", "wk1", "wq2", "wk2", "wv", "wo")})
_NAMES.update({n: "L0_ffn_" + n for n in ("cn_w1", "cn_b1", "cn_w2", "cn_b2", "cn_w3", "cn_b3", "cn_w4", "cn_b4",
                                          "gc_w1", "gc_b1", "gc_w2", "gc_b2", "gc_w3", "gc_b3")})


def kernel(**inputs):
    import numpy as np
    import concourse.bacc as bacc
    from concourse.bass_utils import run_bass_kernel_spmd

    nc = bacc.Bacc("TRN2", target_bir_lowering=False, num_devices=1, dynamic_dma_scratch_size=1024)
    arrays, dram = {}, {}
    for short, name in _NAMES.items():
        a = np.ascontiguousarray(inputs[name])
        if a.ndim == 0:
            a = a.reshape(1)
        arrays[f"in_{name}_dram"] = a
        dram[short] = nc.dram_tensor(f"in_{name}_dram", a.shape, mybir.dt.from_np(a.dtype), kind="ExternalInput").ap()
    out = nc.dram_tensor("out_0_dram", [B, S, D], F32, kind="ExternalOutput").ap()
    build(nc, dram, out)
    r = run_bass_kernel_spmd(nc, [arrays], core_ids=[0])
    return r.results[0]["out_0_dram"]
```

```python
from contextlib import ExitStack

import concourse.bass as bass
from concourse import mybir

F32 = mybir.dt.float32
F32R = mybir.dt.float32r
ALU = mybir.AluOpType
ACT = mybir.ActivationFunctionType
AX = mybir.AxisListType

P = 128
D = 256
KC = D // P
B, S = 8, 256
T = B * S
TT = 512
NT = T // TT
SB = TT // P
NB = T // P
H, DH = 16, 16
HC = P // DH
HX = DH + 1
L = 6
DFF = 1024
FC = DFF // P
LN_EPS = 1e-5
DEN_EPS = 1e-6


def blk(s):
    return slice(s * P, (s + 1) * P)


def wait(eng, sem, value):
    if isinstance(value, int) and value <= 0:
        return
    eng.wait_ge(sem, value)


def encoder(nc, ctx, consts, X, dram, load_next):
    own = ExitStack()

    def sb(name, shape, dt=F32):
        return own.enter_context(nc.sbuf_tensor("e_" + name, [P] + shape, dt))

    def sem(name):
        return ctx.enter_context(nc.semaphore("e_" + name))

    ident, amask, headmask, blockmask = consts["ident"], consts["amask"], consts["headmask"], consts["blockmask"]

    HR = 4

    names_a = ["Wq", "Wk", "Wv", "Wo"]
    raw_a = sb("raw_a", [4, KC, D])
    raw_m = sb("raw_m", [KC * DFF])
    hi = {w: sb(w + "_hi", [KC, D], F32R) for w in names_a}
    lo = {w: sb(w + "_lo", [KC, D], F32R) for w in names_a}
    hi["W1"], lo["W1"] = sb("W1_hi", [KC, DFF], F32R), sb("W1_lo", [KC, DFF], F32R)
    hi["W2"], lo["W2"] = sb("W2_hi", [FC, D], F32R), sb("W2_lo", [FC, D], F32R)
    rows_a = {n: sb(n, [D]) for n in ("bv", "bo", "g1", "be1")}
    rows_m = {n: sb(n, [D]) for n in ("b2", "g2", "be2")}
    qk_bias_all, qk_bias, qk_bias1 = sb("qk_bias_all", [L * 2 * KC]), sb("qk_bias", [2 * KC]), sb("qk_bias1", [2 * KC])
    h_bias_all, h_bias = sb("h_bias_all", [L * FC]), sb("h_bias", [FC])

    xT_hi, xT_lo = sb("xT_hi", [KC, TT], F32R), sb("xT_lo", [KC, TT], F32R)
    qkT = sb("qkT", [2 * KC, TT])
    qx = sb("qx", [KC, HC, TT])
    ktok = sb("ktok", [2, KC, P])
    vx = sb("vx", [SB, H, HX])
    kv = sb("kv", [2, KC, HC * HX])
    am = sb("am", [2, 4, 4, P])
    den, rden = sb("den", [SB, H]), sb("rden", [SB, H])
    a_tok = sb("a_tok", [SB, D])
    yT_hi, yT_lo = sb("yT_hi", [KC, TT], F32R), sb("yT_lo", [KC, TT], F32R)
    h_f = sb("h_f", [HR, TT])
    h_hi, h_lo = sb("h_hi", [FC, TT], F32R), sb("h_lo", [FC, TT], F32R)
    st = {i: sb(f"st{i}", [SB, 6]) for i in (1, 2)}
    mv = {i: sb(f"mv{i}", [SB, 2]) for i in (1, 2)}
    ve = {i: sb(f"ve{i}", [SB]) for i in (1, 2)}
    rs = {i: sb(f"rs{i}", [SB]) for i in (1, 2)}
    table = sb("table", [1])
    half = sb("half", [SB])

    ps_tr = [own.enter_context(nc.psum_tensor(f"e_tr{i}", [P, TT], F32)) for i in range(2)]
    ps_pr = [own.enter_context(nc.psum_tensor(f"e_pr{i}", [P, TT], F32)) for i in range(2)]
    ps_sc = [own.enter_context(nc.psum_tensor(f"e_sc{i}", [P, TT], F32)) for i in range(2)]
    ps_tk = [own.enter_context(nc.psum_tensor(f"e_tk{i}", [P, TT], F32)) for i in range(2)]

    x0_loaded, x_loaded, biases_loaded = sem("x0_loaded"), sem("x_loaded"), sem("biases_loaded")
    raw_qkv_loaded, raw_o_loaded, raw_1_loaded, raw_2_loaded = (
        sem("raw_qkv_loaded"), sem("raw_o_loaded"), sem("raw_1_loaded"), sem("raw_2_loaded"))
    bv_loaded, bo_loaded, ln1_rows_loaded = sem("bv_loaded"), sem("bo_loaded"), sem("ln1_rows_loaded")
    b2_loaded, ln2_rows_loaded = sem("b2_loaded"), sem("ln2_rows_loaded")
    xT_tr, qk_full, v_full, ktr_full = sem("xT_tr"), sem("qk_full"), sem("v_full"), sem("ktr_full")
    kv_full, sc_full, out_full = sem("kv_full"), sem("sc_full"), sem("out_full")
    aT_tr, wo_full = sem("aT_tr"), sem("wo_full")
    yT_tr, h_full, m_full = sem("yT_tr"), sem("h_full"), sem("m_full")
    xT_hi_done, qk_exp, ktok_done, aT_hi_done = sem("xT_hi_done"), sem("qk_exp"), sem("ktok_done"), sem("aT_hi_done")
    yT_hi_done, gelu_done, qx_act_done = sem("yT_hi_done"), sem("gelu_done"), sem("qx_act_done")
    qkv_hi, o_hi, w1_hi, w2_hi = sem("qkv_hi"), sem("o_hi"), sem("w1_hi"), sem("w2_hi")
    xT_lo_done, qk_min, phi_done, qx_done, vx_done = sem("xT_lo_done"), sem("qk_min"), sem("phi_done"), sem("qx_done"), sem("vx_done")
    kv_done, am_done, a_done, aT_lo_done = sem("kv_done"), sem("am_done"), sem("a_done"), sem("aT_lo_done")
    den_done, rden_done = sem("den_done"), sem("rden_done")
    yT_lo_done, h_hi_done = sem("yT_lo_done"), sem("h_hi_done")
    z_done = {i: sem(f"z{i}_done") for i in (1, 2)}
    st_done = {i: sem(f"st{i}_done") for i in (1, 2)}
    mv_done = {i: sem(f"mv{i}_done") for i in (1, 2)}
    ve_done = {i: sem(f"ve{i}_done") for i in (1, 2)}
    xc_done = {i: sem(f"xc{i}_done") for i in (1, 2)}
    ln_done = {i: sem(f"ln{i}_done") for i in (1, 2)}
    qk_bias_set, h_bias_set, ones_set = sem("qk_bias_set"), sem("h_bias_set"), sem("ones_set")
    rs_done = {i: sem(f"rs{i}_done") for i in (1, 2)}
    qx_pool_done, xbo_done, xb2_done, h_lo_done, half_set = sem("qx_pool_done"), sem("xbo_done"), sem("xb2_done"), sem("h_lo_done"), sem("half_set")
    qkv_lo, o_lo, w1_lo, w2_lo = sem("qkv_lo"), sem("o_lo"), sem("w1_lo"), sem("w2_lo")

    def steps(eng, step):
        step(0, -1, -1, True, False, True)
        step(0, 0, 0, True, True, True)
        with eng.Fori(0, L - 1) as l:
            for q in range(1, NT):
                step(l, q, l * NT + q, True, True, True)
            step(l + 1, 0, l * NT + NT, True, True, True)
        for q in range(1, NT):
            step(L - 1, q, (L - 1) * NT + q, q < NT - 1, True, q < NT - 2)

    UP_AT = {(0, 1): 4, (1, 1): 5, (2, 0): 6, (3, 0): 7}

    def lagging(u):
        return not (isinstance(u, int) and u <= 0)

    def split3(pe, out, stat, mov, first, last):
        pe.matmul(out, stat[0], mov[0], start=first, stop=False)
        pe.matmul(out, stat[0], mov[1], start=False, stop=False)
        return pe.matmul(out, stat[1], mov[0], start=False, stop=last)

    def blk(s):
        return slice(s * P, (s + 1) * P)

    with nc.Block() as block:

        @block.sync
        def _(sp):
            def load_attn_weights(l, which, done):
                for w in which:
                    sp.dma_start(raw_a[:, names_a.index(w)], dram[w][l, :, :].rearrange("(c p) n -> p c n", p=P)).then_inc(done, 16)

            def load_rows(l, which, rows, done):
                for n in which:
                    sp.dma_start(rows[n][:, :], dram[n][l, :].partition_broadcast(P)).then_inc(done, 16)

            def load_w1(l):
                sp.dma_start(raw_m[:, :].rearrange("p (c n) -> p c n", c=KC),
                             dram["W1"][l, :, :].rearrange("(c p) n -> p c n", p=P)).then_inc(raw_1_loaded, 16)

            def load_w2(l):
                sp.dma_start(raw_m[:, :].rearrange("p (c n) -> p c n", c=FC),
                             dram["W2"][l, :, :].rearrange("(c p) n -> p c n", p=P)).then_inc(raw_2_loaded, 16)

            xv = dram["x"].rearrange("b (h p) d -> p (b h) d", p=P)
            sp.dma_start(X[:, 0:SB], xv[:, 0:SB]).then_inc(x0_loaded, 16)
            load_attn_weights(0, ["Wq", "Wk", "Wv"], raw_qkv_loaded)
            with nc.allow_non_contiguous_dma(reason="biases by partition, once"):
                for j, (n, c) in enumerate((n, c) for n in ("bq", "bk") for c in range(KC)):
                    sp.dma_start(qk_bias_all[:, j::2 * KC], dram[n][:, blk(c)].rearrange("l p -> p l")).then_inc(biases_loaded, 16)
                for c in range(FC):
                    sp.dma_start(h_bias_all[:, c::FC], dram["b1"][:, blk(c)].rearrange("l p -> p l")).then_inc(biases_loaded, 16)
            load_rows(0, ["bv"], rows_a, bv_loaded)
            sp.dma_start(X[:, SB:NB], xv[:, SB:NB]).then_inc(x_loaded, 16)
            load_rows(0, ["bo"], rows_a, bo_loaded)
            load_attn_weights(0, ["Wo"], raw_o_loaded)
            load_w1(0)
            load_rows(0, ["g1", "be1"], rows_a, ln1_rows_loaded)
            load_rows(0, ["b2"], rows_m, b2_loaded)
            load_rows(0, ["g2", "be2"], rows_m, ln2_rows_loaded)

            sp.wait_ge(w1_lo, 1)
            load_w2(0)
            with sp.Fori(0, L - 1) as l:
                sp.wait_ge(qkv_lo, l + 1)
                load_attn_weights(l + 1, ["Wq", "Wk", "Wv"], raw_qkv_loaded)
                sp.wait_ge(o_lo, l + 1)
                load_attn_weights(l + 1, ["Wo"], raw_o_loaded)
                sp.wait_ge(vx_done, 2 * (NT * l + NT))
                load_rows(l + 1, ["bv"], rows_a, bv_loaded)
                sp.wait_ge(xbo_done, NT * l + NT)
                load_rows(l + 1, ["bo"], rows_a, bo_loaded)
                sp.wait_ge(w2_lo, l + 1)
                load_w1(l + 1)
                sp.wait_ge(ln_done[1], SB * (NT * l + NT))
                load_rows(l + 1, ["g1", "be1"], rows_a, ln1_rows_loaded)
                sp.wait_ge(xb2_done, NT * l + NT)
                load_rows(l + 1, ["b2"], rows_m, b2_loaded)
                sp.wait_ge(w1_lo, l + 2)
                load_w2(l + 1)
                sp.wait_ge(ln_done[2], SB * (NT * l + NT))
                load_rows(l + 1, ["g2", "be2"], rows_m, ln2_rows_loaded)
            load_next(sp)

        @block.tensor
        def _(pe):
            def step(l, q, u, attn, mlp, following):
                t = u + 1
                ta = (q + 1) % NT
                la = l + 1 if q == NT - 1 else l

                def x_transpose(t, tile):
                    for c in range(KC):
                        wait(pe, aT_lo_done, 2 * (t - 1) + c + 1)
                        for s in range(SB):
                            mm = pe.transpose(ps_tr[c][:, blk(s)], X[:, tile * SB + s, blk(c)], ident[:, :])
                        mm.then_inc(xT_tr, 1)

                if q < 0:
                    pe.wait_ge(consts["ready"], consts["count"])
                    pe.wait_ge(x0_loaded, 16)
                    x_transpose(0, 0)

                def qk(j):
                    w = names_a[j // KC]
                    for c in range(KC):
                        cols = blk(j % KC)
                        mm = split3(pe, ps_pr[j % 2][:, :], (hi[w][:, c, cols], lo[w][:, c, cols]),
                                    (xT_hi[:, c, :], xT_lo[:, c, :]), c == 0, c == KC - 1)
                    mm.then_inc(qk_full, 1)

                if attn:
                    pe.wait_ge(qkv_lo, la + 1)
                    pe.wait_ge(xT_lo_done, 2 * t + 2)
                    for j in range(KC):
                        if mlp and lagging(u):
                            pe.wait_ge(gelu_done, FC * u - 1 + j)
                        elif mlp:
                            pe.wait_ge(kv_done, 2 * (t - 1) + j + 1)
                        qk(j)
                    for j in range(2):
                        if mlp and lagging(u):
                            pe.wait_ge(z_done[2], SB * u - 1 + j)
                        for s in (2 * j, 2 * j + 1):
                            for c in range(KC):
                                mm = split3(pe, ps_tk[j][:, (s % 2) * D:(s % 2 + 1) * D],
                                            (xT_hi[:, c, blk(s)], xT_lo[:, c, blk(s)]),
                                            (hi["Wv"][:, c, :], lo["Wv"][:, c, :]), c == 0, c == KC - 1)
                        mm.then_inc(v_full, 1)
                if mlp:
                    pe.wait_ge(ln_done[1], SB * u + SB)
                    for c in range(KC):
                        wait(pe, xT_lo_done if attn else aT_lo_done, 2 * t + c + 1 if attn else 2 * u + c + 1)
                        for s in range(SB):
                            mm = pe.transpose(ps_tr[c][:, blk(s)], X[:, q * SB + s, blk(c)], ident[:, :])
                        mm.then_inc(yT_tr, 1)

                if attn:
                    for j in range(KC, 2 * KC):
                        pe.wait_ge(phi_done, 4 * t + j - 1)
                        qk(j)

                def mlp_up(m):
                    if m < 2:
                        if attn:
                            pe.wait_ge(phi_done, 4 * t + 3 + m)
                        else:
                            pe.wait_ge(gelu_done, FC * u - 1 + m)
                    elif m in (4, 5) and attn:
                        pe.wait_ge(kv_done, 2 * t + m - 3)
                    else:
                        pe.wait_ge(gelu_done, FC * u + m - 1)
                    if m == 0:
                        pe.wait_ge(w1_lo, l + 1)
                        pe.wait_ge(yT_lo_done, 2 * u + 2)
                    for c in range(KC):
                        mm = split3(pe, ps_pr[m % 2][:, :], (hi["W1"][:, c, blk(m)], lo["W1"][:, c, blk(m)]),
                                    (yT_hi[:, c, :], yT_lo[:, c, :]), c == 0, c == KC - 1)
                    mm.then_inc(h_full, 1)

                def mlp_down(s, chunks=range(FC)):
                    if 0 in chunks:
                        if s < 2 and attn:
                            pe.wait_ge(a_done, SB * t + s + 3)
                        elif attn:
                            pe.wait_ge(z_done[1], SB * t + s + 1)
                        else:
                            pe.wait_ge(z_done[2], SB * u + s - 1)
                        if s == 0:
                            pe.wait_ge(w2_lo, l + 1)
                    for c in chunks:
                        if s == 0:
                            pe.wait_ge(h_lo_done, FC * u + c + 1)
                        mm = split3(pe, ps_tk[s % 2][:, 0:D], (h_hi[:, c, blk(s)], h_lo[:, c, blk(s)]),
                                    (hi["W2"][:, c, :], lo["W2"][:, c, :]), c == 0, c == FC - 1)
                    if FC - 1 in chunks:
                        mm.then_inc(m_full, 1)

                def scores(s, banks=range(4)):
                    for k in banks:
                        n = 4 * s + k
                        c, g = k // 2, k % 2
                        if n < 2:
                            wait(pe, am_done, 16 * (t - 1) + 15 + n) if q >= 0 else None
                        else:
                            pe.wait_ge(am_done, 16 * t + n - 1)
                        if s == 0 and k == 0:
                            pe.wait_ge(qx_done, t + 1)
                            pe.wait_ge(qx_act_done, t + 1)
                            pe.wait_ge(qx_pool_done, t + 1)
                        pe.matmul(ps_sc[n % 2][:, :], qkT[:, KC + c, blk(s)], qx[:, c, 4 * g:4 * g + 4, blk(s)],
                                  start=True, stop=True).then_inc(sc_full, 1)

                def attend(s, groups=range(4)):
                    out = ps_tk[s % 2]
                    if 0 in groups:
                        if s >= 2:
                            pe.wait_ge(a_done, SB * t + s - 1)
                        else:
                            pe.wait_ge(vx_done, 2 * t + s + 1)
                    if 0 in groups and s % 2 == 0:
                        pe.wait_ge(kv_done, 2 * t + s // 2 + 1)
                        for c in range(KC):
                            pe.matmul(out[:, c * HC * HX:(c + 1) * HC * HX], qkT[:, c, blk(s)], kv[:, s // 2, c, :],
                                      start=(c == 0), stop=False, skip_group_check=True)
                    for g in groups:
                        pe.wait_ge(am_done, 16 * t + 4 * s + g + 1)
                        for h in range(4 * g, 4 * g + 4):
                            mm = pe.matmul(out[:, h * HX:(h + 1) * HX], am[:, s % 2, g, h % 4, :], vx[:, s, h, :],
                                           start=(s % 2 == 1 and h == 0), stop=(h == H - 1), skip_group_check=True)
                    if 3 in groups:
                        mm.then_inc(out_full, 1)

                if mlp:
                    mlp_up(0)
                if attn:
                    pe.wait_ge(phi_done, 4 * t + 4)
                    pe.wait_ge(yT_lo_done if mlp else xT_lo_done, 2 * u + 2 if mlp else 2 * t + 2)
                    for b in range(2):
                        for c in range(KC):
                            mm = pe.transpose(ps_tr[0][:, blk(b * KC + c)], qkT[:, KC + c, blk(2 * b + 1)], ident[:, :])
                    mm.then_inc(ktr_full, 1)
                if mlp:
                    for m in range(1, 4):
                        mlp_up(m)
                if attn:
                    pe.wait_ge(ktok_done, t + 1)
                    pe.wait_ge(vx_done, 2 * t + 2)
                    for b in range(2):
                        if mlp:
                            pe.wait_ge(gelu_done, FC * u + 3 + b)
                        for c in range(KC):
                            mm = pe.matmul(ps_pr[b][:, c * HC * HX:(c + 1) * HC * HX], ktok[:, b, c, :],
                                           vx[:, 2 * b + 1, c * HC:(c + 1) * HC, :], start=True, stop=True,
                                           skip_group_check=True)
                        mm.then_inc(kv_full, 1)
                    scores(0)
                for s in range(SB):
                    for k in range(4):
                        if attn and s + 1 < SB:
                            scores(s + 1, [k])
                        if mlp and (s, k) in UP_AT:
                            mlp_up(UP_AT[s, k])
                        if attn:
                            attend(s, [k])
                        if mlp and s == SB - 1:
                            mlp_down(0, [2 * k, 2 * k + 1])
                if attn:
                    pe.wait_ge(a_done, SB * t + SB)
                    pe.wait_ge(ktok_done, t + 1)
                    for c in range(KC):
                        for s in range(SB):
                            mm = pe.transpose(ps_tr[c][:, blk(s)], a_tok[:, s, blk(c)], ident[:, :])
                        mm.then_inc(aT_tr, 1)
                if mlp:
                    mlp_down(1)
                if attn:
                    pe.wait_ge(o_lo, la + 1)
                    pe.wait_ge(aT_lo_done, 2 * t + 2)
                    for s in range(SB):
                        if s >= 2:
                            pe.wait_ge(z_done[1], SB * t + s - 1)
                        elif mlp:
                            pe.wait_ge(z_done[2], SB * u + s + 1)
                        for c in range(KC):
                            mm = split3(pe, ps_tk[s % 2][:, 0:D], (xT_hi[:, c, blk(s)], xT_lo[:, c, blk(s)]),
                                        (hi["Wo"][:, c, :], lo["Wo"][:, c, :]), c == 0, c == KC - 1)
                        mm.then_inc(wo_full, 1)
                if mlp:
                    mlp_down(2)
                if following:
                    if q < 0:
                        pe.wait_ge(x_loaded, 16)
                    x_transpose(t + 1, (q + 2) % NT)
                if mlp:
                    mlp_down(3)

            steps(pe, step)

        @block.scalar
        def _(act):
            def split_hi(raw, out, n, ready, value, done):
                act.wait_ge(ready, value)
                for j in range(n):
                    a = act.activation(out[j], raw[j], ACT.Copy)
                a.then_inc(done, 1)

            def split_qkv():
                pass

            def w_qkv(l):
                for j, w in enumerate(names_a[:3]):
                    a = act.activation(hi[w][:, :, :], raw_a[:, j], ACT.Copy)
                a.then_inc(qkv_hi, 1)

            def w_o(l):
                act.activation(hi["Wo"][:, :, :], raw_a[:, 3], ACT.Copy).then_inc(o_hi, 1)

            def w_m(w, done):
                flat = hi[w][:, :, :].rearrange("p c n -> p (c n)")
                for j in range(4):
                    a = act.activation(flat[:, j * TT:(j + 1) * TT], raw_m[:, j * TT:(j + 1) * TT], ACT.Copy)
                a.then_inc(done, 1)

            act.wait_ge(raw_qkv_loaded, 48)
            w_qkv(0)
            act.wait_ge(raw_o_loaded, 16)
            w_o(0)
            act.wait_ge(raw_1_loaded, 16)
            w_m("W1", w1_hi)

            def step(l, q, u, attn, mlp, following):
                t = u + 1
                more = not (isinstance(l, int) and l == L - 1)

                def x_hi(t):
                    for c in range(KC):
                        act.wait_ge(xT_tr, 2 * t + c + 1)
                        if c == 0:
                            wait(act, wo_full, SB * t)
                        act.activation(xT_hi[:, c, :], ps_tr[c][:, :], ACT.Copy).then_inc(xT_hi_done, 1)

                if q < 0:
                    x_hi(0)
                def exp(j):
                    act.wait_ge(qk_min, 4 * t + j + 1)
                    act.activation(qkT[:, j, :], qkT[:, j, :], ACT.Exp).then_inc(qk_exp, 1)

                if attn:
                    act.activation(table[:, :], consts["ident"][:, 0:1], ACT.Exp)
                    for j in range(KC):
                        exp(j)
                if mlp:
                    for c in range(KC):
                        act.wait_ge(yT_tr, 2 * u + c + 1)
                        act.activation(yT_hi[:, c, :], ps_tr[c][:, :], ACT.Copy).then_inc(yT_hi_done, 1)
                if attn:
                    for j in range(KC, 2 * KC):
                        exp(j)
                if mlp:
                    act.activation(table[:, :], consts["ident"][:, 0:1], ACT.Gelu)
                    if q == 0:
                        act.wait_ge(h_bias_set, l + 1)

                def gelu(m):
                    act.wait_ge(h_full, FC * u + m + 1)
                    if m >= HR:
                        act.wait_ge(h_lo_done, FC * u + m - HR + 1)
                    act.activation(h_f[:, m % HR, :], ps_pr[m % 2][:, :], ACT.Gelu,
                                   bias=h_bias[:, m:m + 1]).then_inc(gelu_done, 1)

                for m in range(4):
                    if mlp:
                        gelu(m)
                    if attn and m == 0:
                        act.wait_ge(ktr_full, t + 1)
                        act.activation(ktok[:, :, :, :], ps_tr[0][:, :].rearrange("p (b c n) -> p b c n", b=2, c=KC),
                                       ACT.Copy).then_inc(ktok_done, 1)
                    if attn:
                        if m == 0:
                            act.wait_ge(phi_done, 4 * t + 2)
                        c, h = m // 2, 2 * (m % 2)
                        a = act.activation(qx[:, c, h, :], qkT[:, c, :], ACT.Copy, scale=headmask[:, h:h + 1])
                        if m == 3:
                            a.then_inc(qx_act_done, 1)
                if q == 0:
                    act.wait_ge(raw_2_loaded, 16 * (l + 1))
                    if not isinstance(l, int) or l > 0:
                        wait(act, m_full, SB * NT * l)
                    w_m("W2", w2_hi)
                if more and q == NT - 2:
                    act.wait_ge(raw_qkv_loaded, 48 * (l + 2))
                    act.wait_ge(v_full, 2 * t + 2)
                    w_qkv(l + 1)
                if q == NT - 1 and attn:
                    act.wait_ge(raw_o_loaded, 16 * (l + 2))
                    act.wait_ge(wo_full, SB * t)
                    w_o(l + 1)
                if mlp:
                    for m in range(4, FC):
                        gelu(m)
                if attn:
                    for c in range(KC):
                        act.wait_ge(aT_tr, 2 * t + c + 1)
                        act.activation(xT_hi[:, c, :], ps_tr[c][:, :], ACT.Copy).then_inc(aT_hi_done, 1)
                if following:
                    x_hi(t + 1)
                if more and q == NT - 1:
                    act.wait_ge(raw_1_loaded, 16 * (l + 2))
                    act.wait_ge(h_full, FC * u + FC)
                    w_m("W1", w1_hi)

            steps(act, step)

        @block.gpsimd
        def _(pool):
            def lo_part(w, raw, n, done):
                flat_hi = hi[w][:, :, :].rearrange("p c n -> p (c n)").bitcast(F32)
                flat_lo = lo[w][:, :, :].rearrange("p c n -> p (c n)")
                for j in range(n):
                    cols = slice(j * TT, (j + 1) * TT)
                    a = pool.tensor_tensor(flat_lo[:, cols], raw[:, cols], flat_hi[:, cols], ALU.subtract)
                if done is not None:
                    a.then_inc(done, 1)

            def w_qkv(value):
                pool.wait_ge(qkv_hi, value)
                for j, w in enumerate(names_a[:3]):
                    lo_part(w, raw_a[:, j].rearrange("p c n -> p (c n)"), 1, qkv_lo if j == 2 else None)

            def w_o(value):
                pool.wait_ge(o_hi, value)
                lo_part("Wo", raw_a[:, 3].rearrange("p c n -> p (c n)"), 1, o_lo)

            def w_m(w, ready, value, done):
                pool.wait_ge(ready, value)
                lo_part(w, raw_m, 4, done)

            pool.memset(half[:, :], -0.5).then_inc(half_set, 1)
            w_qkv(1)
            w_o(1)
            w_m("W1", w1_hi, 1, w1_lo)

            def step(l, q, u, attn, mlp, following):
                t = u + 1
                ta = (q + 1) % NT
                la = l + 1 if q == NT - 1 else l
                more = not (isinstance(l, int) and l == L - 1)

                def add_row(tile, row, ready, value, loaded, want, done):
                    pool.wait_ge(loaded, want)
                    pool.wait_ge(ready, value)
                    v = X[:, tile * SB:(tile + 1) * SB, :]
                    pool.tensor_tensor(v, v, row[:, :].unsqueeze(1).broadcast_to([P, SB, D]), ALU.add).then_inc(done, 1)

                def rsqrt(i, ready, value):
                    if q <= 0:
                        pool.wait_ge(half_set, 1)
                    pool.wait_ge(ready, value)
                    pool.tensor_tensor(rs[i][:, :], ve[i][:, :], half[:, :], ALU.pow).then_inc(rs_done[i], 1)

                if q < 0:
                    add_row(0, rows_a["bo"], xT_tr, 2, bo_loaded, 16, xbo_done)
                if attn:
                    pool.wait_ge(phi_done, 4 * t + 2)
                    for c in range(KC):
                        for h in (4, 6):
                            a = pool.tensor_tensor(qx[:, c, h, :], qkT[:, c, :], headmask[:, h:h + 1].broadcast_to([P, TT]), ALU.mult)
                    a.then_inc(qx_pool_done, 1)
                if mlp:
                    add_row(q, rows_m["b2"], yT_tr, 2 * u + 2, b2_loaded, 16 * (l + 1), xb2_done)
                    for m in range(FC):
                        if m == 5 and lagging(u):
                            rsqrt(2, ve_done[2], u)
                        if m == 4 and q == 0:
                            w_m("W2", w2_hi, l + 1, w2_lo)
                        if m == 4 and more and q == NT - 2:
                            w_qkv(l + 2)
                        if m == 4 and attn and q == NT - 1:
                            w_o(l + 2)
                        pool.wait_ge(h_hi_done, FC * u + m + 1)
                        pool.tensor_tensor(h_lo[:, m, :], h_f[:, m % HR, :], h_hi[:, m, :].bitcast(F32),
                                           ALU.subtract).then_inc(h_lo_done, 1)
                if attn:
                    rsqrt(1, ve_done[1], t + 1)
                if following:
                    ln = l + 1 if q >= NT - 2 else l
                    add_row((q + 2) % NT, rows_a["bo"], xT_tr, 2 * t + 4, bo_loaded, 16 * (ln + 1), xbo_done)
                if not attn:
                    rsqrt(2, ve_done[2], u + 1)
                if more and q == NT - 1:
                    w_m("W1", w1_hi, l + 2, w1_lo)

            steps(pool, step)

        @block.vector
        def _(dve):
            def set_bias(out, every, n, l, done):
                dve.tensor_copy(out[:, :], every[:, bass.ds(l * n, n)]).then_inc(done, 1)

            dve.memset(vx[:, :, :, DH:HX], 1.0).then_inc(ones_set, 1)
            dve.wait_ge(biases_loaded, 16 * (2 * KC + FC))
            dve.tensor_copy(qk_bias[:, :], qk_bias_all[:, 0:2 * KC]).then_inc(qk_bias_set, 1)
            dve.tensor_scalar(qk_bias1[:, :], qk_bias_all[:, 0:2 * KC], 1.0, None, ALU.add).then_inc(qk_bias_set, 1)
            dve.tensor_copy(h_bias[:, :], h_bias_all[:, 0:FC]).then_inc(h_bias_set, 1)

            def step(l, q, u, attn, mlp, following):
                t = u + 1
                ta = (q + 1) % NT
                la = l + 1 if q == NT - 1 else l
                more = not (isinstance(l, int) and l == L - 1)

                def low(out, bank, part):
                    return dve.tensor_tensor(out, bank, part.bitcast(F32), ALU.subtract)

                def hidden_hi(m):
                    dve.wait_ge(gelu_done, FC * u + m + 1)
                    dve.tensor_copy(h_hi[:, m, :], h_f[:, m % HR, :]).then_inc(h_hi_done, 1)

                def mask(s):
                    for k in range(4):
                        n = 4 * s + k
                        dve.wait_ge(sc_full, 16 * t + n + 1)
                        if s >= 2 and k == 0:
                            dve.wait_ge(out_full, SB * t + s - 1)
                        dve.tensor_tensor(am[:, s % 2, k, :, :],
                                          ps_sc[n % 2][:, :].rearrange("p (h n) -> p h n", n=P),
                                          amask[:, :].unsqueeze(1).broadcast_to([P, 4, P]), ALU.mult).then_inc(am_done, 1)

                def divide(s):
                    dve.wait_ge(out_full, SB * t + s + 1)
                    o = ps_tk[s % 2][:, 0:H * HX].rearrange("p (h d) -> p h d", d=HX)
                    dve.tensor_scalar(den[:, s, :].unsqueeze(2), o[:, :, DH:HX], DEN_EPS, None, ALU.add).then_inc(den_done, 1)
                    dve.wait_ge(den_done, SB * t + s + 1)
                    dve.reciprocal(rden[:, s, :], den[:, s, :]).then_inc(rden_done, 1)
                    dve.wait_ge(rden_done, SB * t + s + 1)
                    dve.tensor_tensor(a_tok[:, s, :].rearrange("p (h d) -> p h d", d=DH), o[:, :, 0:DH],
                                      rden[:, s, :].unsqueeze(2).broadcast_to([P, H, DH]), ALU.mult).then_inc(a_done, 1)

                def residual(i, s, n, tile, ready, added):
                    dve.wait_ge(ready, SB * n + s + 1)
                    if s == 0:
                        dve.wait_ge(added, n + 1)
                    x = X[:, tile * SB + s, :]
                    dve.tensor_tensor(x, ps_tk[s % 2][:, 0:D], x, ALU.add).then_inc(z_done[i], 1)

                def statistics(i, n, tile):
                    for s in range(SB):
                        dve.wait_ge(z_done[i], SB * n + s + 1)
                        dve.bn_stats(st[i][:, s, :], X[:, tile * SB + s, :]).then_inc(st_done[i], 1)
                    dve.wait_ge(st_done[i], SB * n + SB)
                    dve.memset(ve[i][:, :], LN_EPS)
                    for s in range(SB):
                        dve.bn_aggr(mv[i][:, s, :], st[i][:, s, :]).then_inc(mv_done[i], 1)
                    dve.wait_ge(mv_done[i], SB * n + SB)
                    dve.tensor_tensor(ve[i][:, :].unsqueeze(2), ve[i][:, :].unsqueeze(2), mv[i][:, :, 1:2], ALU.add).then_inc(ve_done[i], 1)

                def centre(i, n, tile, gain, loaded, want):
                    dve.wait_ge(loaded, want)
                    dve.wait_ge(mv_done[i], SB * n + SB)
                    for s in range(SB):
                        x = X[:, tile * SB + s, :]
                        dve.scalar_tensor_tensor(x, x, mv[i][:, s, 0:1], gain[:, :], ALU.subtract, ALU.mult).then_inc(xc_done[i], 1)

                def scale(i, n, tile, bias):
                    dve.wait_ge(rs_done[i], n + 1)
                    for s in range(SB):
                        x = X[:, tile * SB + s, :]
                        dve.wait_ge(xc_done[i], SB * n + s + 1)
                        dve.scalar_tensor_tensor(x, x, rs[i][:, s:s + 1], bias[:, :], ALU.mult, ALU.add).then_inc(ln_done[i], 1)

                def negative(j):
                    dve.wait_ge(qk_full, 4 * t + j + 1)
                    if j == 0 and (q < 0 or q == NT - 1):
                        dve.wait_ge(qk_bias_set, 2 * (la + 1))
                    dve.tensor_scalar(qkT[:, j, :], ps_pr[j % 2][:, :], qk_bias[:, j:j + 1], 0.0,
                                      ALU.add, ALU.min).then_inc(qk_min, 1)

                def phi(j):
                    dve.wait_ge(qk_exp, 4 * t + j + 1)
                    dve.scalar_tensor_tensor(qkT[:, j, :], ps_pr[j % 2][:, :], qk_bias1[:, j:j + 1], qkT[:, j, :],
                                             ALU.add, ALU.max).then_inc(phi_done, 1)

                def x_lo(t):
                    for c in range(KC):
                        dve.wait_ge(xT_hi_done, 2 * t + c + 1)
                        low(xT_lo[:, c, :], ps_tr[c][:, :], xT_hi[:, c, :]).then_inc(xT_lo_done, 1)

                if q < 0:
                    x_lo(0)
                if attn:
                    negative(0)
                    negative(1)
                if mlp:
                    scale(1, u, q, rows_a["be1"])
                if attn:
                    phi(0)
                    phi(1)
                if mlp:
                    for c in range(KC):
                        dve.wait_ge(yT_hi_done, 2 * u + c + 1)
                        low(yT_lo[:, c, :], ps_tr[c][:, :], yT_hi[:, c, :]).then_inc(yT_lo_done, 1)
                if attn:
                    if q < 0 or q == NT - 1:
                        dve.wait_ge(bv_loaded, 16 * (la + 1))
                    for j in range(2):
                        negative(KC + j)
                        dve.wait_ge(v_full, 2 * t + j + 1)
                        dve.tensor_tensor(
                            vx[:, 2 * j:2 * j + 2, :, 0:DH], ps_tk[j][:, :].rearrange("p (s h d) -> p s h d", s=2, d=DH),
                            rows_a["bv"][:, :].rearrange("p (h d) -> p h d", d=DH).unsqueeze(1).broadcast_to([P, 2, H, DH]),
                            ALU.add).then_inc(vx_done, 1)
                        phi(KC + j)
                last = (q - 1) % NT
                rows = 32 * (l if q == 0 else l + 1)
                for c in range(KC):
                    if attn:
                        if c == 0:
                            dve.wait_ge(phi_done, 4 * t + 2)
                        for h in range(1, HC, 2):
                            a = dve.tensor_scalar(qx[:, c, h, :], qkT[:, c, :], headmask[:, h:h + 1], None, ALU.mult)
                        if c == KC - 1:
                            a.then_inc(qx_done, 1)
                    if mlp:
                        hidden_hi(2 * c)
                        hidden_hi(2 * c + 1)
                if more and q == NT - 2:
                    set_bias(qk_bias, qk_bias_all, 2 * KC, l + 1, qk_bias_set)
                    dve.tensor_scalar(qk_bias1[:, :], qk_bias_all[:, bass.ds((l + 1) * 2 * KC, 2 * KC)], 1.0, None,
                                      ALU.add).then_inc(qk_bias_set, 1)
                if attn:
                    for b in range(2):
                        dve.wait_ge(kv_full, 2 * t + b + 1)
                        dve.tensor_tensor(kv[:, b, :, :], ps_pr[b][:, 0:KC * HC * HX].rearrange("p (c n) -> p c n", c=KC),
                                          blockmask[:, :].unsqueeze(1).broadcast_to([P, KC, HC * HX]), ALU.mult).then_inc(kv_done, 1)
                    mask(0)
                for s in range(SB):
                    if attn and s + 1 < SB:
                        mask(s + 1)
                    for k in range(4):
                        if mlp and (s, k) in UP_AT:
                            hidden_hi(UP_AT[s, k])
                    if attn:
                        divide(s)
                    if mlp and lagging(u):
                        if s == 0:
                            statistics(2, u - 1, last)
                        elif s == 1:
                            centre(2, u - 1, last, rows_m["g2"], ln2_rows_loaded, rows)
                        elif s == 2:
                            scale(2, u - 1, last, rows_m["be2"])
                if more and q == NT - 1:
                    set_bias(h_bias, h_bias_all, FC, l + 1, h_bias_set)
                if mlp:
                    residual(2, 0, u, q, m_full, xb2_done)
                if attn:
                    for c in range(KC):
                        dve.wait_ge(aT_hi_done, 2 * t + c + 1)
                        low(xT_lo[:, c, :], ps_tr[c][:, :], xT_hi[:, c, :]).then_inc(aT_lo_done, 1)
                if mlp:
                    residual(2, 1, u, q, m_full, xb2_done)
                if attn:
                    for s in range(SB):
                        residual(1, s, t, ta, wo_full, xbo_done)
                    statistics(1, t, ta)
                if mlp:
                    residual(2, 2, u, q, m_full, xb2_done)
                if attn:
                    centre(1, t, ta, rows_a["g1"], ln1_rows_loaded, 32 * (la + 1))
                if following:
                    x_lo(t + 1)
                if mlp:
                    residual(2, 3, u, q, m_full, xb2_done)
                if not attn:
                    statistics(2, u, q)
                    centre(2, u, q, rows_m["g2"], ln2_rows_loaded, 32 * (l + 1))
                    scale(2, u, q, rows_m["be2"])

            steps(dve, step)

    own.close()


class CrossInputs:
    def __init__(self, nc, ctx, dram):
        def sb(name, shape):
            return ctx.enter_context(nc.sbuf_tensor("x_" + name, [P] + shape, F32))

        def sem(name):
            return ctx.enter_context(nc.semaphore("x_" + name))

        QB = S // P
        self.dram = dram
        self.names_w = ["wq1", "wq2", "wk1", "wk2", "wv"]
        self.raw_w = sb("raw_w", [len(self.names_w), KC, DH])
        self.gain = sb("gain", [1])
        self.ctok = sb("ctok", [QB, D])
        self.w_loaded, self.gain_loaded, self.c_loaded = sem("w_loaded"), sem("gain_loaded"), sem("c_loaded")
        self.cv = dram["ctx"].rearrange("b (h p) d -> p (b h) d", p=P)
        self.QB = QB

    def load(self, sp):
        for i, w in enumerate(self.names_w):
            sp.dma_start(self.raw_w[:, i], self.dram[w].rearrange("(c h) e d -> (h e) c d", c=KC)).then_inc(self.w_loaded, 16)
        sp.dma_start(self.gain[:, :], self.dram["gain"].partition_broadcast(P)).then_inc(self.gain_loaded, 16)
        sp.dma_start(self.ctok[:, :, :], self.cv[:, 0:self.QB]).then_inc(self.c_loaded, 16)


def cross(nc, ctx, consts, X, inputs):
    own = ExitStack()

    def sb(name, shape, dt=F32):
        return own.enter_context(nc.sbuf_tensor("x_" + name, [P] + shape, dt))

    def sem(name):
        return ctx.enter_context(nc.semaphore("x_" + name))

    NP = H // 2
    QB = S // P
    NU = QB * NP
    NJ = 2 * NP
    REP = 4
    XS = 3 * QB
    LS = 2 * QB + 1
    AS = 5
    ident, headmask = consts["ident"], consts["headmask"]
    dram, raw_w, gain, ctok = inputs.dram, inputs.raw_w, inputs.gain, inputs.ctok
    w_loaded, gain_loaded, c_loaded = inputs.w_loaded, inputs.gain_loaded, inputs.c_loaded
    raw_wo, gf, bf = sb("raw_wo", [KC, D]), sb("gf", [D]), sb("bf", [D])
    xo = sb("xo", [QB, D])
    wo_loaded, rows_loaded, xo_loaded = sem("wo_loaded"), sem("rows_loaded"), sem("xo_loaded")
    bd = sb("bd", [5 * KC, HC, DH])
    w4 = sb("w4", [4, KC, HC, REP, DH])
    wv = sb("wv", [KC, P])
    woT = sb("woT", [KC, D])
    neg_gain = sb("neg_gain", [1])
    qlow, klow = sb("qlow", [1]), sb("klow", [1])
    half, halfh = sb("half", [QB]), sb("halfh", [H])

    xw = sb("xw", [QB, D])
    x1 = sb("x1", [2, QB, D])
    x1T, cT = sb("x1T", [KC, S]), sb("cT", [KC, S])
    part = sb("part", [2, 2, S], F32R)
    qs, ks = sb("qs", [2, NP, 2, S], F32R), sb("ks", [2, NP, 2, S], F32R)
    vp = sb("vp", [2, QB, D])
    mx = sb("mx", [2, 2, 2])
    ex = sb("ex", [2, 4, S])
    sums = sb("sums", [2, QB, 2, H])
    rec2, ratio = sb("rec2", [2, 2]), sb("ratio", [2, 2])
    pr = sb("pr", [2, 2, S])
    pT = sb("pT", [2, 2 * QB, P])
    r1, o = sb("r1", [QB, H]), sb("o", [QB, D])
    om, sq, ov, ors = sb("om", [QB, H]), sb("sq", [QB, D]), sb("ov", [QB, H]), sb("ors", [QB, H])
    on, oT = sb("on", [QB, D]), sb("oT", [KC, S])
    z = sb("z", [QB, D])
    st = [sb(f"st{k}", [QB, 6]) for k in range(3)]
    mv = [sb(f"mv{k}", [QB, 2]) for k in range(3)]
    ve = [sb(f"ve{k}", [QB]) for k in range(3)]
    rs = [sb(f"rs{k}", [QB]) for k in range(3)]

    ps_sc = [own.enter_context(nc.psum_tensor(f"x_sc{i}", [P, 2, TT], F32)) for i in range(2)]
    ps_pj = [own.enter_context(nc.psum_tensor(f"x_pj{i}", [P, TT], F32)) for i in range(2)]
    ps_tr = own.enter_context(nc.psum_tensor("x_tr", [P, TT], F32))
    ps_ov = own.enter_context(nc.psum_tensor("x_att", [P, TT], F32))

    half_set, scalars_set = sem("half_set"), sem("scalars_set")
    bd_done, prep_tr, prep_copied = sem("bd_done"), sem("prep_tr"), sem("prep_copied")
    ln_step = [sem(f"ln{k}_step") for k in range(3)]
    rs_done = [sem(f"rs{k}_done") for k in range(3)]
    x1_step, xadd_done, z_done = sem("x1_step"), sem("xadd_done"), sem("z_done")
    c_tr, cT_done, x1_tr, x1T_done = sem("c_tr"), sem("cT_done"), sem("x1_tr"), sem("x1T_done")
    pj_full, part_done, pj_done = sem("pj_full"), sem("part_done"), sem("pj_done")
    v_full, v_done = sem("v_full"), sem("v_done")
    sc_full, mx_done, ex_done = sem("sc_full"), sem("mx_done"), sem("ex_done")
    ratio_step, pr_done, pr2_step = sem("ratio_step"), sem("pr_done"), sem("pr2_step")
    p_tr, pT_done, ov_full = sem("p_tr"), sem("pT_done"), sem("ov_full")
    o_read, norm_step, sq_done, ors_done, on_done = (
        sem("o_read"), sem("norm_step"), sem("sq_done"), sem("ors_done"), sem("on_done"))
    o_tr, oT_done, wo_full = sem("o_tr"), sem("oT_done"), sem("wo_full")

    CTX, X1T, V, OT, WO = 0, 8, 2, 5, 6
    K_AT = [1, 2, 3, 4, 5, 6, 7, 8]
    Q_AT = [9, 10, 11, 12, 13, 14, 15, 15]
    PJ_AT = K_AT + Q_AT

    PJ_BANK = [0, 1, 0, 1, 0, 0, 0, 1] + [0, 1] * (NP // 2)
    END_BANK = 1
    WARM = 2
    FIRST_BANK = [2, 3, 4, 5, 0, 1] * 2 + [4, 5, 0, 1]

    def steps(eng, prepare, seq, tail):
        prepare()
        seq(0, 0, False, True)
        with eng.Fori(0, B // 2 - 1) as g:
            seq(2 * g + 1, 1, True, True)
            seq(2 * g + 2, 0, True, True)
        seq(B - 1, 1, True, False)
        tail()

    def unit(b, j, n):
        if n >= NU:
            return b + 1, 1 - j, n - NU, NU * b + n
        if n < 0:
            return b - 1, 1 - j, n + NU, NU * b + n
        return b, j, n, NU * b + n

    def prep_items():
        return [("w", i, c) for i in range(5) for c in range(KC)] + [("wo", n, m) for n in range(KC) for m in range(KC)]

    def free_bank(i):
        return ps_pj[i][:, :] if i < 2 else ps_sc[(i - 2) // 2][:, i % 2, :]

    FREE = 6

    def prep_bank(n):
        return free_bank(n % FREE)[:, 0:P]

    def pj_bank(p, first):
        return free_bank(FIRST_BANK[p] if first else PJ_BANK[p])

    with nc.Block() as block:

        @block.sync
        def _(sp):
            xv = dram["x"].rearrange("b (h p) d -> p (b h) d", p=P)
            sp.dma_start(raw_wo[:, :, :], dram["wo"].rearrange("(c p) m -> p c m", p=P)).then_inc(wo_loaded, 16)
            sp.dma_start(gf[:, :], dram["gf"].partition_broadcast(P)).then_inc(rows_loaded, 16)
            sp.dma_start(bf[:, :], dram["bf"].partition_broadcast(P)).then_inc(rows_loaded, 16)
            sp.dma_start(xo[:, :, :], xv[:, 0:QB]).then_inc(xo_loaded, 16)
            with sp.Fori(1, B) as e:
                sp.wait_ge(c_tr, e)
                sp.dma_start(ctok[:, :, :], inputs.cv[:, bass.ds(e * QB, QB)]).then_inc(c_loaded, 16)
                sp.wait_ge(xadd_done, e)
                sp.dma_start(xo[:, :, :], xv[:, bass.ds(e * QB, QB)]).then_inc(xo_loaded, 16)

        @block.tensor
        def _(pe):
            for n, (kind, i, c) in enumerate(prep_items()):
                if kind == "w":
                    pe.wait_ge(bd_done, i * KC + c + 1)
                    src = bd[:, i * KC + c, :, :].rearrange("p h d -> p (h d)")
                else:
                    if i == 0 and c == 0:
                        pe.wait_ge(wo_loaded, 16)
                    src = raw_wo[:, i, blk(c)]
                if n >= FREE:
                    pe.wait_ge(prep_copied, n - FREE + 1)
                pe.transpose(prep_bank(n), src, ident[:, :]).then_inc(prep_tr, 1)
            pe.wait_ge(prep_copied, len(prep_items()))

            def transpose_to(bank, src):
                for c in range(KC):
                    for s in range(QB):
                        mm = pe.transpose(bank[:, (c * QB + s) * P:(c * QB + s + 1) * P], src[:, s, blk(c)], ident[:, :])
                return mm

            def context(e):
                pe.wait_ge(c_loaded, 16 * e + 16)
                transpose_to(ps_tr, ctok).then_inc(c_tr, 1)

            def project(e, p, end_before):
                first = isinstance(e, int) and e == 0
                bank = pj_bank(p, first)
                if first:
                    if p >= FREE:
                        pe.wait_ge(pj_done, max(i for i in range(p) if FIRST_BANK[i] == FIRST_BANK[p]) + 1)
                elif p == 7 and end_before:
                    pe.wait_ge(z_done, e - 1)
                else:
                    users = [i for i in range(p) if PJ_BANK[i] == PJ_BANK[p]]
                    wait(pe, pj_done, NJ * e + (users[-1] + 1 if users else p - 1))
                if p == 0:
                    pe.wait_ge(cT_done, e + 1)
                elif p == NP:
                    pe.wait_ge(x1T_done, e + 1)
                r, c = p % NP, (p % NP) // (HC // 2)
                src = cT if p < NP else x1T
                for k in range(2):
                    w = (2 if p < NP else 0) + k
                    h = 2 * r % HC
                    mm = pe.matmul(bank[:, k * S:(k + 1) * S], w4[:, w, c, h:h + 2, :, :].rearrange("p h r e -> p (h r e)"),
                                   src[:, c, :], start=True, stop=True, skip_group_check=True)
                mm.then_inc(pj_full, 1)

            def values(e):
                for s in range(QB):
                    for c in range(KC):
                        mm = pe.matmul(ps_tr[:, s * D + c * P:s * D + (c + 1) * P], cT[:, c, blk(s)], wv[:, c, :],
                                       start=True, stop=True, skip_group_check=True)
                mm.then_inc(v_full, 1)

            def x1_transpose(e, j):
                pe.wait_ge(x1_step, XS * e + XS)
                transpose_to(ps_tr, x1[:, j]).then_inc(x1_tr, 1)

            def scores(b, j, n):
                b, j, n, N = unit(b, j, n)
                i, r = n // NP, n % NP
                pe.wait_ge(pj_done, NJ * b + NP + r + 1)
                if not isinstance(N, int) or N >= 2:
                    pe.wait_ge(ex_done, N - 1)
                for k in range(2):
                    for a in range(2):
                        rows = slice(64 * a, 64 * a + 64)
                        mm = pe.matmul(ps_sc[n % 2][:, a, k * S:(k + 1) * S], qs[rows, j, r, k, blk(i)], ks[rows, j, r, k, :],
                                       start=True, stop=True, skip_group_check=True)
                mm.then_inc(sc_full, 1)

            def transposes(b, j, n):
                b, j, n, N = unit(b, j, n)
                wait(pe, pT_done, N)
                for k in range(WARM):
                    pe.matmul(ps_tr[:, blk(k % 4)], ident[:, :], ident[:, :], start=True, stop=True, skip_group_check=True)
                pe.wait_ge(pr_done, N + 1)
                pe.wait_ge(pr2_step, 2 * N + 2)
                for a in range(2):
                    for c in range(QB):
                        mm = pe.transpose(ps_tr[:, blk(a * QB + c)], pr[:, n % 2, a, blk(c)], ident[:, :])
                mm.then_inc(p_tr, 1)

            def attend(b, j, n):
                b, j, n, N = unit(b, j, n)
                i, r = n // NP, n % NP
                pe.wait_ge(pT_done, N + 1)
                if r == 0:
                    if i == 0:
                        pe.wait_ge(v_done, b + 1)
                    wait(pe, o_read, QB * b + i)
                for a in range(2):
                    h = 2 * r + a
                    for c in range(QB):
                        mm = pe.matmul(ps_ov[:, h * DH:(h + 1) * DH], pT[:, n % 2, a * QB + c, :], vp[:, j, c, h * DH:(h + 1) * DH],
                                       start=(h == 0 and c == 0), stop=(c == QB - 1), skip_group_check=True)
                if r == NP - 1:
                    mm.then_inc(ov_full, 1)

            def out_transpose(d, projected):
                pe.wait_ge(on_done, QB * d + QB)
                pe.wait_ge(pj_done, projected)
                transpose_to(ps_pj[END_BANK], on).then_inc(o_tr, 1)

            def out_project(d):
                pe.wait_ge(oT_done, d + 1)
                for s in range(QB):
                    for c in range(KC):
                        mm = pe.matmul(ps_pj[END_BANK][:, s * D:(s + 1) * D], oT[:, c, blk(s)], woT[:, c, :], start=(c == 0),
                                       stop=(c == KC - 1), skip_group_check=True)
                mm.then_inc(wo_full, 1)

            def projections(n, e, before):
                for p in range(NJ):
                    if before and n == OT and p == 5:
                        out_transpose(e - 2, NJ * e + 4)
                    if before and n == WO and p == 6:
                        out_project(e - 2)
                    if PJ_AT[p] == n:
                        project(e, p, before)

            def beside(n, b, j, before, after):
                e = b + 1
                if after and n in (CTX, X1T, V):
                    wait(pe, pT_done, NU * b + n)
                if after and n == CTX:
                    context(e)
                    pe.wait_ge(cT_done, e + 1)
                if after and n == X1T:
                    x1_transpose(e, 1 - j)
                    pe.wait_ge(x1T_done, e + 1)
                if after and n == V:
                    values(e)
                    pe.wait_ge(v_done, e + 1)

            def prepare():
                for n in range(NU):
                    beside(n, -1, 1, False, True)
                    projections(n, 0, False)
                pe.wait_ge(pj_done, NJ - 2)
                scores(0, 0, 0)
                scores(0, 0, 1)

            def seq(b, j, before, after):
                for n in range(NU):
                    if after or n + 2 < NU:
                        scores(b, j, n + 2)
                    if after:
                        projections(n, b + 1, before)
                    elif n == OT:
                        out_transpose(b - 1, NJ * B)
                    elif n == WO:
                        out_project(b - 1)
                    if before or n >= 2:
                        attend(b, j, n - 2)
                    beside(n, b, j, before, after)
                    transposes(b, j, n)

            def tail():
                attend(B - 1, 1, NU - 2)
                attend(B - 1, 1, NU - 1)
                pe.wait_ge(z_done, B - 1)
                out_transpose(B - 1, NJ * B)
                out_project(B - 1)

            steps(pe, prepare, seq, tail)

        @block.scalar
        def _(act):
            for n, (kind, i, c) in enumerate(prep_items()):
                act.wait_ge(prep_tr, n + 1)
                src = prep_bank(n)
                if kind == "w" and i < 4:
                    out = w4[:, i, c, :, :, :]
                    src = src.rearrange("p (h e) -> p h e", e=DH).unsqueeze(2).broadcast_to([P, HC, REP, DH])
                    a = act.activation(out, src, ACT.Copy, scale=DH ** -0.5 if i < 2 else 1.0)
                elif kind == "w":
                    a = act.activation(wv[:, c, :], src, ACT.Copy)
                else:
                    a = act.activation(woT[:, c, blk(i)], src, ACT.Copy)
                a.then_inc(prep_copied, 1)

            def copy(out, bank, ready, value, done):
                act.wait_ge(ready, value)
                act.activation(out.rearrange("p c n -> p (c n)"), bank[:, :], ACT.Copy).then_inc(done, 1)

            def rounded(e, p):
                act.wait_ge(pj_full, NJ * e + p + 1)
                if p >= 2:
                    act.wait_ge(pj_done, NJ * e + p - 1)
                act.activation(part[:, p % 2, :, :].rearrange("p k n -> p (k n)"), pj_bank(p, isinstance(e, int) and e == 0), ACT.Copy).then_inc(part_done, 1)

            def exps(b, j, n):
                b, j, n, N = unit(b, j, n)
                i, r = n // NP, n % NP
                act.wait_ge(mx_done, N + 1)
                if not isinstance(N, int) or N >= 2:
                    act.wait_ge(pr_done, N - 1)
                    act.wait_ge(pr2_step, 2 * N - 2)
                for a in range(2):
                    for k in range(2):
                        x = act.activation(ex[:, n % 2, 2 * a + k, :], ps_sc[n % 2][:, a, k * S:(k + 1) * S], ACT.Exp,
                                           bias=mx[:, n % 2, a, k:k + 1],
                                           accum_out=sums[:, j, i, k, 2 * r + a:2 * r + a + 1])
                x.then_inc(ex_done, 1)

            def probs(b, j, n):
                b, j, n, N = unit(b, j, n)
                copy(pT[:, n % 2, :, :], ps_tr, p_tr, N + 1, pT_done)

            def beside(n, b, j, before, after):
                e = b + 1
                if after and n == CTX:
                    copy(cT[:, :, :], ps_tr, c_tr, e + 1, cT_done)
                if after and n == X1T:
                    copy(x1T[:, :, :], ps_tr, x1_tr, e + 1, x1T_done)
                if after and n == V:
                    copy(vp[:, 1 - j], ps_tr, v_full, e + 1, v_done)

            def projections(n, e):
                for p in range(NJ):
                    if PJ_AT[p] == n:
                        rounded(e, p)

            def prepare():
                for n in range(NU):
                    beside(n, -1, 1, False, True)
                    projections(n, 0)
                exps(0, 0, 0)

            def seq(b, j, before, after):
                for n in range(NU):
                    if after or n + 1 < NU:
                        exps(b, j, n + 1)
                    if before or n >= 1:
                        probs(b, j, n - 1)
                    beside(n, b, j, before, after)
                    if before and n == OT:
                        copy(oT[:, :, :], ps_pj[END_BANK], o_tr, b, oT_done)
                    if after:
                        projections(n, b + 1)

            def tail():
                probs(B - 1, 1, NU - 1)
                copy(oT[:, :, :], ps_pj[END_BANK], o_tr, B, oT_done)

            steps(act, prepare, seq, tail)

        @block.gpsimd
        def _(pool):
            pool.memset(half[:, :], -0.5).then_inc(half_set, 1)
            pool.memset(halfh[:, :], -0.5).then_inc(half_set, 1)
            pool.wait_ge(half_set, 2)

            def rsqrt(k, i):
                pool.wait_ge(ln_step[k], LS * i + LS)
                pool.tensor_tensor(rs[k][:, :], ve[k][:, :], half[:, :], ALU.pow).then_inc(rs_done[k], 1)

            def second_head(b, j, n):
                N = NU * b + n
                p = pr[:, n % 2, 1, :]
                pool.wait_ge(ratio_step, 2 * N + 2)
                if not isinstance(N, int) or N >= 2:
                    pool.wait_ge(p_tr, N - 1)
                pool.tensor_tensor(p, ex[:, n % 2, 3, :], ratio[:, n % 2, 1:2].broadcast_to([P, S]), ALU.mult).then_inc(pr2_step, 1)
                pool.wait_ge(pr2_step, 2 * N + 1)
                pool.tensor_tensor(p, p, ex[:, n % 2, 2, :], ALU.add).then_inc(pr2_step, 1)

            def squares(b, i):
                pool.wait_ge(norm_step, AS * (QB * b + i) + 3)
                pool.tensor_tensor(sq[:, i, :], o[:, i, :], o[:, i, :], ALU.mult).then_inc(sq_done, 1)

            def heads_scaled(b, i):
                pool.wait_ge(norm_step, AS * (QB * b + i) + AS)
                pool.tensor_tensor(ors[:, i, :], ov[:, i, :], halfh[:, :], ALU.pow).then_inc(ors_done, 1)
                pool.wait_ge(ors_done, QB * b + i + 1)
                pool.tensor_tensor(on[:, i, :].rearrange("p (h d) -> p h d", d=DH), o[:, i, :].rearrange("p (h d) -> p h d", d=DH),
                                   ors[:, i, :].unsqueeze(2).broadcast_to([P, H, DH]), ALU.mult).then_inc(on_done, 1)

            def add_x(e):
                pool.wait_ge(x1_step, XS * e + 2 * QB)
                pool.wait_ge(xo_loaded, 16 * e + 16)
                pool.tensor_tensor(xw[:, :, :], xw[:, :, :], xo[:, :, :], ALU.add).then_inc(xadd_done, 1)

            def prepare():
                rsqrt(0, 0)
                add_x(0)
                rsqrt(1, 0)

            def seq(b, j, before, after):
                for n in range(NU):
                    second_head(b, j, n)
                    if after and n == 0:
                        rsqrt(0, b + 1)
                    if before and n == 2:
                        squares(b - 1, 1)
                    if before and n == 3:
                        heads_scaled(b - 1, 1)
                    if after and n == 4:
                        add_x(b + 1)
                    if after and n == 5:
                        rsqrt(1, b + 1)
                    if before and n == 9:
                        rsqrt(2, b - 1)
                    if n == NP + 2:
                        squares(b, 0)
                    if n == NP + 3:
                        heads_scaled(b, 0)

            def tail():
                squares(B - 1, 1)
                heads_scaled(B - 1, 1)
                rsqrt(2, B - 1)

            steps(pool, prepare, seq, tail)

        @block.vector
        def _(dve):
            dve.tensor_reduce(qlow[:, :], headmask[:, 1::2], AX.X, ALU.add, negate=True).then_inc(scalars_set, 1)
            dve.tensor_reduce(klow[:, :], headmask[:, :].rearrange("p (a b c) -> p a b c", b=2, c=2)[:, :, 1, :],
                              AX.XY, ALU.add, negate=True).then_inc(scalars_set, 1)
            dve.wait_ge(w_loaded, 16 * 5)
            for i in range(5):
                for c in range(KC):
                    dve.tensor_tensor(bd[:, i * KC + c, :, :], raw_w[:, i, c, :].unsqueeze(1).broadcast_to([P, HC, DH]),
                                      headmask[:, :].unsqueeze(2).broadcast_to([P, HC, DH]), ALU.mult).then_inc(bd_done, 1)
            dve.wait_ge(gain_loaded, 16)
            dve.tensor_scalar(neg_gain[:, :], gain[:, :], -1.0, None, ALU.mult).then_inc(scalars_set, 1)
            dve.wait_ge(rows_loaded, 32)
            dve.wait_ge(scalars_set, 3)

            def xt(b, s):
                return X[:, bass.ds(b * QB + s, 1), :].rearrange("p o d -> p (o d)")

            def statistics(k, i, src):
                for s in range(QB):
                    dve.bn_stats(st[k][:, s, :], src(s)).then_inc(ln_step[k], 1)
                dve.wait_ge(ln_step[k], LS * i + QB)
                dve.memset(ve[k][:, :], LN_EPS)
                for s in range(QB):
                    dve.bn_aggr(mv[k][:, s, :], st[k][:, s, :]).then_inc(ln_step[k], 1)
                dve.wait_ge(ln_step[k], LS * i + 2 * QB)
                dve.tensor_tensor(ve[k][:, :].unsqueeze(2), ve[k][:, :].unsqueeze(2), mv[k][:, :, 1:2], ALU.add).then_inc(ln_step[k], 1)

            def encoder_norm_a(e):
                statistics(0, e, lambda s: xt(e, s))

            def encoder_norm_b(e):
                for s in range(QB):
                    dve.scalar_tensor_tensor(xw[:, s, :], xt(e, s), mv[0][:, s, 0:1], gf[:, :], ALU.subtract, ALU.mult).then_inc(x1_step, 1)

            def encoder_norm_c(e):
                dve.wait_ge(rs_done[0], e + 1)
                for s in range(QB):
                    dve.wait_ge(x1_step, XS * e + s + 1)
                    dve.scalar_tensor_tensor(xw[:, s, :], xw[:, s, :], rs[0][:, s:s + 1], bf[:, :], ALU.mult, ALU.add).then_inc(x1_step, 1)

            def x1_norm_a(e):
                dve.wait_ge(xadd_done, e + 1)
                statistics(1, e, lambda s: xw[:, s, :])

            def x1_norm_b(e, j):
                dve.wait_ge(rs_done[1], e + 1)
                wait(dve, z_done, e - 1)
                for s in range(QB):
                    dve.tensor_scalar(x1[:, j, s, :], xw[:, s, :], mv[1][:, s, 0:1], rs[1][:, s:s + 1],
                                      ALU.subtract, ALU.mult).then_inc(x1_step, 1)

            def stacked(e, j, p):
                out, low = (ks, klow) if p < NP else (qs, qlow)
                dve.wait_ge(part_done, NJ * e + p + 1)
                dve.scalar_tensor_tensor(out[:, j, p % NP, :, :].rearrange("p k n -> p (k n)"),
                                         part[:, p % 2, :, :].rearrange("p k n -> p (k n)").bitcast(F32), low[:, :],
                                         pj_bank(p, isinstance(e, int) and e == 0), ALU.mult, ALU.add).then_inc(pj_done, 1)

            def maxima(b, j, n):
                b, j, n, N = unit(b, j, n)
                dve.wait_ge(sc_full, N + 1)
                if not isinstance(N, int) or N >= 2:
                    dve.wait_ge(ex_done, N - 1)
                dve.tensor_reduce(mx[:, n % 2, :, :], ps_sc[n % 2][:, :, :].rearrange("p a (k j) -> p a k j", j=S),
                                  AX.X, ALU.max, negate=True).then_inc(mx_done, 1)

            def combine(b, j, n):
                b, j, n, N = unit(b, j, n)
                i, r = n // NP, n % NP
                dve.wait_ge(ex_done, N + 1)
                dve.reciprocal(rec2[:, n % 2, :], sums[:, j, i, 1, 2 * r:2 * r + 2]).then_inc(ratio_step, 1)
                dve.wait_ge(ratio_step, 2 * N + 1)
                dve.scalar_tensor_tensor(ratio[:, n % 2, :], sums[:, j, i, 0, 2 * r:2 * r + 2], neg_gain[:, :],
                                         rec2[:, n % 2, :], ALU.mult, ALU.mult).then_inc(ratio_step, 1)
                dve.wait_ge(ratio_step, 2 * N + 2)
                if not isinstance(N, int) or N >= 2:
                    dve.wait_ge(p_tr, N - 1)
                dve.scalar_tensor_tensor(pr[:, n % 2, 0, :], ex[:, n % 2, 1, :], ratio[:, n % 2, 0:1],
                                         ex[:, n % 2, 0, :], ALU.mult, ALU.add).then_inc(pr_done, 1)

            def heads(ap):
                return ap.rearrange("p (h d) -> p h d", d=DH)

            def spread(ap):
                return ap.unsqueeze(2).broadcast_to([P, H, DH])

            def norm_a(b, j, i):
                at = AS * (QB * b + i)
                dve.reciprocal(r1[:, i, :], sums[:, j, i, 0, :]).then_inc(norm_step, 1)
                dve.wait_ge(ov_full, QB * b + i + 1)
                dve.wait_ge(norm_step, at + 1)
                dve.tensor_tensor(heads(o[:, i, :]), heads(ps_ov[:, 0:D]), spread(r1[:, i, :]), ALU.mult).then_inc(o_read, 1)

            def norm_b(b, j, i):
                at = AS * (QB * b + i)
                dve.wait_ge(o_read, QB * b + i + 1)
                dve.tensor_reduce(om[:, i, :], heads(o[:, i, :]), AX.X, ALU.add).then_inc(norm_step, 1)
                dve.wait_ge(norm_step, at + 2)
                dve.scalar_tensor_tensor(heads(o[:, i, :]), spread(om[:, i, :]), -1.0 / DH, heads(o[:, i, :]),
                                         ALU.mult, ALU.add).then_inc(norm_step, 1)

            def norm_c(b, i):
                at = AS * (QB * b + i)
                dve.wait_ge(sq_done, QB * b + i + 1)
                dve.tensor_reduce(om[:, i, :], heads(sq[:, i, :]), AX.X, ALU.add).then_inc(norm_step, 1)
                dve.wait_ge(norm_step, at + 4)
                dve.tensor_scalar(ov[:, i, :], om[:, i, :], 1.0 / DH, LN_EPS, ALU.mult, ALU.add).then_inc(norm_step, 1)

            def residual(d, j):
                dve.wait_ge(wo_full, d + 1)
                dve.tensor_tensor(z[:, :, :].rearrange("p s d -> p (s d)"), ps_pj[END_BANK][:, :],
                                  x1[:, j, :, :].rearrange("p s d -> p (s d)"), ALU.add).then_inc(z_done, 1)

            def x2_norm_a(d):
                dve.wait_ge(z_done, d + 1)
                statistics(2, d, lambda s: z[:, s, :])

            def x2_norm_b(d):
                dve.wait_ge(rs_done[2], d + 1)
                for s in range(QB):
                    dve.tensor_scalar(xt(d, s), z[:, s, :], mv[2][:, s, 0:1], rs[2][:, s:s + 1], ALU.subtract, ALU.mult)

            def projections(n, e, j):
                for p in range(NJ):
                    if PJ_AT[p] == n:
                        stacked(e, j, p)

            def early(n, b, j, before, after):
                if before and n == 2:
                    norm_a(b - 1, 1 - j, 1)
                if n == NP + 2:
                    norm_a(b, j, 0)

            def beside(n, b, j, before, after):
                e, d = b + 1, b - 1
                alone = isinstance(b, int) and b < 0
                if after and n == 0:
                    encoder_norm_a(e)
                if after and n == 1:
                    encoder_norm_b(e)
                if before and n == 2:
                    norm_b(d, 1 - j, 1)
                if after and n == 3:
                    encoder_norm_c(e)
                if before and n == 3:
                    norm_c(d, 1)
                if after and n == 5:
                    x1_norm_a(e)
                if before and n == WO + 1:
                    residual(d, 1 - j)
                if after and n == 7:
                    x1_norm_b(e, 1 - j)
                if before and n == 9:
                    x2_norm_a(d)
                if before and n == 12:
                    x2_norm_b(d)
                if not alone and n == NP + 2:
                    norm_b(b, j, 0)
                if not alone and n == NP + 3:
                    norm_c(b, 0)

            def prepare():
                for n in range(NU):
                    beside(n, -1, 1, False, True)
                    projections(n, 0, 0)
                maxima(0, 0, 0)

            def seq(b, j, before, after):
                for n in range(NU):
                    if after or n + 1 < NU:
                        maxima(b, j, n + 1)
                    early(n, b, j, before, after)
                    combine(b, j, n)
                    if after and n > 0:
                        projections(n - 1, b + 1, 1 - j)
                    if before and n == 0:
                        projections(NU - 1, b, j)
                    beside(n, b, j, before, after)

            def tail():
                norm_a(B - 1, 1, 1)
                norm_b(B - 1, 1, 1)
                norm_c(B - 1, 1)
                residual(B - 1, 1)
                x2_norm_a(B - 1)
                x2_norm_b(B - 1)

            steps(dve, prepare, seq, tail)

    own.close()


def feed_forward(nc, ctx, consts, X, dram, out):
    own = ExitStack()

    def sb(name, shape, dt=F32):
        return own.enter_context(nc.sbuf_tensor("f_" + name, [P] + shape, dt))

    def sem(name):
        return ctx.enter_context(nc.semaphore("f_" + name))

    CYCLES = 3
    HALF = P // 2
    D2, D3 = D // 2, D // 4
    ident = consts["ident"]

    w1, w2, w3 = sb("w1", [KC, D]), sb("w2", [KC, D2]), sb("w3", [D3])
    w4, w4r = sb("w4", [1]), sb("w4r", [P])
    g1, g2, g3, g3r = sb("g1", [KC, D2]), sb("g2", [D3]), sb("g3", [1]), sb("g3r", [P])
    b1, b2, b3, b4 = sb("b1", [KC]), sb("b2", [1]), sb("b3", [1]), sb("b4", [1])
    gb1, gb2, gb3 = sb("gb1", [1]), sb("gb2", [1]), sb("gb3", [1])
    b4h, gb3h = sb("b4h", [1]), sb("gb3h", [1])
    ar, sgn, slope, tanh_g = sb("ar", [1]), sb("sgn", [1]), sb("slope", [1]), sb("tanh_g", [B])
    ar7, base, offset = sb("ar7", [1]), sb("base", [B]), sb("offset", [B])
    R = sb("R", [KC, T])
    gsum, gm = sb("gsum", [KC, B]), sb("gm", [KC, B])
    gh1, gh2 = sb("gh1", [B]), sb("gh2", [B])
    h1, h2, h3 = sb("h1", [NT, KC, TT]), sb("h2", [NT, TT]), sb("h3", [NT, TT])
    th, cp = sb("th", [NT, TT]), sb("cp", [NT, TT])
    m0, m1 = sb("m0", [2, TT]), sb("m1", [2, TT])
    st, mv = sb("st", [NT, SB, 6]), sb("mv", [NT, SB, 2])
    ve, rs, half = sb("ve", [NT, SB]), sb("rs", [NT, SB]), sb("half", [SB])
    nmean, shift = sb("nmean", [NT, SB]), sb("shift", [NT, SB])

    banks = [own.enter_context(nc.psum_tensor(f"f_bank{i}", [P, TT], F32)) for i in range(8)]

    w1_loaded, loaded = sem("w1_loaded"), sem("loaded")
    half_set, set1, set2 = sem("half_set"), sem("set1"), sem("set2")
    x_tr, x_copied, mean_step = sem("x_tr"), sem("x_copied"), sem("mean_step")
    g_full, g_act, offset_step = sem("g_full"), sem("g_act"), sem("offset_step")
    f1, f2, f3, f4 = sem("f1"), sem("f2"), sem("f3"), sem("f4")
    a1, a2, a3, a4 = sem("a1"), sem("a2"), sem("a3"), sem("a4")
    cp_done, m0_done, m1_done, r0_done = sem("cp_done"), sem("m0_done"), sem("m1_done"), sem("r0_done")
    r_done = [sem(f"r_done{k}") for k in range(NT)]
    SUMS, MEANS, READY = SB // 2, SB // 2 + 2 * SB, SB // 2 + 2 * SB + 2
    o_tr, norm_step, rs_done, y_done, stored = sem("o_tr"), sem("norm_step"), sem("rs_done"), sem("y_done"), sem("stored")
    LOADS_W1, LOADS = 1 + KC, 13

    REST = ((2, 0), (2, 1), (3, 0), (2, 2), (4, 0), (3, 1), (2, 3), (4, 1), (3, 2), (3, 3), (4, 2))
    LAST = (4, NT - 1)
    UP = [(k, m) for k in range(NT) for m in range(KC)]

    with nc.Block() as block:

        @block.sync
        def _(sp):
            def load(dst, src, arrived=loaded):
                sp.dma_start(dst, src).then_inc(arrived, 16)

            with nc.allow_non_contiguous_dma(reason="weights and biases by partition, once"):
                load(w1[:, :, :], dram["cn_w1"].rearrange("(c p) n -> p c n", p=P), w1_loaded)
                for c in range(KC):
                    load(b1[:, c:c + 1], dram["cn_b1"][blk(c)].rearrange("(p o) -> p o", o=1), w1_loaded)
                load(g1[:, :, :], dram["gc_w1"].rearrange("(c p) n -> p c n", p=P))
                load(g2[:, :], dram["gc_w2"])
                load(g3[0:D3, :], dram["gc_w3"])
                load(gb1[:, :], dram["gc_b1"].rearrange("(p o) -> p o", o=1))
                load(gb2[0:D3, :], dram["gc_b2"].rearrange("(p o) -> p o", o=1))
                load(gb3[:, :], dram["gc_b3"].partition_broadcast(P))
                load(w2[:, :, :], dram["cn_w2"].rearrange("(c p) n -> p c n", p=P))
                load(w3[:, 0:D3], dram["cn_w3"])
                load(w4[0:D3, :], dram["cn_w4"])
                load(b2[:, :], dram["cn_b2"].rearrange("(p o) -> p o", o=1))
                load(b3[0:D3, :], dram["cn_b3"].rearrange("(p o) -> p o", o=1))
                load(b4[:, :], dram["cn_b4"].partition_broadcast(P))
                load(ar[:, :], dram["ar"].partition_broadcast(P))
            ov = out.rearrange("b (h p) d -> p (b h) d", p=P)
            for k in range(NT):
                sp.wait_ge(y_done, SB * k + SB)
                sp.dma_start(ov[:, k * SB:(k + 1) * SB], X[:, k * SB:(k + 1) * SB]).then_inc(stored, 16)
            sp.wait_ge(stored, 16 * NT)

        @block.tensor
        def _(pe):
            for k in range(NT):
                for c in range(KC):
                    for s in range(SB):
                        mm = pe.transpose(banks[2 * k + c][:, blk(s)], X[:, k * SB + s, blk(c)], ident[:, :])
                    mm.then_inc(x_tr, 1)
            def up(y, k, m):
                if m == 0:
                    pe.wait_ge(r_done[k], y + 1)
                for c in range(KC):
                    mm = pe.matmul(banks[2 * k + m][:, :], w1[:, c, blk(m)], R[:, c, k * TT:(k + 1) * TT],
                                   start=(c == 0), stop=(c == KC - 1))
                mm.then_inc(f1, 1)

            def layer(y, stage, k):
                if stage == 2:
                    pe.wait_ge(a1, 2 * NT * y + 2 * k + 2)
                    for c in range(KC):
                        mm = pe.matmul(banks[k][:, :], w2[:, c, :], h1[:, k, c, :], start=(c == 0), stop=(c == KC - 1))
                    mm.then_inc(f2, 1)
                elif stage == 3:
                    pe.wait_ge(a2, NT * y + k + 1)
                    pe.matmul(banks[4 + k][0:D3, :], w3[:, 0:D3], h2[:, k, :], start=True, stop=True).then_inc(f3, 1)
                else:
                    pe.wait_ge(a3, NT * y + k + 1)
                    pe.matmul(banks[k][:, :], w4r[0:D3, :], h3[0:D3, k, :], start=True, stop=True).then_inc(f4, 1)

            pe.wait_ge(w1_loaded, 16 * LOADS_W1)
            for k, m in UP:
                if m == 0:
                    pe.wait_ge(x_copied, k + 1)
                if (k, m) == (2, 0):
                    pe.wait_ge(mean_step, NT + 1)
                    pe.wait_ge(set1, 2)
                    pe.wait_ge(r_done[3], 1)
                    pe.wait_ge(x_copied, NT)
                    for c in range(KC):
                        mm = pe.matmul(banks[6][:, 0:B], g1[:, c, :], gm[:, c, :], start=(c == 0), stop=(c == KC - 1))
                    mm.then_inc(g_full, 1)
                if (k, m) == (3, 0):
                    pe.wait_ge(g_act, 1)
                    pe.matmul(banks[7][0:D3, 0:B], g2[:, :], gh1[:, :], start=True, stop=True).then_inc(g_full, 1)
                if (k, m) == (3, 1):
                    pe.wait_ge(g_act, 2)
                    pe.wait_ge(a1, 1)
                    pe.matmul(banks[0][:, 0:B], g3r[0:D3, :], gh2[0:D3, :], start=True, stop=True).then_inc(g_full, 1)
                up(0, k, m)
            pe.wait_ge(g_act, 3)
            with pe.Fori(0, CYCLES - 1) as y:
                for stage, k in REST:
                    layer(y, stage, k)
                pe.wait_ge(a4, NT * y + 2)
                up(y + 1, *UP[0])
                layer(y, *LAST)
                for k, m in UP[1:]:
                    if (k, m) == (1, 0):
                        pe.wait_ge(a4, NT * y + NT)
                    up(y + 1, k, m)
            for stage, k in REST + (LAST,):
                layer(CYCLES - 1, stage, k)
            for k in range(NT):
                pe.wait_ge(r_done[k], CYCLES + 1)
                pe.wait_ge(a4, NT * CYCLES)
                for s in range(SB):
                    bank = banks[2 * k + s // 2]
                    for c in range(KC):
                        mm = pe.transpose(bank[:, (s % 2) * D + c * P:(s % 2) * D + (c + 1) * P],
                                          R[:, c, k * TT + s * P:k * TT + (s + 1) * P], ident[:, :])
                    if s % 2:
                        mm.then_inc(o_tr, 1)

        @block.scalar
        def _(act):
            def up(y, k, m):
                act.wait_ge(f1, 2 * NT * y + 2 * k + m + 1)
                act.activation(h1[:, k, m, :], banks[2 * k + m][:, :], ACT.Gelu, bias=b1[:, m:m + 1]).then_inc(a1, 1)

            def layer(y, stage, k):
                if stage == 2:
                    act.wait_ge(f2, NT * y + k + 1)
                    act.activation(h2[:, k, :], banks[k][:, :], ACT.Gelu, bias=b2[:, :]).then_inc(a2, 1)
                elif stage == 3:
                    act.wait_ge(f3, NT * y + k + 1)
                    act.activation(h3[0:D3, k, :], banks[4 + k][0:D3, :], ACT.Gelu, bias=b3[0:D3, :]).then_inc(a3, 1)
                else:
                    act.wait_ge(f4, NT * y + k + 1)
                    act.wait_ge(cp_done, 2 * NT * y)
                    act.activation(th[:, k, :], banks[k][:, :], ACT.Tanh, bias=b4h[:, :], scale=0.5).then_inc(a4, 1)

            for k in range(NT):
                act.wait_ge(x_tr, 2 * k + 1)
                act.activation(R[:, 0, k * TT:(k + 1) * TT], banks[2 * k][:, :], ACT.Copy).then_inc(x_copied, 1)
            act.wait_ge(w1_loaded, 16 * LOADS_W1)
            for k, m in UP:
                if (k, m) == (2, 0):
                    act.wait_ge(set1, 4)
                    act.wait_ge(g_full, 1)
                    act.activation(gh1[:, :], banks[6][:, 0:B], ACT.Gelu, bias=gb1[:, :]).then_inc(g_act, 1)
                if (k, m) == (3, 0):
                    act.wait_ge(g_full, 2)
                    act.activation(gh2[0:D3, :], banks[7][0:D3, 0:B], ACT.Gelu, bias=gb2[0:D3, :]).then_inc(g_act, 1)
                if (k, m) == (3, 1):
                    act.wait_ge(g_full, 3)
                    act.activation(tanh_g[:, :], banks[0][:, 0:B], ACT.Tanh, bias=gb3h[:, :], scale=0.5).then_inc(g_act, 1)
                up(0, k, m)
            with act.Fori(0, CYCLES - 1) as y:
                for stage, k in REST:
                    layer(y, stage, k)
                up(y + 1, *UP[0])
                layer(y, *LAST)
                for k, m in UP[1:]:
                    up(y + 1, k, m)
            for stage, k in REST + (LAST,):
                layer(CYCLES - 1, stage, k)
            for k in range(NT):
                act.wait_ge(rs_done, 2 * k + 2)
                for s in range(SB):
                    x = X[:, k * SB + s, :]
                    act.activation(x, x, ACT.Identity, bias=shift[:, k, s:s + 1], scale=rs[:, k, s:s + 1]).then_inc(y_done, 1)

        @block.gpsimd
        def _(pool):
            pool.memset(half[:, :], -0.5).then_inc(half_set, 1)
            pool.wait_ge(half_set, 1)
            with pool.Fori(0, CYCLES) as y:
                for k in range(NT):
                    tok = slice(k * TT, (k + 1) * TT)
                    pool.wait_ge(cp_done, 2 * NT * y + 2 * k + 2)
                    pool.wait_ge(r_done[(k + 2) % NT], y + k // 2 + 1)
                    pool.tensor_tensor(m1[:, k % 2, :], cp[:, k, :], R[:, 0, tok], ALU.mult).then_inc(m1_done, 1)
            for k in range(NT):
                pool.wait_ge(norm_step, READY * (k + 1))
                pool.tensor_tensor(rs[:, k, :], ve[:, k, :], half[:, :], ALU.pow).then_inc(rs_done, 1)
                pool.wait_ge(rs_done, 2 * k + 1)
                pool.tensor_tensor(shift[:, k, :], nmean[:, k, :], rs[:, k, :], ALU.mult).then_inc(rs_done, 1)

        @block.vector
        def _(dve):
            dve.memset(sgn[:, :], -1.0).then_inc(set2, 1)
            dve.wait_ge(set2, 1)
            dve.memset(sgn[0:HALF, :], 1.0).then_inc(set2, 1)
            for k in range(NT):
                dve.wait_ge(x_tr, 2 * k + 2)
                dve.tensor_copy(R[:, 1, k * TT:(k + 1) * TT], banks[2 * k + 1][:, :]).then_inc(r_done[k], 1)
            for k in range(NT):
                dve.wait_ge(x_copied, k + 1)
                dve.wait_ge(r_done[k], 1)
                dve.tensor_reduce(gsum[:, :, 2 * k:2 * k + 2], R[:, :, k * TT:(k + 1) * TT].rearrange("p c (b s) -> p c b s", s=S),
                                  AX.X, ALU.add).then_inc(mean_step, 1)
            dve.wait_ge(mean_step, NT)
            dve.tensor_scalar(gm[:, :, :], gsum[:, :, :], 1.0 / S, None, ALU.mult).then_inc(mean_step, 1)
            dve.wait_ge(loaded, 16 * LOADS)
            dve.tensor_copy(w4r[0:D3, :], w4[0:D3, :].broadcast_to([D3, P])).then_inc(set1, 1)
            dve.tensor_copy(g3r[0:D3, :], g3[0:D3, :].broadcast_to([D3, P])).then_inc(set1, 1)
            dve.tensor_scalar(b4h[:, :], b4[:, :], 0.5, None, ALU.mult).then_inc(set1, 1)
            dve.tensor_scalar(gb3h[:, :], gb3[:, :], 0.5, None, ALU.mult).then_inc(set1, 1)
            dve.tensor_scalar(ar7[:, :], ar[:, :], 0.7, None, ALU.mult).then_inc(set2, 1)
            dve.tensor_scalar(slope[:, :], ar[:, :], 0.3, None, ALU.mult).then_inc(set2, 1)
            dve.wait_ge(set2, 4)
            dve.tensor_tensor(slope[:, :], slope[:, :], sgn[:, :], ALU.mult).then_inc(set2, 1)
            dve.wait_ge(g_act, 3)
            dve.tensor_scalar(base[:, :], tanh_g[:, :], ar7[:, :], 0.1, ALU.mult, ALU.add).then_inc(offset_step, 1)
            dve.wait_ge(offset_step, 1)
            dve.wait_ge(set2, 5)
            dve.tensor_scalar(offset[:, :], base[:, :], sgn[:, :], None, ALU.mult).then_inc(offset_step, 1)
            dve.wait_ge(offset_step, 2)

            def shares(y, k):
                dve.wait_ge(a4, NT * y + k + 1)
                dve.wait_ge(m1_done, NT * y)
                for b in range(2):
                    cols = slice(b * S, (b + 1) * S)
                    dve.tensor_scalar(cp[:, k, cols], th[:, k, cols], slope[:, :], offset[:, 2 * k + b:2 * k + b + 1],
                                      ALU.mult, ALU.add).then_inc(cp_done, 1)
                dve.wait_ge(cp_done, 2 * NT * y + 2 * k + 2)
                dve.wait_ge(r0_done, NT * y + max(k - 1, 0))
                dve.tensor_tensor(m0[:, k % 2, :], cp[:, k, :], R[:, 1, k * TT:(k + 1) * TT], ALU.mult).then_inc(m0_done, 1)

            def update(y, k):
                tok = slice(k * TT, (k + 1) * TT)
                dve.wait_ge(m0_done, NT * y + k + 1)
                dve.wait_ge(m1_done, NT * y + k + 1)
                dve.tensor_tensor(R[:, 0, tok], R[:, 0, tok], m0[:, k % 2, :], ALU.add).then_inc(r0_done, 1)
                dve.tensor_tensor(R[:, 1, tok], R[:, 1, tok], m1[:, k % 2, :], ALU.subtract).then_inc(r_done[k], 1)

            with dve.Fori(0, CYCLES - 1) as y:
                for k in range(NT):
                    shares(y, k)
                    update(y, k)
            for k in range(NT):
                shares(CYCLES - 1, k)
                if k >= 1:
                    update(CYCLES - 1, k - 1)
            update(CYCLES - 1, NT - 1)
            for k in range(NT):
                for h in range(SB // 2):
                    dve.wait_ge(o_tr, 2 * k + h + 1)
                    x = X[:, k * SB + 2 * h:k * SB + 2 * h + 2, :].rearrange("p s d -> p (s d)")
                    dve.tensor_tensor(x, x, banks[2 * k + h][:, :], ALU.add).then_inc(norm_step, 1)
                for s in range(SB):
                    dve.wait_ge(norm_step, READY * k + s // 2 + 1)
                    dve.bn_stats(st[:, k, s, :], X[:, k * SB + s, :]).then_inc(norm_step, 1)
                for s in range(SB):
                    dve.wait_ge(norm_step, READY * k + SUMS + s + 1)
                    dve.bn_aggr(mv[:, k, s, :], st[:, k, s, :]).then_inc(norm_step, 1)
                dve.wait_ge(norm_step, READY * k + MEANS)
                dve.tensor_scalar(ve[:, k, :].unsqueeze(2), mv[:, k, :, 1:2], LN_EPS, None, ALU.add).then_inc(norm_step, 1)
                dve.tensor_scalar(nmean[:, k, :].unsqueeze(2), mv[:, k, :, 0:1], -1.0, None, ALU.mult).then_inc(norm_step, 1)

    own.close()


def constants(nc, ctx):
    consts = {name: ctx.enter_context(nc.sbuf_tensor("c_" + name, shape, F32))
              for name, shape in (("ident", [P, P]), ("amask", [P, P]), ("headmask", [P, HC]), ("blockmask", [P, HC * HX]))}
    ready = ctx.enter_context(nc.semaphore("c_ready"))
    filled = ctx.enter_context(nc.semaphore("c_filled"))
    lower = ctx.enter_context(nc.semaphore("c_lower"))
    ident, amask, headmask = consts["ident"][:, :], consts["amask"][:, :], consts["headmask"][:, :]
    blockmask = consts["blockmask"][:, :].rearrange("p (h d) -> p h d", d=HX)

    with nc.Block() as block:

        @block.gpsimd
        def _(pool):
            pool.memset(ident, 0.0).then_inc(filled, 1)
            for table in (amask, headmask, consts["blockmask"][:, :]):
                pool.memset(table, 1.0).then_inc(filled, 1)
            pool.wait_ge(filled, 4)
            pool.affine_select(ident, ident, [[-1, P]], ALU.not_equal, 1.0, base=0, channel_multiplier=1).then_inc(ready, 1)
            pool.affine_select(amask, amask, [[-1, P]], ALU.is_ge, 0.0, base=0, channel_multiplier=1).then_inc(ready, 1)
            pool.affine_select(headmask, headmask, [[-DH, HC]], ALU.is_ge, 0.0, base=0, channel_multiplier=1).then_inc(lower, 1)
            pool.affine_select(blockmask, blockmask, [[-DH, HC], [0, HX]], ALU.is_ge, 0.0, base=0, channel_multiplier=1).then_inc(lower, 1)
            pool.wait_ge(lower, 2)
            pool.affine_select(headmask, headmask, [[DH, HC]], ALU.is_ge, 0.0, base=DH - 1, channel_multiplier=-1).then_inc(ready, 1)
            pool.affine_select(blockmask, blockmask, [[DH, HC], [0, HX]], ALU.is_ge, 0.0, base=DH - 1, channel_multiplier=-1).then_inc(ready, 1)

    consts["ready"], consts["count"] = ready, 4
    return consts


def build(nc, dram, out):
    with ExitStack() as ctx:
        X = ctx.enter_context(nc.sbuf_tensor("X", [P, NB, D], F32))
        consts = constants(nc, ctx)
        inputs = CrossInputs(nc, ctx, dram)
        encoder(nc, ctx, consts, X, dram, inputs.load)
        cross(nc, ctx, consts, X, inputs)
        feed_forward(nc, ctx, consts, X, dram, out)


_NAMES = {"x": "x", "ctx": "ctx_1024", "ar": "L0_ffn_adaptive_range", "gain": "L0_xattn_gain"}
_NAMES.update({n: "L0_attn_" + n for n in ("Wq", "bq", "Wk", "bk", "Wv", "bv", "Wo", "bo", "g1", "be1", "W1", "b1",
                                           "W2", "b2", "g2", "be2", "gf", "bf")})
_NAMES.update({n: "L0_xattn_" + n for n in ("wq1", "wk1", "wq2", "wk2", "wv", "wo")})
_NAMES.update({n: "L0_ffn_" + n for n in ("cn_w1", "cn_b1", "cn_w2", "cn_b2", "cn_w3", "cn_b3", "cn_w4", "cn_b4",
                                          "gc_w1", "gc_b1", "gc_w2", "gc_b2", "gc_w3", "gc_b3")})


def kernel(**inputs):
    import numpy as np
    import concourse.bacc as bacc
    from concourse.bass_utils import run_bass_kernel_spmd

    nc = bacc.Bacc("TRN2", target_bir_lowering=False, num_devices=1, dynamic_dma_scratch_size=1024)
    arrays, dram = {}, {}
    for short, name in _NAMES.items():
        a = np.ascontiguousarray(inputs[name])
        if a.ndim == 0:
            a = a.reshape(1)
        arrays[f"in_{name}_dram"] = a
        dram[short] = nc.dram_tensor(f"in_{name}_dram", a.shape, mybir.dt.from_np(a.dtype), kind="ExternalInput").ap()
    out = nc.dram_tensor("out_0_dram", [B, S, D], F32, kind="ExternalOutput").ap()
    build(nc, dram, out)
    r = run_bass_kernel_spmd(nc, [arrays], core_ids=[0])
    return r.results[0]["out_0_dram"]
```
